# Optimizing a Trainium2 kernel written in Bass

```python
import numpy as np
import jax
import jax.numpy as jnp

def _softmax(x, axis=-1):
    return jax.nn.softmax(x, axis=axis)

def _gelu(x):
    return jax.nn.gelu(x, approximate=True)

def _silu(x):
    return jax.nn.silu(x)

def _sigmoid(x):
    return jax.nn.sigmoid(x)

def _layernorm(x, axis=-1, eps=1e-05):
    m = jnp.mean(x, axis=axis, keepdims=True)
    v = jnp.var(x, axis=axis, keepdims=True)
    return (x - m) / jnp.sqrt(v + eps)

def _scatter_add(tgt, idx, src, axis=0):
    return tgt.at[idx].add(src)

def _segment_sum(src, seg, n):
    return jax.ops.segment_sum(src, seg, n)
kernel_name = 'mk_seq_postln_d1_jaxref_r8_9aef4d'

def setup_inputs(seed: int=0):
    np.random.seed(seed)
    _w = jnp.asarray

    def _L0_attn_setup():
        import jax, jax.numpy as jnp
        import numpy as np
        D_MODEL = 128
        H = 4
        DK = 128
        DV = 32
        EPS = 1e-05
        SCALE = DK ** (-0.5)

        def _delta_rule(q, k, v, beta):
            b = q.shape[0]
            qt = jnp.moveaxis(q, 1, 0)
            kt = jnp.moveaxis(k, 1, 0)
            vt = jnp.moveaxis(v, 1, 0)
            bt = jnp.moveaxis(beta, 1, 0)
            S0 = jnp.zeros((b, H, DK, DV), q.dtype)

            def step(S, inp):
                q_t, k_t, v_t, b_t = inp
                pred = jnp.einsum('bhk,bhkv->bhv', k_t, S)
                delta = (v_t - pred) * b_t[..., None]
                S = S + k_t[..., :, None] * delta[..., None, :]
                o_t = jnp.einsum('bhk,bhkv->bhv', q_t, S)
                return (S, o_t)
            _, o = jax.lax.scan(step, S0, (qt, kt, vt, bt))
            return jnp.moveaxis(o, 0, 1)
        key = jax.random.key(seed)
        ks = jax.random.split(key, 8)
        w = lambda k, i, o: jax.random.normal(k, (i, o), jnp.float32) * 2.0 ** (-2.5) * (6.0 / (i + o)) ** 0.5 * 2
        return {'x': jax.random.normal(ks[0], (2, 512, D_MODEL), jnp.float32), 'Wq': w(ks[1], D_MODEL, H * DK), 'Wk': w(ks[2], D_MODEL, H * DK), 'Wv': w(ks[3], D_MODEL, H * DV), 'Wb': w(ks[4], D_MODEL, H), 'Wg': w(ks[5], D_MODEL, H * DV), 'Wo': w(ks[6], H * DV, D_MODEL), 'norm_w': jnp.ones((DV,), jnp.float32)}
    _L0_attn_in = _L0_attn_setup()

    def _L0_ffn_setup():
        import jax, jax.numpy as jnp
        import numpy as np
        B, S, H, F, E, K = (4, 256, 128, 448, 8, 2)
        CAP_FACTOR = 1.25

        def _moe_forward(hidden_states, gate_w, w1, w2, w3):
            b, s, h = hidden_states.shape
            dtype = hidden_states.dtype
            x = hidden_states.reshape(-1, h)
            router_logits = x @ gate_w.T
            expert_weights = jax.nn.softmax(router_logits.astype(jnp.float32), axis=1)
            _, selected_experts = jax.lax.top_k(expert_weights, K)
            top_k_idx = selected_experts.reshape(b, s, K)
            probs = expert_weights.reshape(b, s, E)
            capacity = int(s * K / E * CAP_FACTOR)
            expert_mask = jax.nn.one_hot(top_k_idx, E, dtype=jnp.int32)
            mask_fused = expert_mask.reshape(b, s * K, E)
            count_fused = jnp.cumsum(mask_fused, axis=1)
            count = count_fused.reshape(b, s, K, E)
            trunc_mask = expert_mask * (count <= capacity).astype(jnp.int32)
            combined_mask = trunc_mask.sum(axis=2)
            masked_probs = probs * combined_mask
            pos_fused = mask_fused * count_fused
            pos = pos_fused.reshape(b, s, K, E)
            combined_pos = pos.sum(axis=2) * combined_mask
            pos_in_cap = jax.nn.one_hot(combined_pos, capacity + 1, dtype=jnp.int32)
            combine_mask = masked_probs[..., None] * pos_in_cap
            combine_mask = combine_mask[..., 1:].astype(dtype)
            dispatch_mask = (combine_mask != 0).astype(dtype)
            dispatch = jnp.einsum('bsm,bsec->ebcm', hidden_states, dispatch_mask)
            h1 = jnp.einsum('ebcm,emh->ebch', dispatch, w1)
            h3 = jnp.einsum('ebcm,emh->ebch', dispatch, w3)
            expert_out = jnp.einsum('ebch,ehm->ebcm', jax.nn.silu(h1) * h3, w2)
            final = jnp.einsum('ebcm,bsec->bsm', expert_out, combine_mask)
            return final
        key = jax.random.key(seed)
        k1, k2, k3, k4, k5 = jax.random.split(key, 5)
        s_h = 1.0 / np.sqrt(H)
        s_f = 1.0 / np.sqrt(F)
        return {'hidden_states': jax.random.normal(k1, (B, S, H), dtype=jnp.float32), 'gate_w': jax.random.normal(k2, (E, H), dtype=jnp.float32) * s_h, 'w1': jax.random.normal(k3, (E, H, F), dtype=jnp.float32) * s_h, 'w2': jax.random.normal(k4, (E, F, H), dtype=jnp.float32) * s_f, 'w3': jax.random.normal(k5, (E, H, F), dtype=jnp.float32) * s_h}
    _L0_ffn_in = _L0_ffn_setup()
    _d = {'L0_attn_x': _L0_attn_in['x'], 'L0_attn_Wq': _L0_attn_in['Wq'], 'L0_attn_Wk': _L0_attn_in['Wk'], 'L0_attn_Wv': _L0_attn_in['Wv'], 'L0_attn_Wb': _L0_attn_in['Wb'], 'L0_attn_Wg': _L0_attn_in['Wg'], 'L0_attn_Wo': _L0_attn_in['Wo'], 'L0_attn_norm_w': _L0_attn_in['norm_w'], 'L0_ffn_gate_w': _L0_ffn_in['gate_w'], 'L0_ffn_w1': _L0_ffn_in['w1'], 'L0_ffn_w2': _L0_ffn_in['w2'], 'L0_ffn_w3': _L0_ffn_in['w3']}
    _x0 = _d['L0_attn_x']
    _d['L0_attn_x'] = jax.random.normal(jax.random.fold_in(jax.random.key(seed), 1), (2, 2048, 128), dtype=_x0.dtype)
    del _x0
    return _d

def reference(L0_attn_x, L0_attn_Wq, L0_attn_Wk, L0_attn_Wv, L0_attn_Wb, L0_attn_Wg, L0_attn_Wo, L0_attn_norm_w, L0_ffn_gate_w, L0_ffn_w1, L0_ffn_w2, L0_ffn_w3):

    def _L0_attn_ref(x, Wq, Wk, Wv, Wb, Wg, Wo, norm_w):
        import jax, jax.numpy as jnp
        import numpy as np
        D_MODEL = 128
        H = 4
        DK = 128
        DV = 32
        EPS = 1e-05
        SCALE = DK ** (-0.5)

        def _delta_rule(q, k, v, beta):
            b = q.shape[0]
            qt = jnp.moveaxis(q, 1, 0)
            kt = jnp.moveaxis(k, 1, 0)
            vt = jnp.moveaxis(v, 1, 0)
            bt = jnp.moveaxis(beta, 1, 0)
            S0 = jnp.zeros((b, H, DK, DV), q.dtype)

            def step(S, inp):
                q_t, k_t, v_t, b_t = inp
                pred = jnp.einsum('bhk,bhkv->bhv', k_t, S)
                delta = (v_t - pred) * b_t[..., None]
                S = S + k_t[..., :, None] * delta[..., None, :]
                o_t = jnp.einsum('bhk,bhkv->bhv', q_t, S)
                return (S, o_t)
            _, o = jax.lax.scan(step, S0, (qt, kt, vt, bt))
            return jnp.moveaxis(o, 0, 1)
        b, n, _ = x.shape
        q = (x @ Wq).reshape(b, n, H, DK)
        k = (x @ Wk).reshape(b, n, H, DK)
        v = (x @ Wv).reshape(b, n, H, DV)
        beta = jax.nn.sigmoid(x @ Wb)
        k = k * jax.lax.rsqrt(jnp.sum(k * k, axis=-1, keepdims=True) + 1e-12)
        q = q * SCALE
        o = _delta_rule(q, k, v, beta)
        g = (x @ Wg).reshape(b, n, H, DV)
        o = o * jax.lax.rsqrt(jnp.mean(o * o, axis=-1, keepdims=True) + EPS) * norm_w
        o = o * (g * jax.nn.sigmoid(g))
        return o.reshape(b, n, H * DV) @ Wo

    def _L0_ffn_ref(hidden_states, gate_w, w1, w2, w3):
        import jax, jax.numpy as jnp
        import numpy as np
        B, S, H, F, E, K = (4, 256, 128, 448, 8, 2)
        CAP_FACTOR = 1.25

        def _moe_forward(hidden_states, gate_w, w1, w2, w3):
            b, s, h = hidden_states.shape
            dtype = hidden_states.dtype
            x = hidden_states.reshape(-1, h)
            router_logits = x @ gate_w.T
            expert_weights = jax.nn.softmax(router_logits.astype(jnp.float32), axis=1)
            _, selected_experts = jax.lax.top_k(expert_weights, K)
            top_k_idx = selected_experts.reshape(b, s, K)
            probs = expert_weights.reshape(b, s, E)
            capacity = int(s * K / E * CAP_FACTOR)
            expert_mask = jax.nn.one_hot(top_k_idx, E, dtype=jnp.int32)
            mask_fused = expert_mask.reshape(b, s * K, E)
            count_fused = jnp.cumsum(mask_fused, axis=1)
            count = count_fused.reshape(b, s, K, E)
            trunc_mask = expert_mask * (count <= capacity).astype(jnp.int32)
            combined_mask = trunc_mask.sum(axis=2)
            masked_probs = probs * combined_mask
            pos_fused = mask_fused * count_fused
            pos = pos_fused.reshape(b, s, K, E)
            combined_pos = pos.sum(axis=2) * combined_mask
            pos_in_cap = jax.nn.one_hot(combined_pos, capacity + 1, dtype=jnp.int32)
            combine_mask = masked_probs[..., None] * pos_in_cap
            combine_mask = combine_mask[..., 1:].astype(dtype)
            dispatch_mask = (combine_mask != 0).astype(dtype)
            dispatch = jnp.einsum('bsm,bsec->ebcm', hidden_states, dispatch_mask)
            h1 = jnp.einsum('ebcm,emh->ebch', dispatch, w1)
            h3 = jnp.einsum('ebcm,emh->ebch', dispatch, w3)
            expert_out = jnp.einsum('ebch,ehm->ebcm', jax.nn.silu(h1) * h3, w2)
            final = jnp.einsum('ebcm,bsec->bsm', expert_out, combine_mask)
            return final
        return _moe_forward(hidden_states, gate_w, w1, w2, w3)
    x = L0_attn_x
    x = _layernorm(x + _L0_attn_ref(x, L0_attn_Wq, L0_attn_Wk, L0_attn_Wv, L0_attn_Wb, L0_attn_Wg, L0_attn_Wo, L0_attn_norm_w), axis=-1)
    x = _layernorm(x + _L0_ffn_ref(x, L0_ffn_gate_w, L0_ffn_w1, L0_ffn_w2, L0_ffn_w3), axis=-1)
    return x

_drawn_inputs = setup_inputs


def setup_inputs(seed=0):
    import zlib

    import numpy as np

    out = dict(_drawn_inputs(seed))
    spreads = {'L0_attn_norm_w': (1.0, 0.2)}
    factors = {}
    for name, (base, spread) in spreads.items():
        noise = np.random.default_rng([zlib.crc32(name.encode()), seed]).standard_normal(out[name].shape)
        drawn = base * np.exp(spread * noise) if base else spread * noise
        out[name] = jnp.asarray(drawn.astype(out[name].dtype))
    for name, factor in factors.items():
        out[name] = (out[name] * factor).astype(out[name].dtype)
    return out
```

```python
from contextlib import ExitStack

import numpy as np

import concourse.bass as bass
from concourse import mybir

F32 = mybir.dt.float32
BF16 = mybir.dt.bfloat16
I32 = mybir.dt.int32
U32 = mybir.dt.uint32
ALU = mybir.AluOpType
ACT = mybir.ActivationFunctionType
AX = mybir.AxisListType

P = 128
B, S, D = 2, 2048, 128
H, DK, DV = 4, 128, 32
E, F, TOPK = 8, 448, 2
CAP = int(S * TOPK / E * 1.25)
FC, FW = 4, F // 4
NT = B * S // P
NP = NT // 2
PB = NP // B
U = 2 * H
ROWS = B * E * CAP
SPARE = 4 * P
CT = CAP // P
HALF = CAP // 2
EPS = 1e-5
SCALE = DK ** -0.5
LOOP0, LOOP1 = 2, NP - 2


def wait(eng, sem, value):
    if isinstance(value, int) and value <= 0:
        return
    eng.wait_ge(sem, value)


def apart(eng):
    eng.nop(nofuse=True)


class Link:

    def __init__(self, eng, sem):
        self.eng, self.sem, self.n, self.off = eng, sem, 0, 0

    def __call__(self, ins):
        ins.then_inc(self.sem, 1)
        self.n += 1
        self.eng.wait_ge(self.sem, self.n + self.off)

    def enter(self, step, per_step):
        self.start, self.per, self.off = self.n, per_step, step * per_step

    def leave(self, steps):
        assert self.n - self.start == self.per, (self.n - self.start, self.per)
        self.n, self.off = self.start + self.per * steps, 0


def bc(ap, axis, n):
    shape = list(ap.shape)
    shape.insert(axis, n)
    return ap.unsqueeze(axis).to_broadcast(shape)


def build(nc, x, xT, Wq, Wk, Wvg, Wb, Wo, norm_w, gateT, w1, w2, w3, out):
    xs_d = nc.dram_tensor("slots_in", (ROWS + SPARE, D), F32, kind="Internal").ap()
    ys_d = nc.dram_tensor("slots_out", (ROWS + SPARE, D), F32, kind="Internal").ap()
    x1_d = nc.dram_tensor("x1_store", (NT * P, D), F32, kind="Internal").ap()
    ad_d = nc.dram_tensor("a_diag", (U, P, 32), F32, kind="Internal").ap()
    xi_d = nc.dram_tensor("inv16", (2, U, P, 16), F32, kind="Internal").ap()
    x_v = x.rearrange("(t p) d -> p t d", p=P)
    x1_v = x1_d.rearrange("(t p) d -> p t d", p=P)
    out_v = out.rearrange("(t p) d -> p t d", p=P)

    ctx = ExitStack()
    with ctx:
        def sb(name, shape, dt=F32):
            return ctx.enter_context(nc.sbuf_tensor(name, shape, dt))

        def sem(name):
            return ctx.enter_context(nc.semaphore(name))

        ps = ctx.enter_context(nc.psum_tensor("ps", [P, 8, 512], F32))

        ident = sb("ident", [P, P])
        strict = sb("strict", [P, P])
        upper = sb("upper", [P, P])
        tri = sb("tri", [P, P], BF16)
        ones = sb("ones", [P, P], BF16)
        iota8 = sb("iota8", [P, E])
        pidx = sb("pidx", [P, 1], I32)
        pbit = sb("pbit", [P, 1], I32)
        pcol = sb("pcol", [P, 1])
        low = sb("low", [P, 1])
        high = sb("high", [P, 1])
        spare = sb("spare", [P, 4])
        keep_s = sb("keep_s", [P, NP + 1])
        keep_c = sb("keep_c", [P, NP + 1])
        base = sb("base", [P, NP + 1])
        id16 = sb("id16", [64, 16, 16])
        zeros = sb("zeros", [P, 8 * P])
        wq = sb("wq", [P, H * DK])
        wk = sb("wk", [P, H * DK])
        wvg = sb("wvg", [P, 2 * H * DV])
        wb = sb("wb", [P, H])
        wo0 = sb("wo0", [P, D])
        wo = sb("wo", [P, D])
        nw = sb("nw", [P, 1])
        gt = sb("gt", [P, E])

        xTs = sb("xTs", [P, 2, 2 * P])
        xk = sb("xk", [P, 2, 2, D])
        KT = sb("KT", [P, 2, H, 2 * P])
        QT = sb("QT", [P, 2, H, 2 * P])
        K = sb("K", [P, 2, 2, H * DK])
        A = sb("A", [P, 2, U, P])
        PT = sb("PT", [P, 2, U, P])
        VG = sb("VG", [P, 2, 2 * H * DV])
        Vp = sb("Vp", [P, 2, 2, H * DV])
        silu = sb("silu", [P, 2, 2, H * DV])
        c2 = sb("c2", [P, 2, U])
        eb = sb("eb", [P, U])
        bden = sb("bden", [P, U])
        beta = sb("beta", [P, U])
        ss = sb("ss", [P, U])
        ssp = sb("ssp", [P, U])
        rr = sb("rr", [P, U])
        lnk = sb("lnk", [P, U])
        rk = sb("rk", [P, U])
        br = sb("br", [P, U])
        eg = sb("eg", [P, 2, H * DV])
        gden = sb("gden", [P, 2, H * DV])
        sig = sb("sig", [P, 2, H * DV])
        junk = sb("junk", [P, U, P])
        ab = sb("ab", [64, 16, 16])
        xs = sb("xs", [64, 16, 16])
        xsT = sb("xsT", [64, 16, 16])
        prod = sb("prod", [64, 240])
        ac = sb("ac", [P, U, 16])
        x16 = sb("x16", [P, U, 16])
        x16T = sb("x16T", [P, U, 16])
        m32 = sb("m32", [P, U, 32])
        x16d = sb("x16d", [P, U, 32])
        z32 = sb("z32", [P, U, 16])
        x32T = sb("x32T", [P, U, 32])
        x32 = sb("x32", [P, U, 32])
        z64 = sb("z64", [P, U, 32])
        x64 = sb("x64", [64, U, 64])
        z128 = sb("z128", [64, U, 64])
        TT = sb("TT", [P, U, P])
        St = sb("St", [P, H * DV])
        tmp = sb("tmp", [P, H * DV])
        R = sb("R", [P, H * DV])
        dl = sb("dl", [P, H * DV])
        o = sb("o", [P, 2, H * DV])
        osq = sb("osq", [P, 2, H * DV])
        oss = sb("oss", [P, U])
        oms = sb("oms", [P, U])
        oln = sb("oln", [P, U])
        orms = sb("orms", [P, U])
        on = sb("on", [P, 2, H * DV])
        og = sb("og", [P, 2, H * DV])
        oT = sb("oT", [P, 2 * P])
        r1 = sb("r1", [P, 2, D])
        bst = sb("bst", [P, 2, 6])
        mv = sb("mv", [P, 2, 2])
        ve = sb("ve", [P, 2])
        vl = sb("vl", [P, 2])
        rstd = sb("rstd", [P, 2])
        x1 = sb("x1", [P, 2, 2, D])
        x1T = sb("x1T", [P, 2 * P])
        lg = sb("lg", [P, 2, E])
        v8 = sb("v8", [P, 2, 8])
        i8 = sb("i8", [P, 2, 8], U32)
        nm = sb("nm", [P, 2])
        e8 = sb("e8", [P, 2, 8])
        es = sb("es", [P, 2])
        idxf = sb("idxf", [P, 2, TOPK])
        oh = sb("oh", [P, 2, TOPK, E])
        M = sb("M", [P, 2, E], BF16)
        cc = sb("cc", [P, 2, E])
        carry0 = sb("carry0", [P, E])
        carry = sb("carry", [P, E])
        pr = sb("pr", [P, 2, TOPK, E])
        cnt = sb("cnt", [P, 4])
        valid = sb("valid", [P, 4])
        sl = sb("sl", [P, 4])
        sd = sb("sd", [P, 4])
        sv = sb("sv", [P, 4])
        slf = sb("slf", [P, 4])
        rs = sb("rs", [P, 2])
        wv = sb("wv", [P, 2, TOPK])
        slot = sb("slot", [P, 2, 4], U32)
        gates = sb("gates", [P, 4 * NP])
        slots = sb("slots", [P, 4 * NP], U32)

        w1s = sb("w1s", [P, 2, F])
        w3s = sb("w3s", [P, 2, F])
        w2s = sb("w2s", [FW, 2, FC, D])
        xe = sb("xe", [P, 2, CT, D])
        xeT = sb("xeT", [P, 2, CAP])
        hs = sb("hs", [FW, 2, HALF])
        hb = sb("hb", [FW, 2, FC, CAP])
        ye = sb("ye", [P, 2, CT, D])
        gi = sb("gi", [P, 2, 4], U32)
        gb = sb("gb", [P, 2, 4, D])
        x1c = sb("x1c", [P, 2, 2, D])
        ya = sb("ya", [P, 2, D])
        yb = sb("yb", [P, 2, D])
        yo = sb("yo", [P, 2, 2, D])

        w_ld = sem("w_ld")
        zero_st = sem("zero_st")
        consts_pool = sem("consts_pool")
        consts_dve = sem("consts_dve")
        wo_ready = sem("wo_ready")
        xT_ld = [sem("xT_ld0"), sem("xT_ld1")]
        xk_ld = [sem("xk_ld0"), sem("xk_ld1")]
        filled = sem("filled")
        freed_act = sem("freed_act")
        freed_dve = sem("freed_dve")
        eb_ready = sem("eb_ready")
        ss_ready = sem("ss_ready")
        ssp_ready = sem("ssp_ready")
        rk_ready = sem("rk_ready")
        br_ready = sem("br_ready")
        eg_ready = sem("eg_ready")
        sig_ready = sem("sig_ready")
        gate_ready = sem("gate_ready")
        a_st = sem("a_st")
        ab_ld = sem("ab_ld")
        ac_ld = sem("ac_ld")
        solved = sem("solved")
        xi_st = sem("xi_st")
        x16_ld = sem("x16_ld")
        prep = sem("prep")
        lvl_mm = sem("lvl_mm")
        lvl_dve = sem("lvl_dve")
        lvl_act = sem("lvl_act")
        x64_diag = sem("x64_diag")
        chain_mm = sem("chain_mm")
        r_ready = sem("r_ready")
        s_ready = sem("s_ready")
        d_ready = sem("d_ready")
        o_ready = sem("o_ready")
        osq_ready = sem("osq_ready")
        oms_ready = sem("oms_ready")
        orms_ready = sem("orms_ready")
        og_ready = sem("og_ready")
        out_mm = sem("out_mm")
        oT_ready = sem("oT_ready")
        r1_ready = sem("r1_ready")
        ve_ready = sem("ve_ready")
        rstd_ready = sem("rstd_ready")
        x1_ready = sem("x1_ready")
        x1_st = [sem("x1_st0"), sem("x1_st1")]
        x1T_ready = sem("x1T_ready")
        nm_ready = sem("nm_ready")
        e8_ready = sem("e8_ready")
        M_ready = sem("M_ready")
        slot_ready = sem("slot_ready")
        scat = [sem("scat0"), sem("scat1")]
        link_dve = sem("link_dve")
        link_act = sem("link_act")
        link_pool = sem("link_pool")
        ew_ld = [sem("ew_ld0"), sem("ew_ld1")]
        xe_ld = [sem("xe_ld0"), sem("xe_ld1")]
        xeT_mm = sem("xeT_mm")
        xeT_ready = sem("xeT_ready")
        h_mm = sem("h_mm")
        hs_ready = sem("hs_ready")
        h_ready = sem("h_ready")
        y_mm = sem("y_mm")
        ye_ready = sem("ye_ready")
        ye_st = [sem("ye_st0"), sem("ye_st1")]
        gi_ready = sem("gi_ready")
        gb_ld = [sem("gb_ld0"), sem("gb_ld1")]
        x1c_ld = [sem("x1c_ld0"), sem("x1c_ld1")]
        cve_ready = sem("cve_ready")
        crstd_ready = sem("crstd_ready")
        yo_ready = sem("yo_ready")
        out_st = [sem("out_st0"), sem("out_st1")]

        block = ctx.enter_context(nc.Block())

        def phase_a(eng, step, link=None, per_body=0):
            step(-1, 1, True, False, False)
            step(0, 0, True, True, False)
            step(1, 1, True, True, True)
            with eng.Fori(0, (LOOP1 - LOOP0) // 2) as i:
                if link:
                    link.enter(i, per_body)
                step(LOOP0 + 2 * i, 0, True, True, True)
                step(LOOP0 + 2 * i + 1, 1, True, True, True)
            if link:
                link.leave((LOOP1 - LOOP0) // 2)
            step(NP - 2, 0, True, True, True)
            step(NP - 1, 1, False, True, True)
            step(NP, 0, False, False, True)

        @block.sync
        def _(sp):
            for dst, src in ((wk, Wk), (wb, Wb), (wq, Wq), (wvg, Wvg), (wo0, Wo), (gt, gateT)):
                sp.dma_start(dst[:], src[:, :]).then_inc(w_ld, 16)
            for h in range(H):
                sp.dma_start(nw[h * DV:(h + 1) * DV, :], norm_w.rearrange("(d o) -> d o", o=1)).then_inc(w_ld, 16)

            def load_xT(r, par):
                wait(sp, filled, 12 * (r - 2) + 10)
                sp.dma_start(xTs[:, par, :], xT[:, bass.ds(r * 2 * P, 2 * P)]).then_inc(xT_ld[par], 16)

            def step(p, par, s1, main, outq):
                q = p + 1
                if isinstance(p, int) and p == -1:
                    load_xT(0, 0)
                    sp.wait_ge(consts_pool, 1)
                    for k in range(ROWS // P // 8):
                        sp.dma_start(xs_d[k * 8 * P:(k + 1) * 8 * P, :].rearrange("(p r) d -> p (r d)", p=P),
                                     zeros[:]).then_inc(zero_st, 16)
                    sp.dma_start(ys_d[ROWS:ROWS + SPARE, :].rearrange("(p r) d -> p (r d)", p=P),
                                 zeros[:, 0:SPARE]).then_inc(zero_st, 16)
                if not (isinstance(p, int) and p + 2 > NP - 1):
                    load_xT(p + 2, par)
                if main:
                    wait(sp, r1_ready, p - 1)
                    sp.dma_start(xk[:, par], x_v[:, bass.ds(p * 2, 2), :]).then_inc(xk_ld[par], 16)
                if outq:
                    wait(sp, x1_ready, p)
                    sp.dma_start(x1_v[:, bass.ds(2 * p - 2, 2), :], x1[:, 1 - par]).then_inc(x1_st[1 - par], 16)
                if s1:
                    sp.wait_ge(freed_dve, 4 * q + 2)
                    apart(sp)
                    wait(sp, ac_ld, 16 * q)
                    for k in range(4):
                        sp.dma_start(ad_d[:, 32 * k:32 * k + 32, :].rearrange("u r c -> r u c"),
                                     A[32 * k:32 * k + 32, 1 - par, :, 32 * k:32 * k + 32]).then_inc(a_st, 16)
                    sp.wait_ge(a_st, 64 * q + 64)
                    wait(sp, solved, q)
                    blocks = ad_d.rearrange("u (m r) c -> (u m) r c", r=32)
                    for k in range(2):
                        sp.dma_start(ab[32 * k:32 * k + 32],
                                     blocks[:, 16 * k:16 * k + 16, 16 * k:16 * k + 16]).then_inc(ab_ld, 16)
                    wait(sp, prep, q)
                    sp.dma_start(ac[:], ad_d[:, :, 0:16].rearrange("u r c -> r u c")).then_inc(ac_ld, 16)
                    sp.wait_ge(solved, q + 1)
                    for t, src in enumerate((xs, xsT)):
                        inv = xi_d[t].rearrange("u (m k r) c -> k (u m) (r c)", k=2, r=16)
                        for k in range(2):
                            sp.dma_start(inv[k], src[32 * k:32 * k + 32].rearrange("p r c -> p (r c)")).then_inc(xi_st, 16)
                    sp.wait_ge(xi_st, 64 * q + 64)
                    wait(sp, lvl_dve, 4 * (q - 1) + 2)
                    sp.dma_start(x16[:], xi_d[0].rearrange("u r c -> r u c")).then_inc(x16_ld, 16)
                    sp.dma_start(x16T[:], xi_d[1].rearrange("u r c -> r u c")).then_inc(x16_ld, 16)

            phase_a(sp, step)

            sp.wait_ge(x1_st[0], 16 * (NP // 2))
            sp.wait_ge(x1_st[1], 16 * (NP // 2))
            sp.wait_ge(scat[0], 64 * (NP // 2))
            sp.wait_ge(scat[1], 64 * (NP // 2))
            sp.wait_ge(zero_st, 16 * (ROWS // P // 8 + 1))

            xs_n = xs_d[0:ROWS, :].rearrange("(n p i) d -> n p i d", p=P, i=CT)
            ys_n = ys_d[0:ROWS, :].rearrange("(n p i) d -> n p i d", p=P, i=CT)

            def load_unit(n, e, par):
                wait(sp, h_mm, 8 * (n - 1))
                sp.dma_start(w1s[:, par, :], w1[bass.ds(e, 1)].rearrange("o p f -> p (o f)")).then_inc(ew_ld[par], 16)
                sp.dma_start(w3s[:, par, :], w3[bass.ds(e, 1)].rearrange("o p f -> p (o f)")).then_inc(ew_ld[par], 16)
                wait(sp, y_mm, n - 1)
                sp.dma_start(w2s[:, par], w2[bass.ds(e, 1)].rearrange("o (c p) d -> p (o c) d", p=FW)).then_inc(ew_ld[par], 16)
                wait(sp, xeT_mm, n - 1)
                sp.dma_start(xe[:, par], xs_n[bass.ds(n, 1)].rearrange("o p i d -> p (o i) d")).then_inc(xe_ld[par], 16)

            def store_unit(n, par):
                sp.wait_ge(ye_ready, n + 1)
                sp.dma_start(ys_n[bass.ds(n, 1)].rearrange("o p i d -> p (o i) d"), ye[:, par]).then_inc(ye_st[par], 16)

            load_unit(0, 0, 0)
            load_unit(1, 1, 1)
            for b in range(B):
                with sp.Fori(0, E // 2 - 1) as i:
                    for par in range(2):
                        load_unit(b * E + 2 * i + par + 2, 2 * i + par + 2, par)
                        store_unit(b * E + 2 * i + par, par)
                for par in range(2):
                    if b + 1 < B:
                        load_unit((b + 1) * E + par, par, par)
                    store_unit(b * E + E - 2 + par, par)

            sp.wait_ge(ye_st[0], 16 * B * E // 2)
            sp.wait_ge(ye_st[1], 16 * B * E // 2)

            def load_x1(p, par):
                wait(sp, yo_ready, p - 1)
                sp.dma_start(x1c[:, par], x1_v[:, bass.ds(2 * p, 2), :]).then_inc(x1c_ld[par], 16)

            def store(p, par):
                sp.wait_ge(yo_ready, p + 1)
                sp.dma_start(out_v[:, bass.ds(2 * p, 2), :], yo[:, par]).then_inc(out_st[par], 16)

            load_x1(0, 0)
            load_x1(1, 1)
            with sp.Fori(0, NP // 2 - 1) as i:
                for par in range(2):
                    load_x1(2 * i + par + 2, par)
                    store(2 * i + par, par)
            for par in range(2):
                store(NP - 2 + par, par)
            for par in range(2):
                sp.wait_ge(out_st[par], 16 * NP // 2)

        @block.tensor
        def _(pe):
            mm = nc.tensor.matmul
            fill_bank = [g % 3 for g in range(12)]
            ZB, WB, CB, OB, MB = 3, 4, 5, 6, 7

            pe.wait_ge(w_ld, 160)
            pe.wait_ge(consts_pool, 5)

            def act_free(q, n):
                wait(pe, freed_act, 8 * q + n)

            def dve_free(q, n):
                wait(pe, freed_dve, 4 * q + n)

            def kt(q, par, g):
                if g == 0:
                    pe.wait_ge(xT_ld[par], xt_count(q))
                    act_free(q - 1, 8)
                else:
                    dve_free(q - 1, 3)
                for k in range(2):
                    h = 2 * g + k
                    last = mm(ps[:, fill_bank[g], 256 * k:256 * k + 256], wk[:, DK * h:DK * h + DK], xTs[:, par, :],
                              start=True, stop=True)
                last.then_inc(filled, 1)

            def beta_k0(q, par):
                dve_free(q - 1, 4)
                for j in range(2):
                    last = mm(ps[:, fill_bank[2], 4 * j:4 * j + 4], xTs[:, par, P * j:P * j + P], wb[:, :],
                              start=True, stop=True)
                last.then_inc(filled, 1)
                k_tok(q, par, 0)

            def k_tok(q, par, j):
                act_free(q, 1 + j)
                mm(ps[:, fill_bank[3 + j], :], xTs[:, par, P * j:P * j + P], wk[:, :],
                   start=True, stop=True).then_inc(filled, 1)

            def kk(q, par, j):
                act_free(q, 3 + j)
                for h in range(H):
                    kc = KT[:, par, h, P * j:P * j + P]
                    last = mm(ps[:, fill_bank[5 + j], P * h:P * h + P], kc, kc, start=True, stop=True)
                last.then_inc(filled, 1)

            def vg(q, par):
                act_free(q, 5)
                for j in range(2):
                    last = mm(ps[:, fill_bank[7], 256 * j:256 * j + 256], xTs[:, par, P * j:P * j + P], wvg[:, :],
                              start=True, stop=True)
                last.then_inc(filled, 1)

            def qt(q, par, g):
                dve_free(q, 1 + g)
                for k in range(2):
                    h = 2 * g + k
                    last = mm(ps[:, fill_bank[8 + g], 256 * k:256 * k + 256], wq[:, DK * h:DK * h + DK], xTs[:, par, :],
                              start=True, stop=True)
                last.then_inc(filled, 1)

            def kq(q, par, j):
                act_free(q, 8)
                for h in range(H):
                    last = mm(ps[:, fill_bank[10 + j], P * h:P * h + P], KT[:, par, h, P * j:P * j + P],
                              QT[:, par, h, P * j:P * j + P], start=True, stop=True)
                last.then_inc(filled, 1)

            def z_32(p):
                pe.wait_ge(prep, p + 1)
                wait(pe, lvl_act, 3 * p - 1)
                apart(pe)
                for u in range(U):
                    for k in range(4):
                        s = slice(32 * k, 32 * k + 32)
                        last = mm(ps[s, ZB, 16 * u:16 * u + 16], m32[s, u, :], x16T[s, u, :], start=True, stop=True)
                last.then_inc(lvl_mm, 1)

            def w_32(p):
                pe.wait_ge(lvl_dve, 4 * p + 1)
                wait(pe, lvl_act, 3 * p)
                apart(pe)
                for u in range(U):
                    for k in range(4):
                        s = slice(32 * k, 32 * k + 32)
                        last = mm(ps[s, WB, 16 * u:16 * u + 16], x16d[s, u, :], z32[s, u, :], start=True, stop=True)
                last.then_inc(lvl_mm, 1)

            def z_64(p, par):
                pe.wait_ge(lvl_dve, 4 * p + 2)
                apart(pe)
                for u in range(U):
                    for m in range(2):
                        s = slice(64 * m + 32, 64 * m + 64)
                        last = mm(ps[64 * m:64 * m + 64, ZB, 32 * u:32 * u + 32], A[s, par, u, 64 * m:64 * m + 64],
                                  x32T[s, u, :], start=True, stop=True)
                last.then_inc(lvl_mm, 1)

            def w_64(p):
                pe.wait_ge(lvl_dve, 4 * p + 3)
                apart(pe)
                for u in range(U):
                    for m in range(2):
                        s = slice(64 * m, 64 * m + 32)
                        last = mm(ps[s, WB, 32 * u:32 * u + 32], x32[s, u, :], z64[s, u, :], start=True, stop=True)
                last.then_inc(lvl_mm, 1)

            def z_128(p, par):
                pe.wait_ge(lvl_dve, 4 * p + 4)
                pe.wait_ge(lvl_act, 3 * p + 1)
                apart(pe)
                for u in range(U):
                    last = mm(ps[0:64, ZB, 64 * u:64 * u + 64], A[64:128, par, u, 0:64], TT[64:128, u, 64:128],
                              start=True, stop=True)
                last.then_inc(lvl_mm, 1)

            def w_128(p):
                pe.wait_ge(lvl_act, 3 * p + 2)
                pe.wait_ge(x64_diag, p + 1)
                apart(pe)
                for u in range(U):
                    last = mm(ps[0:64, WB, 64 * u:64 * u + 64], x64[:, u, :], z128[:, u, :], start=True, stop=True)
                last.then_inc(lvl_mm, 1)

            def ks(p, par, j):
                if j == 0:
                    wait(pe, s_ready, 2 * p) if not isinstance(p, int) or p > 0 else pe.wait_ge(consts_dve, 1)
                else:
                    pe.wait_ge(s_ready, 2 * p + 1)
                for h in range(H):
                    mm(ps[:, CB, 32 * h:32 * h + 32], KT[:, par, h, P * j:P * j + P], St[:, 32 * h:32 * h + 32],
                       start=True, stop=True)
                wait(pe, o_ready, 2 * p + j)
                for h in range(H):
                    last = mm(ps[:, OB, 32 * h:32 * h + 32], QT[:, par, h, P * j:P * j + P],
                              St[:, 32 * h:32 * h + 32], start=(h == 0), stop=False, skip_group_check=True)
                last.then_inc(chain_mm, 1)

            def t_r(p, j):
                pe.wait_ge(r_ready, 2 * p + j + 1)
                if j == 0:
                    pe.wait_ge(lvl_act, 3 * p + 3)
                for h in range(H):
                    last = mm(ps[:, CB, 128 + 32 * h:160 + 32 * h], TT[:, H * j + h, :], R[:, 32 * h:32 * h + 32],
                              start=True, stop=True)
                last.then_inc(chain_mm, 1)

            def p_d(p, par, j):
                pe.wait_ge(d_ready, 2 * p + j + 1)
                for h in range(H):
                    mm(ps[:, CB, 256 + 32 * h:288 + 32 * h], K[:, par, j, DK * h:DK * h + DK],
                       dl[:, 32 * h:32 * h + 32], start=True, stop=True)
                if j == 0:
                    pe.wait_ge(freed_dve, 4 * p + 4)
                for h in range(H):
                    last = mm(ps[:, OB, 32 * h:32 * h + 32], PT[:, par, H * j + h, :], dl[:, 32 * h:32 * h + 32],
                              start=False, stop=(h == H - 1), skip_group_check=True)
                last.then_inc(chain_mm, 1)

            def o_t(q):
                pe.wait_ge(og_ready, q + 1)
                wait(pe, slot_ready, q)
                for j in range(2):
                    last = nc.tensor.transpose(ps[:, MB, P * j:P * j + P], og[:, j, :], ident[:])
                last.then_inc(out_mm, 1)

            def o_proj(q):
                pe.wait_ge(oT_ready, q + 1)
                pe.wait_ge(wo_ready, 1)
                for j in range(2):
                    last = mm(ps[:, MB, P * j:P * j + P], oT[:, P * j:P * j + P], wo[:], start=True, stop=True)
                last.then_inc(out_mm, 1)

            def x1_t(q, par):
                pe.wait_ge(x1_ready, q + 1)
                for j in range(2):
                    last = nc.tensor.transpose(ps[:, MB, P * j:P * j + P], x1[:, par, j, :], ident[:])
                last.then_inc(out_mm, 1)

            def logits(q):
                pe.wait_ge(x1T_ready, q + 1)
                for j in range(2):
                    last = mm(ps[:, MB, E * j:E * j + E], x1T[:, P * j:P * j + P], gt[:], start=True, stop=True)
                last.then_inc(out_mm, 1)

            def cum(q):
                pe.wait_ge(M_ready, q + 1)
                mm(ps[:, MB, 0:E], tri[:], M[:, 0, :], start=True, stop=True)
                mm(ps[:, MB, E:2 * E], tri[:], M[:, 1, :], start=True, stop=False)
                mm(ps[:, MB, E:2 * E], ones[:], M[:, 0, :], start=False, stop=True)
                mm(ps[:, MB, 2 * E:3 * E], ones[:], M[:, 0, :], start=True, stop=False)
                mm(ps[:, MB, 2 * E:3 * E], ones[:], M[:, 1, :], start=False, stop=True).then_inc(out_mm, 1)

            def step(p, par, s1, main, outq):
                q, npar = p + 1, 1 - par
                if s1:
                    kt(q, npar, 0)
                    kt(q, npar, 1)
                if main:
                    z_32(p)
                if s1:
                    beta_k0(q, npar)
                if main:
                    w_32(p)
                if s1:
                    k_tok(q, npar, 1)
                if outq:
                    o_t(p - 1)
                if main:
                    z_64(p, par)
                if s1:
                    kk(q, npar, 0)
                if main:
                    w_64(p)
                if s1:
                    kk(q, npar, 1)
                if outq:
                    o_proj(p - 1)
                if main:
                    z_128(p, par)
                if s1:
                    vg(q, npar)
                if main:
                    w_128(p)
                if outq:
                    x1_t(p - 1, npar)
                if main:
                    ks(p, par, 0)
                if s1:
                    qt(q, npar, 0)
                if main:
                    t_r(p, 0)
                if s1:
                    qt(q, npar, 1)
                if outq:
                    logits(p - 1)
                if main:
                    p_d(p, par, 0)
                if s1:
                    kq(q, npar, 0)
                if main:
                    ks(p, par, 1)
                if outq:
                    cum(p - 1)
                if main:
                    t_r(p, 1)
                if s1:
                    kq(q, npar, 1)
                if main:
                    p_d(p, par, 1)

            def xt_count(q):
                return xt_counts[0](q)

            xt_counts = [None]

            def step_counted(p, par, s1, main, outq):
                npar = 1 - par
                xt_counts[0] = lambda q: 8 * q + 16 - 8 * npar
                step(p, par, s1, main, outq)

            phase_a(pe, step_counted)

            def flip(n, par):
                pe.wait_ge(xe_ld[par], 8 * n + 16 - 8 * par)
                wait(pe, xeT_ready, 2 * n)
                for i in range(CT):
                    last = nc.tensor.transpose(ps[:, i // 4, P * (i % 4):P * (i % 4) + P], xe[:, par, i, :], ident[:])
                last.then_inc(xeT_mm, 1)

            def hidden(n, par):
                pe.wait_ge(ew_ld[par], 3 * (8 * n + 16 - 8 * par))
                pe.wait_ge(xeT_ready, 2 * n + 2)
                for c in range(FC):
                    for g in range(2):
                        s = 2 * c + g
                        wait(pe, h_ready, 8 * n + s - 1)
                        cols = slice(HALF * g, HALF * g + HALF)
                        mm(ps[0:FW, 2 + g, 0:HALF], w1s[:, par, FW * c:FW * c + FW], xeT[:, par, cols],
                           start=True, stop=True)
                        mm(ps[0:FW, 4 + g, 0:HALF], w3s[:, par, FW * c:FW * c + FW], xeT[:, par, cols],
                           start=True, stop=True).then_inc(h_mm, 1)

            def down(n, par):
                pe.wait_ge(h_ready, 8 * n + 8)
                wait(pe, ye_ready, n)
                for i in range(CT):
                    for c in range(FC):
                        last = mm(ps[:, 6 + i // 4, P * (i % 4):P * (i % 4) + P], hb[:, par, c, P * i:P * i + P],
                                  w2s[:, par, c, :], start=(c == 0), stop=(c == FC - 1))
                last.then_inc(y_mm, 1)

            pe.wait_ge(slot_ready, NP)
            def unit(n, par):
                hidden(n, par)
                flip(n + 1, 1 - par)
                down(n, par)

            flip(0, 0)
            for par in range(2):
                unit(par, par)
            with pe.Fori(1, B * E // 2 - 1) as i:
                for par in range(2):
                    unit(2 * i + par, par)
            hidden(B * E - 2, 0)
            flip(B * E - 1, 1)
            down(B * E - 2, 0)
            hidden(B * E - 1, 1)
            down(B * E - 1, 1)

        @block.scalar
        def _(act):
            link = Link(act, link_act)
            af = nc.scalar.activation
            nc.scalar.preload_act_table_set("natural_log_exp_and_others")
            fill_bank = [g % 3 for g in range(12)]
            ZB, WB, CB, OB, MB = 3, 4, 5, 6, 7

            def rsqrt(out_ap, ln_ap, in_ap):
                link(af(ln_ap, in_ap, ACT.Ln))
                return af(out_ap, ln_ap, ACT.Exp, scale=-0.5)

            def step(p, par, s1, main, outq):
                q, npar = p + 1, 1 - par
                if s1:
                    for g in range(2):
                        act.wait_ge(filled, 12 * q + g + 1)
                        if g == 0:
                            wait(act, chain_mm, 6 * (q - 2) + 4)
                        af(KT[:, npar, 2 * g:2 * g + 2, :], ps[:, fill_bank[g], :].rearrange("p (h t) -> p h t", h=2),
                           ACT.Copy).then_inc(freed_act, 1)
                    act.wait_ge(filled, 12 * q + 3)
                    wait(act, br_ready, q)
                    af(eb[:], ps[:, fill_bank[2], 0:U], ACT.Exp, scale=-1.0).then_inc(freed_act, 1)
                    k_out(q, npar, 0)
                if main:
                    act.wait_ge(lvl_dve, 4 * p + 2)
                    wait(act, chain_mm, 6 * (p - 1) + 5)
                    for k in range(4):
                        s = slice(32 * k, 32 * k + 32)
                        last = af(TT[s, :, 32 * k:32 * k + 32], x32T[s, :, :], ACT.Copy)
                    last.then_inc(lvl_act, 1)
                    wait(act, lvl_mm, 6 * p)
                    for k in range(2):
                        s = slice(32 * k, 32 * k + 32)
                        last = af(x64[s, :, 32 * k:32 * k + 32], x32[s, :, :], ACT.Copy)
                    last.then_inc(x64_diag, 1)
                if s1:
                    k_out(q, npar, 1)
                if outq:
                    act.wait_ge(out_mm, 5 * (p - 1) + 1)
                    af(oT[:], ps[:, MB, 0:256], ACT.Copy).then_inc(oT_ready, 1)
                if s1:
                    act.wait_ge(ssp_ready, q + 1)
                    rsqrt(rk[:], lnk[:], ssp[:]).then_inc(rk_ready, 1)
                if outq:
                    act.wait_ge(ve_ready, p)
                    rsqrt(rstd[:], vl[:], ve[:]).then_inc(rstd_ready, 1)
                if main:
                    act.wait_ge(lvl_mm, 6 * p + 5)
                    af(z128[:], ps[0:64, ZB, :].rearrange("p (u c) -> p u c", u=U), ACT.Copy).then_inc(lvl_act, 1)
                if s1:
                    act.wait_ge(filled, 12 * q + 8)
                    wait(act, gate_ready, 2 * q)
                    af(VG[:], ps[:, fill_bank[7], :].rearrange("p (j c) -> p j c", j=2), ACT.Copy)
                    af(eg[:], ps[:, fill_bank[7], :].rearrange("p (j c) -> p j c", j=2)[:, :, H * DV:], ACT.Exp,
                       scale=-1.0).then_inc(freed_act, 1)
                if main:
                    act.wait_ge(lvl_mm, 6 * p + 6)
                    af(TT[0:64, :, 64:128], ps[0:64, WB, :].rearrange("p (u c) -> p u c", u=U), ACT.Copy,
                       scale=-1.0).then_inc(lvl_act, 1)
                if outq:
                    act.wait_ge(out_mm, 5 * (p - 1) + 3)
                    af(x1T[:], ps[:, MB, 0:256], ACT.Copy).then_inc(x1T_ready, 1)
                if s1:
                    q_out(q, npar, 0)
                if main:
                    delta(p, 0)
                if s1:
                    q_out(q, npar, 1)
                if main:
                    act.wait_ge(chain_mm, 6 * p + 3)
                    wait(act, og_ready, p)
                    af(o[:, 0, :], ps[:, OB, 0:H * DV], ACT.Copy).then_inc(o_ready, 1)
                if outq:
                    act.wait_ge(nm_ready, p)
                    for j in range(2):
                        last = af(e8[:, j, :], v8[:, j, :], ACT.Exp, bias=nm[:, j:j + 1], accum_out=es[:, j:j + 1])
                    last.then_inc(e8_ready, 1)
                if main:
                    delta(p, 1)
                    act.wait_ge(chain_mm, 6 * p + 6)
                    af(o[:, 1, :], ps[:, OB, 0:H * DV], ACT.Copy).then_inc(o_ready, 1)
                    act.wait_ge(oms_ready, p + 1)
                    rsqrt(orms[:], oln[:], oms[:]).then_inc(orms_ready, 1)

            def k_out(q, par, j):
                act.wait_ge(filled, 12 * q + 4 + j)
                if j == 0:
                    wait(act, chain_mm, 6 * (q - 1))
                af(K[:, par, j, :], ps[:, fill_bank[3 + j], :], ACT.Copy)
                for h in range(H):
                    last = af(junk[:, H * j + h, :], ps[:, fill_bank[3 + j], DK * h:DK * h + DK], ACT.Square,
                              accum_out=ss[:, H * j + h:H * j + h + 1])
                last.then_inc(freed_act, 1)

            def q_out(q, par, g):
                act.wait_ge(filled, 12 * q + 9 + g)
                af(QT[:, par, 2 * g:2 * g + 2, :], ps[:, fill_bank[8 + g], :].rearrange("p (h t) -> p h t", h=2),
                   ACT.Copy, scale=SCALE).then_inc(freed_act, 1)

            def delta(p, j):
                act.wait_ge(chain_mm, 6 * p + 3 * j + 2)
                af(dl[:], ps[:, CB, 128:256], ACT.Copy).then_inc(d_ready, 1)

            phase_a(act, step, link, ACT_LINKS)

            def turn(n, par):
                act.wait_ge(xeT_mm, n + 1)
                wait(act, h_mm, 8 * (n - 1))
                af(xeT[:, par, 0:512], ps[:, 0, :], ACT.Copy).then_inc(xeT_ready, 1)
                af(xeT[:, par, 512:CAP], ps[:, 1, 0:CAP - 512], ACT.Copy).then_inc(xeT_ready, 1)

            def gate(n, s):
                act.wait_ge(h_mm, 8 * n + s + 1)
                wait(act, h_ready, 8 * n + s - 1)
                af(hs[:, s % 2, :], ps[0:FW, 2 + s % 2, 0:HALF], ACT.Silu).then_inc(hs_ready, 1)

            def y_out(n, par):
                act.wait_ge(y_mm, n + 1)
                wait(act, ye_st[par], 8 * n - 8 * par)
                af(ye[:, par, 0:4, :], ps[:, 6, :].rearrange("p (i d) -> p i d", i=4), ACT.Copy)
                af(ye[:, par, 4, :], ps[:, 7, 0:P], ACT.Copy).then_inc(ye_ready, 1)

            turn(0, 0)
            for s in range(8):
                gate(0, s)
            turn(1, 1)
            y_out(0, 0)
            for s in range(8):
                gate(1, s)
            turn(2, 0)
            y_out(1, 1)
            with act.Fori(1, B * E // 2 - 1) as i:
                for par in range(2):
                    n = 2 * i + par
                    for s in range(8):
                        gate(n, s)
                    turn(n + 1, 1 - par)
                    y_out(n, par)
            for s in range(8):
                gate(B * E - 2, s)
            turn(B * E - 1, 1)
            y_out(B * E - 2, 0)
            for s in range(8):
                gate(B * E - 1, s)
            y_out(B * E - 1, 1)

            nc.scalar.preload_act_table_set("natural_log_exp_and_others")
            with act.Fori(0, NP // 2) as i:
                link.enter(i, 2)
                for par in range(2):
                    act.wait_ge(cve_ready, 2 * i + par + 1)
                    rsqrt(rstd[:], vl[:], ve[:]).then_inc(crstd_ready, 1)
            link.leave(NP // 2)

        @block.vector
        def _(dve):
            link = Link(dve, link_dve)
            v = nc.vector
            fill_bank = [g % 3 for g in range(12)]
            ZB, WB, CB, OB, MB = 3, 4, 5, 6, 7

            for t in (m32, TT, x64, St, carry):
                v.memset(t[:], 0.0)
            for t, at in ((keep_s, PB - 1), (keep_c, PB)):
                link(v.memset(t[:], 1.0))
                v.memset(t[:, at:at + 1], 0.0)
            link(v.memset(base[:], -1.0))
            v.memset(base[:, PB + 1:], float(E * CAP - 1))
            dve.wait_ge(consts_pool, 6)
            link(v.tensor_scalar(pbit[:], pidx[:], 16, None, ALU.bitwise_and))
            link(v.tensor_copy(pcol[:], pbit[:]))
            link(v.tensor_scalar(high[:], pcol[:], 1.0 / 16, None, ALU.mult))
            link(v.tensor_scalar(low[:], high[:], -1.0, 1.0, ALU.mult, ALU.add))
            link(v.tensor_copy(pcol[:], pidx[:]))
            for k in range(4):
                v.tensor_scalar(spare[:, k:k + 1], pcol[:], float(ROWS + P * k), None, ALU.add)
            v.tensor_copy(tri[:], upper[:])
            link(v.memset(ones[:], 1.0))
            v.tensor_copy(M[:, 0, :], tri[:, 0:E]).then_inc(consts_dve, 1)
            dve.wait_ge(w_ld, 160)
            v.tensor_scalar(wo[:], wo0[:], nw[:], None, ALU.mult).then_inc(wo_ready, 1)

            def step(p, par, s1, main, outq):
                q, npar = p + 1, 1 - par
                if main:
                    dve.wait_ge(x16_ld, 32 * p + 32)
                    dve.wait_ge(ac_ld, 16 * p + 16)
                    v.tensor_scalar(m32[:, :, 0:16], ac[:], high[:], None, ALU.mult)
                    v.tensor_scalar(x32T[:, :, 0:16], x16T[:], low[:], None, ALU.mult)
                    v.tensor_scalar(x16d[:, :, 0:16], x16[:], low[:], None, ALU.mult)
                    v.tensor_scalar(x16d[:, :, 16:32], x16[:], high[:], None, ALU.mult).then_inc(prep, 1)
                    dve.wait_ge(lvl_mm, 6 * p + 1)
                    v.tensor_copy(z32[:], ps[:, ZB, 0:128].rearrange("p (u c) -> p u c", u=U)).then_inc(lvl_dve, 1)
                    dve.wait_ge(lvl_mm, 6 * p + 2)
                    link(v.scalar_tensor_tensor(out=x32T[:, :, 16:32], in0=x16T[:], scalar=high[:],
                                                in1=ps[:, WB, 0:128].rearrange("p (u c) -> p u c", u=U),
                                                op0=ALU.mult, op1=ALU.subtract))
                    v.transpose(x32[:].rearrange("p u c -> p (u c)"),
                                x32T[:].rearrange("p u c -> p (u c)")).then_inc(lvl_dve, 1)
                if s1:
                    dve.wait_ge(freed_act, 8 * q + 3)
                    link(v.tensor_scalar(bden[:], eb[:], 1.0, None, ALU.add))
                    link(v.reciprocal(beta[:], bden[:]))
                    dve.wait_ge(freed_act, 8 * q + 5)
                    v.tensor_scalar(ssp[:], ss[:], 1e-12, None, ALU.add).then_inc(ssp_ready, 1)
                    dve.wait_ge(ssp_ready, q + 1)
                    link(v.reciprocal(rr[:], ssp[:]))
                    link(v.tensor_tensor(c2[:, npar, :], beta[:], rr[:], ALU.mult))
                if main:
                    dve.wait_ge(lvl_mm, 6 * p + 3)
                    v.tensor_copy(z64[:], ps[:, ZB, 0:256].rearrange("p (u c) -> p u c", u=U)).then_inc(lvl_dve, 1)
                if s1:
                    lower(q, npar, 0)
                    dve.wait_ge(rk_ready, q + 1)
                    v.tensor_tensor(br[:], beta[:], rk[:], ALU.mult).then_inc(br_ready, 1)
                if main:
                    dve.wait_ge(lvl_mm, 6 * p + 4)
                    dve.wait_ge(lvl_act, 3 * p + 1)
                    for m in (1, 0):
                        s = slice(64 * m, 64 * m + 32)
                        last = v.tensor_scalar(TT[s, :, 64 * m + 32:64 * m + 64],
                                               ps[s, WB, 0:256].rearrange("p (u c) -> p u c", u=U), -1.0, None, ALU.mult)
                    link(last)
                    for u in range(U):
                        last = v.transpose(x64[32:64, u, 0:32], TT[0:32, u, 32:64])
                    last.then_inc(lvl_dve, 1)
                if s1:
                    lower(q, npar, 1)
                if outq:
                    dve.wait_ge(out_mm, 5 * (p - 1) + 2)
                    dve.wait_ge(xk_ld[npar], 8 * (p - 1) + 16 - 8 * npar)
                    v.tensor_tensor(r1[:], ps[:, MB, 0:256].rearrange("p (j d) -> p j d", j=2), xk[:, npar],
                                    ALU.add).then_inc(r1_ready, 1)
                    dve.wait_ge(r1_ready, p)
                    moments(r1).then_inc(ve_ready, 1)
                    dve.wait_ge(rstd_ready, p)
                    wait(dve, x1_st[npar], 8 * (p - 1) - 8 * npar)
                    wait(dve, scat[npar], 4 * (8 * (p - 1) - 8 * npar))
                    for j in range(2):
                        last = v.tensor_scalar(x1[:, npar, j, :], r1[:, j, :], mv[:, j, 0:1], rstd[:, j:j + 1],
                                               ALU.subtract, ALU.mult)
                    last.then_inc(x1_ready, 1)
                if s1:
                    dve.wait_ge(freed_act, 8 * q + 6)
                    link(v.tensor_scalar(gden[:], eg[:], 1.0, None, ALU.add))
                    wait(dve, gate_ready, 2 * q)
                    v.reciprocal(sig[:], gden[:]).then_inc(sig_ready, 1)
                if main:
                    chain_r(p, par, 0)
                    chain_s(p, 0)
                if outq:
                    route(p - 1)
                if s1:
                    masked_q(q, npar, 0)
                if main:
                    chain_r(p, par, 1)
                if outq:
                    place(p - 1, p, npar)
                if main:
                    chain_s(p, 1)
                if s1:
                    masked_q(q, npar, 1)
                if main:
                    dve.wait_ge(osq_ready, p + 1)
                    link(v.tensor_reduce(oss[:], osq[:].rearrange("p j (h d) -> p (j h) d", h=H), AX.X, ALU.add))
                    v.tensor_scalar(oms[:], oss[:], 1.0 / DV, EPS, ALU.mult, ALU.add).then_inc(oms_ready, 1)

            def moments(src):
                for j in range(2):
                    last = v.bn_stats(bst[:, j, :], src[:, j, :])
                link(last)
                apart(dve)
                for j in range(2):
                    last = v.bn_aggr(mv[:, j, :], bst[:, j, :])
                link(last)
                return v.tensor_scalar(ve[:], mv[:, :, 1], EPS, None, ALU.add)

            def lower(q, par, j):
                dve.wait_ge(filled, 12 * q + 6 + j)
                if j == 0:
                    wait(dve, a_st, 64 * q)
                for h in range(H):
                    last = v.scalar_tensor_tensor(out=A[:, par, H * j + h, :], in0=ps[:, fill_bank[5 + j], P * h:P * h + P],
                                                  scalar=c2[:, par, H * j + h:H * j + h + 1], in1=strict[:],
                                                  op0=ALU.mult, op1=ALU.mult)
                last.then_inc(freed_dve, 1)

            def masked_q(q, par, j):
                dve.wait_ge(filled, 12 * q + 11 + j)
                v.tensor_tensor(PT[:, par, H * j:H * j + H, :],
                                ps[:, fill_bank[10 + j], :].rearrange("p (h t) -> p h t", h=H),
                                bc(upper[:], 1, H), ALU.mult).then_inc(freed_dve, 1)

            def chain_r(p, par, j):
                dve.wait_ge(chain_mm, 6 * p + 3 * j + 1)
                if j == 0:
                    dve.wait_ge(gate_ready, 2 * p + 2)
                link(v.tensor_tensor(tmp[:].rearrange("p (h d) -> p h d", h=H),
                                     ps[:, CB, 0:128].rearrange("p (h d) -> p h d", h=H),
                                     bc(c2[:, par, H * j:H * j + H], 2, DV), ALU.mult))
                v.tensor_tensor(R[:], Vp[:, par, j, :], tmp[:], ALU.subtract).then_inc(r_ready, 1)

            def chain_s(p, j):
                dve.wait_ge(chain_mm, 6 * p + 3 * j + 3)
                if j == 0:
                    v.tensor_tensor(St[:], St[:], ps[:, CB, 256:384], ALU.add).then_inc(s_ready, 1)
                else:
                    link(v.tensor_tensor(St[:], St[:], ps[:, CB, 256:384], ALU.add))
                    v.tensor_scalar(St[:], St[:], keep_s[:, bass.ds(p, 1)], None, ALU.mult).then_inc(s_ready, 1)

            def route(q):
                dve.wait_ge(out_mm, 5 * q + 4)
                link(v.tensor_copy(lg[:], ps[:, MB, 0:2 * E].rearrange("p (j e) -> p j e", j=2)))
                apart(dve)
                for j in range(2):
                    last = v.max(v8[:, j, :], lg[:, j, :])
                link(last)
                apart(dve)
                for j in range(2):
                    last = v.max_index(i8[:, j, :], v8[:, j, :], lg[:, j, :])
                v.tensor_scalar(nm[:], v8[:, :, 0], -1.0, None, ALU.mult).then_inc(nm_ready, 1)
                dve.wait_ge(nm_ready, q + 1)
                link(v.tensor_copy(idxf[:], i8[:, :, 0:TOPK]))
                link(v.tensor_tensor(oh[:].rearrange("p j k e -> p (j k) e"), bc(iota8[:], 1, 4),
                                     bc(idxf[:].rearrange("p j k -> p (j k)"), 2, E), ALU.is_equal))
                v.tensor_tensor(M[:], oh[:, :, 0, :], oh[:, :, 1, :], ALU.add).then_inc(M_ready, 1)

            def place(q, p, par):
                dve.wait_ge(out_mm, 5 * q + 5)
                v.tensor_tensor(cc[:], ps[:, MB, 0:2 * E].rearrange("p (j e) -> p j e", j=2), bc(carry[:], 1, 2), ALU.add)
                link(v.tensor_tensor(carry0[:], ps[:, MB, 2 * E:3 * E], carry[:], ALU.add))
                v.tensor_scalar(carry[:], carry0[:], keep_c[:, bass.ds(p, 1)], None, ALU.mult)
                for j in range(2):
                    last = v.tensor_tensor(pr[:, j], oh[:, j], bc(cc[:, j, :], 1, TOPK), ALU.mult)
                link(last)
                link(v.tensor_reduce(cnt[:], pr[:].rearrange("p j k e -> p (j k) e"), AX.X, ALU.add))
                v.tensor_scalar(valid[:], cnt[:], float(CAP), None, ALU.is_le)
                link(v.scalar_tensor_tensor(out=sl[:], in0=idxf[:].rearrange("p j k -> p (j k)"), scalar=float(CAP),
                                            in1=cnt[:], op0=ALU.mult, op1=ALU.add))
                link(v.scalar_tensor_tensor(out=sd[:], in0=sl[:], scalar=base[:, bass.ds(p, 1)], in1=spare[:],
                                            op0=ALU.add, op1=ALU.subtract))
                link(v.tensor_tensor(sv[:], sd[:], valid[:], ALU.mult))
                link(v.tensor_tensor(slf[:], sv[:], spare[:], ALU.add))
                v.tensor_copy(slots[:, bass.ds(4 * q, 4)], slf[:])
                wait(dve, scat[par], 4 * (8 * q - 8 * par))
                v.tensor_copy(slot[:, par, :], slf[:])
                dve.wait_ge(e8_ready, q + 1)
                link(v.reciprocal(rs[:], es[:]))
                link(v.tensor_tensor(wv[:], e8[:, :, 0:TOPK], bc(rs[:], 2, TOPK), ALU.mult))
                v.tensor_tensor(gates[:, bass.ds(4 * q, 4)], wv[:].rearrange("p j k -> p (j k)"), valid[:],
                                ALU.mult).then_inc(slot_ready, 1)

            phase_a(dve, step, link, DVE_LINKS)

            def gated(n, par, s):
                dve.wait_ge(hs_ready, 8 * n + s + 1)
                if s == 0:
                    wait(dve, y_mm, n - 1)
                c, g = s // 2, s % 2
                v.tensor_tensor(hb[:, par, c, HALF * g:HALF * g + HALF], ps[0:FW, 4 + g, 0:HALF], hs[:, g, :],
                                ALU.mult).then_inc(h_ready, 1)

            for n in range(2):
                for s in range(8):
                    gated(n, n, s)
            with dve.Fori(1, B * E // 2) as i:
                for par in range(2):
                    for s in range(8):
                        gated(2 * i + par, par, s)

            def indices(p, par):
                wait(dve, gb_ld[par], 4 * (8 * p - 8 * par))
                v.tensor_copy(gi[:, par, :], slots[:, bass.ds(4 * p, 4)]).then_inc(gi_ready, 1)

            def combine(p, par):
                dve.wait_ge(gb_ld[par], 4 * (8 * p + 16 - 8 * par))
                dve.wait_ge(x1c_ld[par], 8 * p + 16 - 8 * par)
                for j in range(2):
                    last = v.scalar_tensor_tensor(out=ya[:, j, :], in0=gb[:, par, 2 * j, :],
                                                  scalar=gates[:, bass.ds(4 * p + 2 * j, 1)],
                                                  in1=x1c[:, par, j, :], op0=ALU.mult, op1=ALU.add)
                link(last)
                for j in range(2):
                    last = v.scalar_tensor_tensor(out=yb[:, j, :], in0=gb[:, par, 2 * j + 1, :],
                                                  scalar=gates[:, bass.ds(4 * p + 2 * j + 1, 1)],
                                                  in1=ya[:, j, :], op0=ALU.mult, op1=ALU.add)
                link(last)
                moments(yb).then_inc(cve_ready, 1)
                dve.wait_ge(crstd_ready, p + 1)
                wait(dve, out_st[par], 8 * p - 8 * par)
                for j in range(2):
                    last = v.tensor_scalar(yo[:, par, j, :], yb[:, j, :], mv[:, j, 0:1], rstd[:, j:j + 1],
                                           ALU.subtract, ALU.mult)
                last.then_inc(yo_ready, 1)

            indices(0, 0)
            indices(1, 1)
            combine(0, 0)
            indices(2, 0)
            combine(1, 1)
            indices(3, 1)
            with dve.Fori(1, NP // 2 - 1) as i:
                link.enter(i - 1, 8)
                for par in range(2):
                    combine(2 * i + par, par)
                    indices(2 * i + par + 2, par)
            link.leave(NP // 2 - 2)
            combine(NP - 2, 0)
            combine(NP - 1, 1)

        @block.gpsimd
        def _(pool):
            link = Link(pool, link_pool)
            g = nc.gpsimd
            g.memset(zeros[:], 0.0).then_inc(consts_pool, 1)
            for t, fill in ((ident, 0.0), (strict, 1.0), (upper, 1.0), (id16, 0.0)):
                last = g.memset(t[:], fill)
            link(last)
            g.affine_select(out=ident[:], in_=ident[:], compare_op=ALU.not_equal, fill=1.0, base=0,
                            pattern=[[-1, P]], channel_multiplier=1).then_inc(consts_pool, 1)
            g.affine_select(out=strict[:], in_=strict[:], compare_op=ALU.is_ge, fill=0.0, base=-1,
                            pattern=[[-1, P]], channel_multiplier=1).then_inc(consts_pool, 1)
            g.affine_select(out=upper[:], in_=upper[:], compare_op=ALU.is_ge, fill=0.0, base=0,
                            pattern=[[1, P]], channel_multiplier=-1).then_inc(consts_pool, 1)
            g.iota(pidx[:], pattern=[[0, 1]], base=0, channel_multiplier=1).then_inc(consts_pool, 1)
            g.iota(iota8[:], pattern=[[1, E]], base=0, channel_multiplier=0,
                   allow_small_or_imprecise_dtypes=True).then_inc(consts_pool, 1)
            link(g.affine_select(out=id16[:], in_=id16[:], compare_op=ALU.not_equal, fill=1.0, base=0,
                                 pattern=[[-1, 16], [1, 16]], channel_multiplier=0))

            def solve(q):
                wait(pool, xi_st, 64 * q)
                apart(pool)
                link(g.tensor_copy(xs[:], id16[:]))
                pool.wait_ge(ab_ld, 32 * q + 32)
                for j in range(15):
                    n = 15 - j
                    pr_ = prod[:, 0:n * (j + 1)].rearrange("p (i c) -> p i c", c=j + 1)
                    link(g.tensor_tensor(pr_, bc(ab[:, j + 1:, j], 2, j + 1), bc(xs[:, j, 0:j + 1], 1, n), ALU.mult))
                    link(g.tensor_tensor(xs[:, j + 1:, 0:j + 1], xs[:, j + 1:, 0:j + 1], pr_, ALU.subtract))
                apart(pool)
                g.tensor_copy(xsT[:], xs[:].rearrange("p r c -> p c r")).then_inc(solved, 1)

            def step(p, par, s1, main, outq):
                q, npar = p + 1, 1 - par
                if s1:
                    pool.wait_ge(sig_ready, q + 1)
                    wait(pool, og_ready, q - 1)
                    g.tensor_tensor(silu[:, npar], VG[:, :, H * DV:], sig[:], ALU.mult).then_inc(gate_ready, 1)
                    pool.wait_ge(br_ready, q + 1)
                    wait(pool, r_ready, 2 * (q - 1))
                    for j in range(2):
                        last = g.tensor_tensor(Vp[:, npar, j, :].rearrange("p (h d) -> p h d", h=H),
                                               VG[:, j, 0:H * DV].rearrange("p (h d) -> p h d", h=H),
                                               bc(br[:, H * j:H * j + H], 2, DV), ALU.mult)
                    last.then_inc(gate_ready, 1)
                if s1:
                    solve(q)
                if outq:
                    pool.wait_ge(slot_ready, p)
                    if isinstance(p, int) and p == 1:
                        pool.wait_ge(zero_st, 16 * (ROWS // P // 8 + 1))
                    apart(pool)
                    for j in range(2):
                        for k in range(TOPK):
                            g.indirect_dma_start(
                                out=xs_d[:, :], out_offset=bass.IndirectOffsetOnAxis(ap=slot[:, npar, 2 * j + k:2 * j + k + 1], axis=0),
                                in_=x1[:, npar, j, :], in_offset=None).then_inc(scat[npar], 16)
                if main:
                    pool.wait_ge(o_ready, 2 * p + 2)
                    g.tensor_tensor(osq[:], o[:], o[:], ALU.mult).then_inc(osq_ready, 1)
                    pool.wait_ge(orms_ready, p + 1)
                    for j in range(2):
                        last = g.tensor_tensor(on[:, j, :].rearrange("p (h d) -> p h d", h=H),
                                               o[:, j, :].rearrange("p (h d) -> p h d", h=H),
                                               bc(orms[:, H * j:H * j + H], 2, DV), ALU.mult)
                    link(last)
                    wait(pool, out_mm, 5 * (p - 1) + 1)
                    g.tensor_tensor(og[:], on[:], silu[:, par], ALU.mult).then_inc(og_ready, 1)

            phase_a(pool, step, link, POOL_LINKS)

            def gather(p, par):
                pool.wait_ge(gi_ready, p + 1)
                wait(pool, yo_ready, p - 1)
                apart(pool)
                for k in range(4):
                    g.indirect_dma_start(
                        out=gb[:, par, k, :], out_offset=None, in_=ys_d[:, :],
                        in_offset=bass.IndirectOffsetOnAxis(ap=gi[:, par, k:k + 1], axis=0)).then_inc(gb_ld[par], 16)

            pool.wait_ge(ye_st[0], 16 * B * E // 2)
            pool.wait_ge(ye_st[1], 16 * B * E // 2)
            gather(0, 0)
            gather(1, 1)
            with pool.Fori(1, NP // 2) as i:
                for par in range(2):
                    gather(2 * i + par, par)


ACT_LINKS = 6
DVE_LINKS = 52
POOL_LINKS = 64


def kernel(L0_attn_x, L0_attn_Wq, L0_attn_Wk, L0_attn_Wv, L0_attn_Wb, L0_attn_Wg, L0_attn_Wo, L0_attn_norm_w,
           L0_ffn_gate_w, L0_ffn_w1, L0_ffn_w2, L0_ffn_w3):
    import concourse.bacc as bacc
    from concourse.bass_utils import run_bass_kernel_spmd

    x = np.ascontiguousarray(L0_attn_x).reshape(B * S, D)
    arrays = {
        "x": x, "xT": np.ascontiguousarray(x.T),
        "Wq": np.ascontiguousarray(L0_attn_Wq), "Wk": np.ascontiguousarray(L0_attn_Wk),
        "Wvg": np.ascontiguousarray(np.concatenate([np.asarray(L0_attn_Wv), np.asarray(L0_attn_Wg)], axis=1)),
        "Wb": np.ascontiguousarray(L0_attn_Wb), "Wo": np.ascontiguousarray(L0_attn_Wo),
        "norm_w": np.ascontiguousarray(L0_attn_norm_w),
        "gateT": np.ascontiguousarray(np.asarray(L0_ffn_gate_w).T),
        "w1": np.ascontiguousarray(L0_ffn_w1), "w2": np.ascontiguousarray(L0_ffn_w2),
        "w3": np.ascontiguousarray(L0_ffn_w3),
    }
    nc = bacc.Bacc("TRN2", target_bir_lowering=False, num_devices=1)
    args = [nc.dram_tensor(n, a.shape, F32, kind="ExternalInput").ap() for n, a in arrays.items()]
    out = nc.dram_tensor("result", (B * S, D), F32, kind="ExternalOutput").ap()
    build(nc, *args, out)
    r = run_bass_kernel_spmd(nc, [arrays], core_ids=[0])
    return r.results[0]["result"].reshape(B, S, D)
```

```python
from contextlib import ExitStack

import numpy as np

import concourse.bass as bass
from concourse import mybir

F32 = mybir.dt.float32
BF16 = mybir.dt.bfloat16
I32 = mybir.dt.int32
U32 = mybir.dt.uint32
ALU = mybir.AluOpType
ACT = mybir.ActivationFunctionType
AX = mybir.AxisListType

P = 128
B, S, D = 2, 2048, 128
H, DK, DV = 4, 128, 32
E, F, TOPK = 8, 448, 2
CAP = int(S * TOPK / E * 1.25)
FC, FW = 4, F // 4
NT = B * S // P
NP = NT // 2
PB = NP // B
U = 2 * H
ROWS = B * E * CAP
SPARE = 4 * P
CT = CAP // P
HALF = CAP // 2
EPS = 1e-5
SCALE = DK ** -0.5
BLK = 16 * 32 + 16
VW = H * DV + H
W_LOADS = 16 * (6 + H)
LOOP0, LOOP1 = 2, NP - 2


def wait(eng, sem, value):
    if isinstance(value, int) and value <= 0:
        return
    eng.wait_ge(sem, value)


def apart(eng):
    eng.nop(nofuse=True)


class Link:

    def __init__(self, eng, sem):
        self.eng, self.sem, self.n, self.off = eng, sem, 0, 0

    def __call__(self, ins):
        ins.then_inc(self.sem, 1)
        self.n += 1
        self.eng.wait_ge(self.sem, self.n + self.off)

    def enter(self, step, per_step):
        self.start, self.per, self.off = self.n, per_step, step * per_step

    def leave(self, steps):
        assert self.n - self.start == self.per, (self.n - self.start, self.per)
        self.n, self.off = self.start + self.per * steps, 0


def bc(ap, axis, n):
    shape = list(ap.shape)
    shape.insert(axis, n)
    return ap.unsqueeze(axis).to_broadcast(shape)


def build(nc, x, xT, Wq, Wk, Wvb, Wg, Wo, norm_w, gateT, w1, w2, w3, out):
    xs_d = nc.dram_tensor("slots_in", (ROWS + SPARE, D), F32, kind="Internal").ap()
    ys_d = nc.dram_tensor("slots_out", (ROWS + SPARE, D), F32, kind="Internal").ap()
    x1_d = nc.dram_tensor("x1_store", (NT * P, D), F32, kind="Internal").ap()
    ad_d = nc.dram_tensor("a_diag", (U * 4, 2 * BLK), F32, kind="Internal").ap()
    xi_d = nc.dram_tensor("inv16", (2, U * P, 16), F32, kind="Internal").ap()
    x_v = x.rearrange("(t p) d -> p t d", p=P)
    x1_v = x1_d.rearrange("(t p) d -> p t d", p=P)
    out_v = out.rearrange("(t p) d -> p t d", p=P)

    ctx = ExitStack()
    with ctx:
        def sb(name, shape, dt=F32):
            return ctx.enter_context(nc.sbuf_tensor(name, shape, dt))

        def sem(name):
            return ctx.enter_context(nc.semaphore(name))

        ps = ctx.enter_context(nc.psum_tensor("ps", [P, 8, 512], F32))

        ident = sb("ident", [P, P])
        strict = sb("strict", [P, P])
        upper = sb("upper", [P, P])
        tri = sb("tri", [P, P], BF16)
        ones = sb("ones", [P, P], BF16)
        iota8 = sb("iota8", [P, E])
        pidx = sb("pidx", [P, 1], I32)
        pbit = sb("pbit", [P, 1], I32)
        pcol = sb("pcol", [P, 1])
        low = sb("low", [P, 1])
        high = sb("high", [P, 1])
        spare = sb("spare", [P, 4])
        keep_s = sb("keep_s", [P, NP + 1])
        keep_c = sb("keep_c", [P, NP + 1])
        base = sb("base", [P, NP + 1])
        id16 = sb("id16", [64, 16, 16])
        heads = sb("heads", [P, P])
        eps = sb("eps", [P, 1])
        one = sb("one", [P, 1])
        zeros = sb("zeros", [P, 8 * P])
        mask16 = sb("mask16", [P, P])
        mask32 = sb("mask32", [P, P])
        wq = sb("wq", [P, H * DK])
        wk = sb("wk", [P, H * DK])
        wvb = sb("wvb", [P, VW])
        wg = sb("wg", [P, H * DV])
        wo0 = sb("wo0", [P, D])
        wo = sb("wo", [P, D])
        nw = sb("nw", [P, 1])
        gt = sb("gt", [P, E])

        xTs = sb("xTs", [P, 2, 2 * P])
        xk = sb("xk", [P, 2, 2, D])
        KT = sb("KT", [P, 2, H, 2 * P])
        QT = sb("QT", [P, 2, H, 2 * P])
        K = sb("K", [P, 2, 2, H * DK])
        A = sb("A", [P, 2, U, P])
        PT = sb("PT", [P, 2, U, P])
        V = sb("V", [P, 2, H * DV])
        G = sb("G", [P, 2 * P])
        Vp = sb("Vp", [P, 2, 2, H * DV])
        silu = sb("silu", [P, 2, 2 * P])
        c2 = sb("c2", [P, 2, U])
        ss = sb("ss", [P, U])
        ssp = sb("ssp", [P, U])
        rr = sb("rr", [P, U])
        lnk = sb("lnk", [P, U])
        rk = sb("rk", [P, U])
        br = sb("br", [P, U])
        eb = sb("eb", [P, 2, H])
        bden = sb("bden", [P, U])
        beta = sb("beta", [P, U])
        eg = sb("eg", [P, 2 * P])
        lsg = sb("lsg", [P, 2 * P])
        sg = sb("sg", [P, 2 * P])
        junk = sb("junk", [P, U, P])
        ab = sb("ab", [64, 16, 16])
        xs = sb("xs", [64, 2, 16, 16])
        prod = sb("prod", [64, 240])
        xi = sb("xi", [P, 2, U, 16])
        m32 = sb("m32", [P, U, P])
        x16d = sb("x16d", [P, U, P])
        z32 = sb("z32", [P, U, 16])
        x32T = sb("x32T", [P, U, 32])
        x32 = sb("x32", [P, U, 32])
        z64 = sb("z64", [P, U, 32])
        x64 = sb("x64", [64, U, 64])
        z128 = sb("z128", [64, U, 64])
        TT = sb("TT", [P, U, P])
        St = sb("St", [P, H * DV])
        tmp = sb("tmp", [P, H * DV])
        R = sb("R", [P, H * DV])
        dl = sb("dl", [P, H * DV])
        o = sb("o", [P, 2 * P])
        osq = sb("osq", [P, 2 * P])
        oln = sb("oln", [P, 2 * P])
        orms = sb("orms", [P, 2 * P])
        on = sb("on", [P, 2 * P])
        og = sb("og", [P, 2 * P])
        r1 = sb("r1", [P, 2, D])
        bst = sb("bst", [P, 2, 6])
        mv = sb("mv", [P, 2, 2])
        ve = sb("ve", [P, 2])
        vl = sb("vl", [P, 2])
        rstd = sb("rstd", [P, 2])
        x1 = sb("x1", [P, 2, 2, D])
        x1T = sb("x1T", [P, 2 * P])
        lg = sb("lg", [P, 2, E])
        v8 = sb("v8", [P, 2, 8])
        i8 = sb("i8", [P, 2, 8], U32)
        nm = sb("nm", [P, 2])
        e8 = sb("e8", [P, 2, 8])
        es = sb("es", [P, 2])
        idxf = sb("idxf", [P, 2, TOPK])
        oh = sb("oh", [P, 2, TOPK, E])
        M = sb("M", [P, 2, E], BF16)
        cc = sb("cc", [P, 2, E])
        carry0 = sb("carry0", [P, E])
        carry = sb("carry", [P, E])
        pr = sb("pr", [P, 2, TOPK, E])
        cnt = sb("cnt", [P, 4])
        valid = sb("valid", [P, 4])
        sl = sb("sl", [P, 4])
        sd = sb("sd", [P, 4])
        sv = sb("sv", [P, 4])
        slf = sb("slf", [P, 4])
        rs = sb("rs", [P, 2])
        wv = sb("wv", [P, 2, TOPK])
        slot = sb("slot", [P, 2, 4], U32)
        gates = sb("gates", [P, 4 * NP])
        slots = sb("slots", [P, 4 * NP], U32)

        w1s = sb("w1s", [P, 2, F])
        w3s = sb("w3s", [P, 2, F])
        w2s = sb("w2s", [FW, 2, FC, D])
        xe = sb("xe", [P, 2, CT, D])
        xeT = sb("xeT", [P, 2, CAP])
        hs = sb("hs", [FW, 2, HALF])
        hb = sb("hb", [FW, 2, FC, CAP])
        ye = sb("ye", [P, 2, CT, D])
        gi = sb("gi", [P, 2, 4], U32)
        gb = sb("gb", [P, 2, 4, D])
        x1c = sb("x1c", [P, 2, 2, D])
        ya = sb("ya", [P, 2, D])
        yb = sb("yb", [P, 2, D])
        yo = sb("yo", [P, 2, 2, D])

        w_ld = sem("w_ld")
        zero_st = sem("zero_st")
        consts_pool = sem("consts_pool")
        consts_dve = sem("consts_dve")
        wo_ready = sem("wo_ready")
        xT_ld = [sem("xT_ld0"), sem("xT_ld1")]
        xk_ld = [sem("xk_ld0"), sem("xk_ld1")]
        filled = sem("filled")
        freed_act = sem("freed_act")
        freed_dve = sem("freed_dve")
        ssp_ready = sem("ssp_ready")
        rk_ready = sem("rk_ready")
        br_ready = sem("br_ready")
        sg_ready = sem("sg_ready")
        gate_ready = sem("gate_ready")
        a_st = sem("a_st")
        ab_ld = sem("ab_ld")
        m32_ready = sem("m32_ready")
        solved = sem("solved")
        xi_st = sem("xi_st")
        xi_ld = sem("xi_ld")
        prep = sem("prep")
        lvl_mm = sem("lvl_mm")
        lvl_dve = sem("lvl_dve")
        lvl_act = sem("lvl_act")
        x64_diag = sem("x64_diag")
        chain_mm = sem("chain_mm")
        r_ready = sem("r_ready")
        s_ready = sem("s_ready")
        d_ready = sem("d_ready")
        o_ready = sem("o_ready")
        osq_ready = sem("osq_ready")
        orms_ready = sem("orms_ready")
        og_ready = sem("og_ready")
        out_mm = sem("out_mm")
        r1_ready = sem("r1_ready")
        ve_ready = sem("ve_ready")
        rstd_ready = sem("rstd_ready")
        x1_ready = sem("x1_ready")
        x1_st = [sem("x1_st0"), sem("x1_st1")]
        x1T_ready = sem("x1T_ready")
        nm_ready = sem("nm_ready")
        e8_ready = sem("e8_ready")
        M_ready = sem("M_ready")
        slot_ready = sem("slot_ready")
        scat = [sem("scat0"), sem("scat1")]
        link_dve = sem("link_dve")
        link_act = sem("link_act")
        link_pool = sem("link_pool")
        ew_ld = [sem("ew_ld0"), sem("ew_ld1")]
        xe_ld = [sem("xe_ld0"), sem("xe_ld1")]
        xeT_mm = sem("xeT_mm")
        xeT_ready = sem("xeT_ready")
        h_mm = sem("h_mm")
        hs_ready = sem("hs_ready")
        h_ready = sem("h_ready")
        y_mm = sem("y_mm")
        ye_ready = sem("ye_ready")
        ye_st = [sem("ye_st0"), sem("ye_st1")]
        gi_ready = sem("gi_ready")
        gb_ld = [sem("gb_ld0"), sem("gb_ld1")]
        x1c_ld = [sem("x1c_ld0"), sem("x1c_ld1")]
        cve_ready = sem("cve_ready")
        crstd_ready = sem("crstd_ready")
        yo_ready = sem("yo_ready")
        out_st = [sem("out_st0"), sem("out_st1")]

        block = ctx.enter_context(nc.Block())

        def phase_a(eng, step, link=None, per_body=0):
            step(-1, 1, True, False, False)
            step(0, 0, True, True, False)
            step(1, 1, True, True, True)
            with eng.Fori(0, (LOOP1 - LOOP0) // 2) as i:
                if link:
                    link.enter(i, per_body)
                step(LOOP0 + 2 * i, 0, True, True, True)
                step(LOOP0 + 2 * i + 1, 1, True, True, True)
            if link:
                link.leave((LOOP1 - LOOP0) // 2)
            step(NP - 2, 0, True, True, True)
            step(NP - 1, 1, False, True, True)
            step(NP, 0, False, False, True)

        @block.sync
        def _(sp):
            for dst, src in ((wk, Wk), (wvb, Wvb), (wg, Wg), (wq, Wq), (wo0, Wo), (gt, gateT)):
                sp.dma_start(dst[:], src[:, :]).then_inc(w_ld, 16)
            for h in range(H):
                sp.dma_start(nw[h * DV:(h + 1) * DV, :], norm_w.rearrange("(d o) -> d o", o=1)).then_inc(w_ld, 16)

            def load_xT(r, par):
                wait(sp, filled, 12 * (r - 2) + 10)
                sp.dma_start(xTs[:, par, :], xT[:, bass.ds(r * 2 * P, 2 * P)]).then_inc(xT_ld[par], 16)

            blocks = ad_d.rearrange("b (k x) -> (b k) x", x=BLK)[:, 0:512].rearrange("b (r c) -> b r c", c=32)[:, :, 0:16]

            def step(p, par, s1, main, outq):
                q = p + 1
                if isinstance(p, int) and p == -1:
                    load_xT(0, 0)
                    sp.wait_ge(consts_pool, 1)
                    for k in range(ROWS // P // 8):
                        sp.dma_start(xs_d[k * 8 * P:(k + 1) * 8 * P, :].rearrange("(p r) d -> p (r d)", p=P),
                                     zeros[:]).then_inc(zero_st, 16)
                    sp.dma_start(ys_d[ROWS:ROWS + SPARE, :].rearrange("(p r) d -> p (r d)", p=P),
                                 zeros[:, 0:SPARE]).then_inc(zero_st, 16)
                if not (isinstance(p, int) and p + 2 > NP - 1):
                    load_xT(p + 2, par)
                if main:
                    wait(sp, r1_ready, p - 1)
                    sp.dma_start(xk[:, par], x_v[:, bass.ds(p * 2, 2), :]).then_inc(xk_ld[par], 16)
                if s1:
                    sp.wait_ge(freed_dve, 4 * q + 2)
                    apart(sp)
                    for k in range(4):
                        sp.dma_start(ad_d[k::4, 0:1024].rearrange("u (r c) -> r u c", c=32),
                                     A[32 * k:32 * k + 32, 1 - par, :, 32 * k:32 * k + 32]).then_inc(a_st, 16)
                    sp.wait_ge(a_st, 64 * q + 64)
                    wait(sp, solved, q)
                    sp.dma_start(ab[:], blocks).then_inc(ab_ld, 16)
                if outq:
                    wait(sp, x1_ready, p)
                    sp.dma_start(x1_v[:, bass.ds(2 * p - 2, 2), :], x1[:, 1 - par]).then_inc(x1_st[1 - par], 16)
                if s1:
                    sp.wait_ge(solved, q + 1)
                    sp.dma_start(xi_d.rearrange("t (b r) c -> b t (r c)", r=16),
                                 xs[:].rearrange("p t r c -> p t (r c)")).then_inc(xi_st, 16)
                    sp.wait_ge(xi_st, 16 * q + 16)
                    wait(sp, lvl_dve, 4 * (q - 1) + 2)
                    sp.dma_start(xi[:], xi_d.rearrange("t (u r) c -> r t u c", r=P)).then_inc(xi_ld, 16)

            phase_a(sp, step)

            sp.wait_ge(x1_st[0], 16 * (NP // 2))
            sp.wait_ge(x1_st[1], 16 * (NP // 2))
            sp.wait_ge(scat[0], 64 * (NP // 2))
            sp.wait_ge(scat[1], 64 * (NP // 2))
            sp.wait_ge(zero_st, 16 * (ROWS // P // 8 + 1))

            xs_n = xs_d[0:ROWS, :].rearrange("(n p i) d -> n p i d", p=P, i=CT)
            ys_n = ys_d[0:ROWS, :].rearrange("(n p i) d -> n p i d", p=P, i=CT)

            def load_unit(n, e, par):
                wait(sp, h_mm, 8 * (n - 1))
                sp.dma_start(w1s[:, par, :], w1[bass.ds(e, 1)].rearrange("o p f -> p (o f)")).then_inc(ew_ld[par], 16)
                sp.dma_start(w3s[:, par, :], w3[bass.ds(e, 1)].rearrange("o p f -> p (o f)")).then_inc(ew_ld[par], 16)
                wait(sp, y_mm, n - 1)
                sp.dma_start(w2s[:, par], w2[bass.ds(e, 1)].rearrange("o (c p) d -> p (o c) d", p=FW)).then_inc(ew_ld[par], 16)
                wait(sp, xeT_mm, n - 1)
                sp.dma_start(xe[:, par], xs_n[bass.ds(n, 1)].rearrange("o p i d -> p (o i) d")).then_inc(xe_ld[par], 16)

            def store_unit(n, par):
                sp.wait_ge(ye_ready, n + 1)
                sp.dma_start(ys_n[bass.ds(n, 1)].rearrange("o p i d -> p (o i) d"), ye[:, par]).then_inc(ye_st[par], 16)

            load_unit(0, 0, 0)
            load_unit(1, 1, 1)
            for b in range(B):
                with sp.Fori(0, E // 2 - 1) as i:
                    for par in range(2):
                        load_unit(b * E + 2 * i + par + 2, 2 * i + par + 2, par)
                        store_unit(b * E + 2 * i + par, par)
                for par in range(2):
                    if b + 1 < B:
                        load_unit((b + 1) * E + par, par, par)
                    store_unit(b * E + E - 2 + par, par)

            sp.wait_ge(ye_st[0], 16 * B * E // 2)
            sp.wait_ge(ye_st[1], 16 * B * E // 2)

            def load_x1(p, par):
                wait(sp, yo_ready, p - 1)
                sp.dma_start(x1c[:, par], x1_v[:, bass.ds(2 * p, 2), :]).then_inc(x1c_ld[par], 16)

            def store(p, par):
                sp.wait_ge(yo_ready, p + 1)
                sp.dma_start(out_v[:, bass.ds(2 * p, 2), :], yo[:, par]).then_inc(out_st[par], 16)

            load_x1(0, 0)
            load_x1(1, 1)
            with sp.Fori(0, NP // 2 - 1) as i:
                for par in range(2):
                    load_x1(2 * i + par + 2, par)
                    store(2 * i + par, par)
            for par in range(2):
                store(NP - 2 + par, par)
            for par in range(2):
                sp.wait_ge(out_st[par], 16 * NP // 2)

        @block.tensor
        def _(pe):
            mm = nc.tensor.matmul
            fill_bank = [g % 3 for g in range(12)]
            ZB, WB, CB, OB, MB = 3, 4, 5, 6, 7

            pe.wait_ge(w_ld, W_LOADS)
            pe.wait_ge(consts_pool, 5)

            def act_free(q, n):
                wait(pe, freed_act, 8 * q + n)

            def dve_free(q, n):
                wait(pe, freed_dve, 4 * q + n)

            def kt(q, par, g):
                if g == 0:
                    pe.wait_ge(xT_ld[par], 8 * q + 16 - 8 * par)
                    act_free(q - 1, 8)
                else:
                    dve_free(q - 1, 3)
                for k in range(2):
                    h = 2 * g + k
                    last = mm(ps[:, fill_bank[g], 256 * k:256 * k + 256], wk[:, DK * h:DK * h + DK], xTs[:, par, :],
                              start=True, stop=True)
                last.then_inc(filled, 1)

            def k_tok(q, par, j):
                if j == 0:
                    dve_free(q - 1, 4)
                else:
                    act_free(q, 1)
                mm(ps[:, fill_bank[2 + j], :], xTs[:, par, P * j:P * j + P], wk[:, :],
                   start=True, stop=True).then_inc(filled, 1)

            def vb(q, par):
                act_free(q, 2)
                for j in range(2):
                    last = mm(ps[:, fill_bank[4], VW * j:VW * j + VW], xTs[:, par, P * j:P * j + P], wvb[:],
                              start=True, stop=True)
                last.then_inc(filled, 1)

            def kk(q, par, j):
                act_free(q, 3 + j)
                for h in range(H):
                    kc = KT[:, par, h, P * j:P * j + P]
                    last = mm(ps[:, fill_bank[5 + j], P * h:P * h + P], kc, kc, start=True, stop=True)
                last.then_inc(filled, 1)

            def gate_t(q, par):
                act_free(q, 5)
                mm(ps[:, fill_bank[7], 0:2 * P], wg[:], xTs[:, par, :], start=True, stop=True).then_inc(filled, 1)

            def qt(q, par, g):
                dve_free(q, 1 + g)
                for k in range(2):
                    h = 2 * g + k
                    last = mm(ps[:, fill_bank[8 + g], 256 * k:256 * k + 256], wq[:, DK * h:DK * h + DK], xTs[:, par, :],
                              start=True, stop=True)
                last.then_inc(filled, 1)

            def kq(q, par, j):
                if j == 0:
                    act_free(q, 8)
                for h in range(H):
                    last = mm(ps[:, fill_bank[10 + j], P * h:P * h + P], KT[:, par, h, P * j:P * j + P],
                              QT[:, par, h, P * j:P * j + P], start=True, stop=True)
                last.then_inc(filled, 1)

            def z_32(p):
                pe.wait_ge(m32_ready, p + 1)
                pe.wait_ge(xi_ld, 16 * p + 16)
                wait(pe, lvl_act, 3 * p - 1)
                for u in range(U):
                    last = mm(ps[:, ZB, 16 * u:16 * u + 16], m32[:, u, :], xi[:, 1, u, :], start=True, stop=True)
                last.then_inc(lvl_mm, 1)

            def w_32(p):
                pe.wait_ge(prep, p + 1)
                pe.wait_ge(lvl_dve, 4 * p + 1)
                wait(pe, lvl_act, 3 * p)
                for u in range(U):
                    last = mm(ps[:, WB, 16 * u:16 * u + 16], x16d[:, u, :], z32[:, u, :], start=True, stop=True)
                last.then_inc(lvl_mm, 1)

            def z_64(p, par):
                pe.wait_ge(lvl_dve, 4 * p + 2)
                apart(pe)
                for u in range(U):
                    for m in range(2):
                        s = slice(64 * m + 32, 64 * m + 64)
                        last = mm(ps[64 * m:64 * m + 64, ZB, 32 * u:32 * u + 32], A[s, par, u, 64 * m:64 * m + 64],
                                  x32T[s, u, :], start=True, stop=True)
                last.then_inc(lvl_mm, 1)

            def w_64(p):
                pe.wait_ge(lvl_dve, 4 * p + 3)
                apart(pe)
                for u in range(U):
                    for m in range(2):
                        s = slice(64 * m, 64 * m + 32)
                        last = mm(ps[s, WB, 32 * u:32 * u + 32], x32[s, u, :], z64[s, u, :], start=True, stop=True)
                last.then_inc(lvl_mm, 1)

            def z_128(p, par):
                pe.wait_ge(lvl_dve, 4 * p + 4)
                pe.wait_ge(lvl_act, 3 * p + 1)
                apart(pe)
                for u in range(U):
                    last = mm(ps[0:64, ZB, 64 * u:64 * u + 64], A[64:128, par, u, 0:64], TT[64:128, u, 64:128],
                              start=True, stop=True)
                last.then_inc(lvl_mm, 1)

            def w_128(p):
                pe.wait_ge(lvl_act, 3 * p + 2)
                pe.wait_ge(x64_diag, p + 1)
                apart(pe)
                for u in range(U):
                    last = mm(ps[0:64, WB, 64 * u:64 * u + 64], x64[:, u, :], z128[:, u, :], start=True, stop=True)
                last.then_inc(lvl_mm, 1)

            def ks(p, par, j):
                if isinstance(p, int) and p == 0 and j == 0:
                    pe.wait_ge(consts_dve, 1)
                else:
                    pe.wait_ge(s_ready, 2 * p + j)
                for h in range(H):
                    last = mm(ps[:, CB, 32 * h:32 * h + 32], KT[:, par, h, P * j:P * j + P], St[:, 32 * h:32 * h + 32],
                              start=True, stop=True)
                last.then_inc(chain_mm, 1)

            def qs(p, par, j):
                if j == 0:
                    wait(pe, o_ready, p)
                for h in range(H):
                    mm(ps[32 * h:32 * h + 32, OB, P * j:P * j + P], St[:, 32 * h:32 * h + 32],
                       QT[:, par, h, P * j:P * j + P], start=True, stop=False, skip_group_check=True)

            def t_r(p, j):
                pe.wait_ge(r_ready, 2 * p + j + 1)
                if j == 0:
                    pe.wait_ge(lvl_act, 3 * p + 3)
                for h in range(H):
                    last = mm(ps[:, CB, 128 + 32 * h:160 + 32 * h], TT[:, H * j + h, :], R[:, 32 * h:32 * h + 32],
                              start=True, stop=True)
                last.then_inc(chain_mm, 1)

            def k_d(p, par, j):
                pe.wait_ge(d_ready, 2 * p + j + 1)
                for h in range(H):
                    last = mm(ps[:, CB, 256 + 32 * h:288 + 32 * h], K[:, par, j, DK * h:DK * h + DK],
                              dl[:, 32 * h:32 * h + 32], start=True, stop=True)
                last.then_inc(chain_mm, 1)

            def p_d(p, par, j):
                if j == 0:
                    pe.wait_ge(freed_dve, 4 * p + 4)
                for h in range(H):
                    last = mm(ps[32 * h:32 * h + 32, OB, P * j:P * j + P],
                              dl[:, 32 * h:32 * h + 32], PT[:, par, H * j + h, :],
                              start=False, stop=True, skip_group_check=True)
                last.then_inc(chain_mm, 1)

            def o_sums(q):
                pe.wait_ge(osq_ready, q + 1)
                wait(pe, slot_ready, q)
                mm(ps[:, MB, 0:2 * P], heads[:], osq[:], start=True, stop=True).then_inc(out_mm, 1)

            def o_proj(q):
                pe.wait_ge(og_ready, q + 1)
                pe.wait_ge(wo_ready, 1)
                for j in range(2):
                    last = mm(ps[:, MB, P * j:P * j + P], og[:, P * j:P * j + P], wo[:], start=True, stop=True)
                last.then_inc(out_mm, 1)

            def x1_t(q, par):
                pe.wait_ge(x1_ready, q + 1)
                for j in range(2):
                    last = nc.tensor.transpose(ps[:, MB, P * j:P * j + P], x1[:, par, j, :], ident[:])
                last.then_inc(out_mm, 1)

            def logits(q):
                pe.wait_ge(x1T_ready, q + 1)
                for j in range(2):
                    last = mm(ps[:, MB, E * j:E * j + E], x1T[:, P * j:P * j + P], gt[:], start=True, stop=True)
                last.then_inc(out_mm, 1)

            def cum(q):
                pe.wait_ge(M_ready, q + 1)
                mm(ps[:, MB, 0:E], tri[:], M[:, 0, :], start=True, stop=True)
                mm(ps[:, MB, E:2 * E], tri[:], M[:, 1, :], start=True, stop=False)
                mm(ps[:, MB, E:2 * E], ones[:], M[:, 0, :], start=False, stop=True)
                mm(ps[:, MB, 2 * E:3 * E], ones[:], M[:, 0, :], start=True, stop=False)
                mm(ps[:, MB, 2 * E:3 * E], ones[:], M[:, 1, :], start=False, stop=True).then_inc(out_mm, 1)

            def step(p, par, s1, main, outq):
                q, npar, o_ = p + 1, 1 - par, p - 1
                if outq:
                    ks(o_, npar, 1)
                if s1:
                    kt(q, npar, 0)
                if outq:
                    qs(o_, npar, 1)
                if s1:
                    kt(q, npar, 1)
                if outq:
                    t_r(o_, 1)
                if s1:
                    k_tok(q, npar, 0)
                if outq:
                    k_d(o_, npar, 1)
                    p_d(o_, npar, 1)
                if s1:
                    k_tok(q, npar, 1)
                    vb(q, npar)
                    kk(q, npar, 0)
                    kk(q, npar, 1)
                if outq:
                    o_sums(o_)
                if main:
                    z_32(p)
                if s1:
                    gate_t(q, npar)
                if main:
                    w_32(p)
                if s1:
                    qt(q, npar, 0)
                if main:
                    z_64(p, par)
                if outq:
                    o_proj(o_)
                if s1:
                    qt(q, npar, 1)
                if main:
                    w_64(p)
                if s1:
                    kq(q, npar, 0)
                if main:
                    z_128(p, par)
                if outq:
                    x1_t(o_, npar)
                if s1:
                    kq(q, npar, 1)
                if main:
                    w_128(p)
                if outq:
                    logits(o_)
                if main:
                    ks(p, par, 0)
                    qs(p, par, 0)
                    t_r(p, 0)
                if outq:
                    cum(o_)
                if main:
                    k_d(p, par, 0)
                    p_d(p, par, 0)

            phase_a(pe, step)

            def flip(n, par):
                pe.wait_ge(xe_ld[par], 8 * n + 16 - 8 * par)
                wait(pe, xeT_ready, 2 * n)
                for i in range(CT):
                    last = nc.tensor.transpose(ps[:, i // 4, P * (i % 4):P * (i % 4) + P], xe[:, par, i, :], ident[:])
                last.then_inc(xeT_mm, 1)

            def hidden(n, par):
                pe.wait_ge(ew_ld[par], 3 * (8 * n + 16 - 8 * par))
                pe.wait_ge(xeT_ready, 2 * n + 2)
                for c in range(FC):
                    for g in range(2):
                        s = 2 * c + g
                        wait(pe, h_ready, 8 * n + s - 1)
                        cols = slice(HALF * g, HALF * g + HALF)
                        mm(ps[0:FW, 2 + g, 0:HALF], w1s[:, par, FW * c:FW * c + FW], xeT[:, par, cols],
                           start=True, stop=True)
                        mm(ps[0:FW, 4 + g, 0:HALF], w3s[:, par, FW * c:FW * c + FW], xeT[:, par, cols],
                           start=True, stop=True).then_inc(h_mm, 1)

            def down(n, par):
                pe.wait_ge(h_ready, 8 * n + 8)
                wait(pe, ye_ready, n)
                for i in range(CT):
                    for c in range(FC):
                        last = mm(ps[:, 6 + i // 4, P * (i % 4):P * (i % 4) + P], hb[:, par, c, P * i:P * i + P],
                                  w2s[:, par, c, :], start=(c == 0), stop=(c == FC - 1))
                last.then_inc(y_mm, 1)

            pe.wait_ge(slot_ready, NP)
            def unit(n, par):
                hidden(n, par)
                flip(n + 1, 1 - par)
                down(n, par)

            flip(0, 0)
            for par in range(2):
                unit(par, par)
            with pe.Fori(1, B * E // 2 - 1) as i:
                for par in range(2):
                    unit(2 * i + par, par)
            hidden(B * E - 2, 0)
            flip(B * E - 1, 1)
            down(B * E - 2, 0)
            hidden(B * E - 1, 1)
            down(B * E - 1, 1)

        @block.scalar
        def _(act):
            link = Link(act, link_act)
            af = nc.scalar.activation
            nc.scalar.preload_act_table_set("natural_log_exp_and_others")
            fill_bank = [g % 3 for g in range(12)]
            ZB, WB, CB, OB, MB = 3, 4, 5, 6, 7

            def rsqrt(out_ap, ln_ap, in_ap):
                link(af(ln_ap, in_ap, ACT.Ln))
                return af(out_ap, ln_ap, ACT.Exp, scale=-0.5)

            def k_out(q, par, j):
                act.wait_ge(filled, 12 * q + 3 + j)
                if j == 0:
                    wait(act, chain_mm, 8 * (q - 2) + 7)
                    wait(act, br_ready, q)
                af(K[:, par, j, :], ps[:, fill_bank[2 + j], :], ACT.Copy)
                for h in range(H):
                    last = af(junk[:, H * j + h, :], ps[:, fill_bank[2 + j], DK * h:DK * h + DK], ACT.Square,
                              accum_out=ss[:, H * j + h:H * j + h + 1])
                last.then_inc(freed_act, 1)

            def vb_out(q):
                act.wait_ge(filled, 12 * q + 5)
                wait(act, gate_ready, 2 * q)
                both = ps[:, fill_bank[4], 0:2 * VW].rearrange("p (j c) -> p j c", j=2)
                af(eb[:], both[:, :, H * DV:], ACT.Exp, scale=-1.0)
                af(V[:], both[:, :, 0:H * DV], ACT.Copy).then_inc(freed_act, 1)

            def g_out(q):
                act.wait_ge(filled, 12 * q + 8)
                af(G[:], ps[:, fill_bank[7], 0:2 * P], ACT.Copy)
                ins = af(eg[:], ps[:, fill_bank[7], 0:2 * P], ACT.Exp, scale=-1.0)
                ins.then_inc(freed_act, 1)
                act.wait_ge(freed_act, 8 * q + 6)
                link(af(lsg[:], eg[:], ACT.Ln, bias=one[:]))
                af(sg[:], lsg[:], ACT.Exp, scale=-1.0).then_inc(sg_ready, 1)

            def q_out(q, par, g):
                act.wait_ge(filled, 12 * q + 9 + g)
                af(QT[:, par, 2 * g:2 * g + 2, :], ps[:, fill_bank[8 + g], :].rearrange("p (h t) -> p h t", h=2),
                   ACT.Copy, scale=SCALE).then_inc(freed_act, 1)

            def delta(p, j):
                act.wait_ge(chain_mm, 8 * p + 4 * j + 2)
                af(dl[:], ps[:, CB, 128:256], ACT.Copy).then_inc(d_ready, 1)

            def o_out(p, par):
                act.wait_ge(chain_mm, 8 * p + 8)
                wait(act, og_ready, p)
                af(o[:], ps[:, OB, 0:2 * P], ACT.Copy).then_inc(o_ready, 1)

            def step(p, par, s1, main, outq):
                q, npar, o_ = p + 1, 1 - par, p - 1
                if s1:
                    for g in range(2):
                        act.wait_ge(filled, 12 * q + g + 1)
                        if g == 0:
                            wait(act, chain_mm, 8 * (q - 2) + 5)
                        af(KT[:, npar, 2 * g:2 * g + 2, :], ps[:, fill_bank[g], :].rearrange("p (h t) -> p h t", h=2),
                           ACT.Copy).then_inc(freed_act, 1)
                if outq:
                    delta(o_, 1)
                if s1:
                    k_out(q, npar, 0)
                if outq:
                    o_out(o_, npar)
                if s1:
                    k_out(q, npar, 1)
                    vb_out(q)
                    act.wait_ge(ssp_ready, q + 1)
                    rsqrt(rk[:], lnk[:], ssp[:]).then_inc(rk_ready, 1)
                if outq:
                    act.wait_ge(out_mm, 5 * o_ + 1)
                    link(af(oln[:], ps[:, MB, 0:2 * P], ACT.Ln, scale=1.0 / DV, bias=eps[:]))
                    af(orms[:], oln[:], ACT.Exp, scale=-0.5).then_inc(orms_ready, 1)
                if s1:
                    g_out(q)
                if main:
                    act.wait_ge(lvl_dve, 4 * p + 2)
                    wait(act, chain_mm, 8 * (p - 1) + 6)
                    for k in range(4):
                        s = slice(32 * k, 32 * k + 32)
                        last = af(TT[s, :, 32 * k:32 * k + 32], x32T[s, :, :], ACT.Copy)
                    last.then_inc(lvl_act, 1)
                    wait(act, lvl_mm, 6 * p)
                    for k in range(2):
                        s = slice(32 * k, 32 * k + 32)
                        last = af(x64[s, :, 32 * k:32 * k + 32], x32[s, :, :], ACT.Copy)
                    last.then_inc(x64_diag, 1)
                if s1:
                    q_out(q, npar, 0)
                    q_out(q, npar, 1)
                if outq:
                    act.wait_ge(ve_ready, p)
                    rsqrt(rstd[:], vl[:], ve[:]).then_inc(rstd_ready, 1)
                if main:
                    act.wait_ge(lvl_mm, 6 * p + 5)
                    af(z128[:], ps[0:64, ZB, :].rearrange("p (u c) -> p u c", u=U), ACT.Copy).then_inc(lvl_act, 1)
                if outq:
                    act.wait_ge(out_mm, 5 * o_ + 3)
                    af(x1T[:], ps[:, MB, 0:256], ACT.Copy).then_inc(x1T_ready, 1)
                if main:
                    act.wait_ge(lvl_mm, 6 * p + 6)
                    af(TT[0:64, :, 64:128], ps[0:64, WB, :].rearrange("p (u c) -> p u c", u=U), ACT.Copy,
                       scale=-1.0).then_inc(lvl_act, 1)
                if outq:
                    act.wait_ge(nm_ready, p)
                    for j in range(2):
                        last = af(e8[:, j, :], v8[:, j, :], ACT.Exp, bias=nm[:, j:j + 1], accum_out=es[:, j:j + 1])
                    last.then_inc(e8_ready, 1)
                if main:
                    delta(p, 0)

            phase_a(act, step, link, ACT_LINKS)

            def turn(n, par):
                act.wait_ge(xeT_mm, n + 1)
                wait(act, h_mm, 8 * (n - 1))
                af(xeT[:, par, 0:512], ps[:, 0, :], ACT.Copy).then_inc(xeT_ready, 1)
                af(xeT[:, par, 512:CAP], ps[:, 1, 0:CAP - 512], ACT.Copy).then_inc(xeT_ready, 1)

            def gate(n, s):
                act.wait_ge(h_mm, 8 * n + s + 1)
                wait(act, h_ready, 8 * n + s - 1)
                af(hs[:, s % 2, :], ps[0:FW, 2 + s % 2, 0:HALF], ACT.Silu).then_inc(hs_ready, 1)

            def y_out(n, par):
                act.wait_ge(y_mm, n + 1)
                wait(act, ye_st[par], 8 * n - 8 * par)
                af(ye[:, par, 0:4, :], ps[:, 6, :].rearrange("p (i d) -> p i d", i=4), ACT.Copy)
                af(ye[:, par, 4, :], ps[:, 7, 0:P], ACT.Copy).then_inc(ye_ready, 1)

            turn(0, 0)
            for s in range(8):
                gate(0, s)
            turn(1, 1)
            y_out(0, 0)
            for s in range(8):
                gate(1, s)
            turn(2, 0)
            y_out(1, 1)
            with act.Fori(1, B * E // 2 - 1) as i:
                for par in range(2):
                    n = 2 * i + par
                    for s in range(8):
                        gate(n, s)
                    turn(n + 1, 1 - par)
                    y_out(n, par)
            for s in range(8):
                gate(B * E - 2, s)
            turn(B * E - 1, 1)
            y_out(B * E - 2, 0)
            for s in range(8):
                gate(B * E - 1, s)
            y_out(B * E - 1, 1)

            nc.scalar.preload_act_table_set("natural_log_exp_and_others")
            with act.Fori(0, NP // 2) as i:
                link.enter(i, 2)
                for par in range(2):
                    act.wait_ge(cve_ready, 2 * i + par + 1)
                    rsqrt(rstd[:], vl[:], ve[:]).then_inc(crstd_ready, 1)
            link.leave(NP // 2)

        @block.vector
        def _(dve):
            link = Link(dve, link_dve)
            v = nc.vector
            fill_bank = [g % 3 for g in range(12)]
            ZB, WB, CB, OB, MB = 3, 4, 5, 6, 7

            for t in (TT, x64, St, carry):
                v.memset(t[:], 0.0)
            for t, at in ((keep_s, PB - 1), (keep_c, PB)):
                link(v.memset(t[:], 1.0))
                v.memset(t[:, at:at + 1], 0.0)
            v.memset(eps[:], EPS)
            v.memset(one[:], 1.0)
            link(v.memset(base[:], -1.0))
            v.memset(base[:, PB + 1:], float(E * CAP - 1))
            dve.wait_ge(consts_pool, 6)
            link(v.tensor_scalar(pbit[:], pidx[:], 16, None, ALU.bitwise_and))
            link(v.tensor_copy(pcol[:], pbit[:]))
            link(v.tensor_scalar(high[:], pcol[:], 1.0 / 16, None, ALU.mult))
            link(v.tensor_scalar(low[:], high[:], -1.0, 1.0, ALU.mult, ALU.add))
            link(v.tensor_copy(pcol[:], pidx[:]))
            for k in range(4):
                v.tensor_scalar(spare[:, k:k + 1], pcol[:], float(ROWS + P * k), None, ALU.add)
            v.tensor_copy(tri[:], upper[:])
            link(v.memset(ones[:], 1.0))
            v.tensor_copy(M[:, 0, :], tri[:, 0:E]).then_inc(consts_dve, 1)
            dve.wait_ge(w_ld, W_LOADS)
            v.tensor_scalar(wo[:], wo0[:], nw[:], None, ALU.mult).then_inc(wo_ready, 1)

            def step(p, par, s1, main, outq):
                q, npar, o_ = p + 1, 1 - par, p - 1
                if outq:
                    chain_r(o_, npar, 1)
                    chain_s(o_, 1)
                if main:
                    dve.wait_ge(xi_ld, 16 * p + 16)
                    v.tensor_tensor(x16d[:].rearrange("p u (b c) -> p u b c", c=16), bc(xi[:, 0], 2, 8),
                                    bc(mask16[:].rearrange("p (b c) -> p b c", c=16), 1, U), ALU.mult)
                    v.tensor_scalar(x32T[:, :, 0:16], xi[:, 1], low[:], None, ALU.mult).then_inc(prep, 1)
                if s1:
                    dve.wait_ge(freed_act, 8 * q + 4)
                    v.tensor_scalar(ssp[:], ss[:], 1e-12, None, ALU.add).then_inc(ssp_ready, 1)
                    dve.wait_ge(ssp_ready, q + 1)
                    v.reciprocal(rr[:], ssp[:])
                    dve.wait_ge(freed_act, 8 * q + 5)
                    link(v.tensor_scalar(bden[:], eb[:].rearrange("p j h -> p (j h)"), 1.0, None, ALU.add))
                    link(v.reciprocal(beta[:], bden[:]))
                    v.tensor_tensor(c2[:, npar, :], beta[:], rr[:], ALU.mult)
                    dve.wait_ge(rk_ready, q + 1)
                    v.tensor_tensor(br[:], beta[:], rk[:], ALU.mult).then_inc(br_ready, 1)
                    dve.wait_ge(br_ready, q + 1)
                    lower(q, npar, 0)
                    lower(q, npar, 1)
                if main:
                    dve.wait_ge(lvl_mm, 6 * p + 1)
                    v.tensor_copy(z32[:], ps[:, ZB, 0:128].rearrange("p (u c) -> p u c", u=U)).then_inc(lvl_dve, 1)
                    dve.wait_ge(lvl_mm, 6 * p + 2)
                    link(v.scalar_tensor_tensor(out=x32T[:, :, 16:32], in0=xi[:, 1], scalar=high[:],
                                                in1=ps[:, WB, 0:128].rearrange("p (u c) -> p u c", u=U),
                                                op0=ALU.mult, op1=ALU.subtract))
                    v.transpose(x32[:].rearrange("p u c -> p (u c)"),
                                x32T[:].rearrange("p u c -> p (u c)")).then_inc(lvl_dve, 1)
                    dve.wait_ge(lvl_mm, 6 * p + 3)
                    v.tensor_copy(z64[:], ps[:, ZB, 0:256].rearrange("p (u c) -> p u c", u=U)).then_inc(lvl_dve, 1)
                if outq:
                    dve.wait_ge(out_mm, 5 * o_ + 2)
                    dve.wait_ge(xk_ld[npar], 8 * o_ + 16 - 8 * npar)
                    v.tensor_tensor(r1[:], ps[:, MB, 0:256].rearrange("p (j d) -> p j d", j=2), xk[:, npar],
                                    ALU.add).then_inc(r1_ready, 1)
                    dve.wait_ge(r1_ready, p)
                    moments(r1).then_inc(ve_ready, 1)
                if main:
                    dve.wait_ge(lvl_mm, 6 * p + 4)
                    dve.wait_ge(lvl_act, 3 * p + 1)
                    for m in (1, 0):
                        s = slice(64 * m, 64 * m + 32)
                        last = v.tensor_scalar(TT[s, :, 64 * m + 32:64 * m + 64],
                                               ps[s, WB, 0:256].rearrange("p (u c) -> p u c", u=U), -1.0, None, ALU.mult)
                    link(last)
                    for u in range(U):
                        last = v.transpose(x64[32:64, u, 0:32], TT[0:32, u, 32:64])
                    last.then_inc(lvl_dve, 1)
                if outq:
                    dve.wait_ge(rstd_ready, p)
                    wait(dve, x1_st[npar], 8 * o_ - 8 * npar)
                    wait(dve, scat[npar], 4 * (8 * o_ - 8 * npar))
                    for j in range(2):
                        last = v.tensor_scalar(x1[:, npar, j, :], r1[:, j, :], mv[:, j, 0:1], rstd[:, j:j + 1],
                                               ALU.subtract, ALU.mult)
                    last.then_inc(x1_ready, 1)
                if s1:
                    masked_q(q, npar, 0)
                    masked_q(q, npar, 1)
                if outq:
                    route(o_)
                if main:
                    chain_r(p, par, 0)
                if outq:
                    place(o_, p, npar)
                if main:
                    chain_s(p, 0)

            def moments(src):
                for j in range(2):
                    last = v.bn_stats(bst[:, j, :], src[:, j, :])
                link(last)
                apart(dve)
                for j in range(2):
                    last = v.bn_aggr(mv[:, j, :], bst[:, j, :])
                link(last)
                return v.tensor_scalar(ve[:], mv[:, :, 1], EPS, None, ALU.add)

            def lower(q, par, j):
                dve.wait_ge(filled, 12 * q + 6 + j)
                if j == 0:
                    wait(dve, a_st, 64 * q)
                    wait(dve, m32_ready, q - 1)
                for h in range(H):
                    last = v.scalar_tensor_tensor(out=A[:, par, H * j + h, :], in0=ps[:, fill_bank[5 + j], P * h:P * h + P],
                                                  scalar=c2[:, par, H * j + h:H * j + h + 1], in1=strict[:],
                                                  op0=ALU.mult, op1=ALU.mult)
                last.then_inc(freed_dve, 1)

            def masked_q(q, par, j):
                dve.wait_ge(filled, 12 * q + 11 + j)
                if j == 0:
                    wait(dve, chain_mm, 8 * (q - 2) + 8)
                v.tensor_tensor(PT[:, par, H * j:H * j + H, :],
                                ps[:, fill_bank[10 + j], :].rearrange("p (h t) -> p h t", h=H),
                                bc(upper[:], 1, H), ALU.mult).then_inc(freed_dve, 1)

            def chain_r(p, par, j):
                dve.wait_ge(chain_mm, 8 * p + 4 * j + 1)
                if j == 0:
                    dve.wait_ge(gate_ready, 2 * p + 2)
                link(v.tensor_tensor(tmp[:].rearrange("p (h d) -> p h d", h=H),
                                     ps[:, CB, 0:128].rearrange("p (h d) -> p h d", h=H),
                                     bc(c2[:, par, H * j:H * j + H], 2, DV), ALU.mult))
                v.tensor_tensor(R[:], Vp[:, par, j, :], tmp[:], ALU.subtract).then_inc(r_ready, 1)

            def chain_s(p, j):
                dve.wait_ge(chain_mm, 8 * p + 4 * j + 3)
                if j == 0:
                    v.tensor_tensor(St[:], St[:], ps[:, CB, 256:384], ALU.add).then_inc(s_ready, 1)
                else:
                    link(v.tensor_tensor(St[:], St[:], ps[:, CB, 256:384], ALU.add))
                    v.tensor_scalar(St[:], St[:], keep_s[:, bass.ds(p, 1)], None, ALU.mult).then_inc(s_ready, 1)

            def route(q):
                dve.wait_ge(out_mm, 5 * q + 4)
                link(v.tensor_copy(lg[:], ps[:, MB, 0:2 * E].rearrange("p (j e) -> p j e", j=2)))
                apart(dve)
                for j in range(2):
                    last = v.max(v8[:, j, :], lg[:, j, :])
                link(last)
                apart(dve)
                for j in range(2):
                    last = v.max_index(i8[:, j, :], v8[:, j, :], lg[:, j, :])
                v.tensor_scalar(nm[:], v8[:, :, 0], -1.0, None, ALU.mult).then_inc(nm_ready, 1)
                dve.wait_ge(nm_ready, q + 1)
                link(v.tensor_copy(idxf[:], i8[:, :, 0:TOPK]))
                link(v.tensor_tensor(oh[:].rearrange("p j k e -> p (j k) e"), bc(iota8[:], 1, 4),
                                     bc(idxf[:].rearrange("p j k -> p (j k)"), 2, E), ALU.is_equal))
                v.tensor_tensor(M[:], oh[:, :, 0, :], oh[:, :, 1, :], ALU.add).then_inc(M_ready, 1)

            def place(q, p, par):
                dve.wait_ge(out_mm, 5 * q + 5)
                v.tensor_tensor(cc[:], ps[:, MB, 0:2 * E].rearrange("p (j e) -> p j e", j=2), bc(carry[:], 1, 2), ALU.add)
                link(v.tensor_tensor(carry0[:], ps[:, MB, 2 * E:3 * E], carry[:], ALU.add))
                v.tensor_scalar(carry[:], carry0[:], keep_c[:, bass.ds(p, 1)], None, ALU.mult)
                for j in range(2):
                    last = v.tensor_tensor(pr[:, j], oh[:, j], bc(cc[:, j, :], 1, TOPK), ALU.mult)
                link(last)
                link(v.tensor_reduce(cnt[:], pr[:].rearrange("p j k e -> p (j k) e"), AX.X, ALU.add))
                v.tensor_scalar(valid[:], cnt[:], float(CAP), None, ALU.is_le)
                link(v.scalar_tensor_tensor(out=sl[:], in0=idxf[:].rearrange("p j k -> p (j k)"), scalar=float(CAP),
                                            in1=cnt[:], op0=ALU.mult, op1=ALU.add))
                link(v.scalar_tensor_tensor(out=sd[:], in0=sl[:], scalar=base[:, bass.ds(p, 1)], in1=spare[:],
                                            op0=ALU.add, op1=ALU.subtract))
                link(v.tensor_tensor(sv[:], sd[:], valid[:], ALU.mult))
                link(v.tensor_tensor(slf[:], sv[:], spare[:], ALU.add))
                v.tensor_copy(slots[:, bass.ds(4 * q, 4)], slf[:])
                wait(dve, scat[par], 4 * (8 * q - 8 * par))
                v.tensor_copy(slot[:, par, :], slf[:])
                dve.wait_ge(e8_ready, q + 1)
                link(v.reciprocal(rs[:], es[:]))
                link(v.tensor_tensor(wv[:], e8[:, :, 0:TOPK], bc(rs[:], 2, TOPK), ALU.mult))
                v.tensor_tensor(gates[:, bass.ds(4 * q, 4)], wv[:].rearrange("p j k -> p (j k)"), valid[:],
                                ALU.mult).then_inc(slot_ready, 1)

            phase_a(dve, step, link, DVE_LINKS)

            def gated(n, par, s):
                dve.wait_ge(hs_ready, 8 * n + s + 1)
                if s == 0:
                    wait(dve, y_mm, n - 1)
                c, g = s // 2, s % 2
                v.tensor_tensor(hb[:, par, c, HALF * g:HALF * g + HALF], ps[0:FW, 4 + g, 0:HALF], hs[:, g, :],
                                ALU.mult).then_inc(h_ready, 1)

            for n in range(2):
                for s in range(8):
                    gated(n, n, s)
            with dve.Fori(1, B * E // 2) as i:
                for par in range(2):
                    for s in range(8):
                        gated(2 * i + par, par, s)

            def indices(p, par):
                wait(dve, gb_ld[par], 4 * (8 * p - 8 * par))
                v.tensor_copy(gi[:, par, :], slots[:, bass.ds(4 * p, 4)]).then_inc(gi_ready, 1)

            def combine(p, par):
                dve.wait_ge(gb_ld[par], 4 * (8 * p + 16 - 8 * par))
                dve.wait_ge(x1c_ld[par], 8 * p + 16 - 8 * par)
                for j in range(2):
                    last = v.scalar_tensor_tensor(out=ya[:, j, :], in0=gb[:, par, 2 * j, :],
                                                  scalar=gates[:, bass.ds(4 * p + 2 * j, 1)],
                                                  in1=x1c[:, par, j, :], op0=ALU.mult, op1=ALU.add)
                link(last)
                for j in range(2):
                    last = v.scalar_tensor_tensor(out=yb[:, j, :], in0=gb[:, par, 2 * j + 1, :],
                                                  scalar=gates[:, bass.ds(4 * p + 2 * j + 1, 1)],
                                                  in1=ya[:, j, :], op0=ALU.mult, op1=ALU.add)
                link(last)
                moments(yb).then_inc(cve_ready, 1)
                dve.wait_ge(crstd_ready, p + 1)
                wait(dve, out_st[par], 8 * p - 8 * par)
                for j in range(2):
                    last = v.tensor_scalar(yo[:, par, j, :], yb[:, j, :], mv[:, j, 0:1], rstd[:, j:j + 1],
                                           ALU.subtract, ALU.mult)
                last.then_inc(yo_ready, 1)

            indices(0, 0)
            indices(1, 1)
            combine(0, 0)
            indices(2, 0)
            combine(1, 1)
            indices(3, 1)
            with dve.Fori(1, NP // 2 - 1) as i:
                link.enter(i - 1, 8)
                for par in range(2):
                    combine(2 * i + par, par)
                    indices(2 * i + par + 2, par)
            link.leave(NP // 2 - 2)
            combine(NP - 2, 0)
            combine(NP - 1, 1)

        @block.gpsimd
        def _(pool):
            link = Link(pool, link_pool)
            g = nc.gpsimd
            g.memset(zeros[:], 0.0).then_inc(consts_pool, 1)
            for t, fill in ((ident, 0.0), (strict, 1.0), (upper, 1.0), (id16, 0.0), (mask16, 1.0), (mask32, 1.0),
                            (heads, 1.0)):
                last = g.memset(t[:], fill)
            link(last)
            g.affine_select(out=ident[:], in_=ident[:], compare_op=ALU.not_equal, fill=1.0, base=0,
                            pattern=[[-1, P]], channel_multiplier=1).then_inc(consts_pool, 1)
            g.affine_select(out=strict[:], in_=strict[:], compare_op=ALU.is_ge, fill=0.0, base=-1,
                            pattern=[[-1, P]], channel_multiplier=1).then_inc(consts_pool, 1)
            g.affine_select(out=upper[:], in_=upper[:], compare_op=ALU.is_ge, fill=0.0, base=0,
                            pattern=[[1, P]], channel_multiplier=-1).then_inc(consts_pool, 1)
            by16 = mask16[:].rearrange("p (b c) -> p b c", c=16)
            link(g.affine_select(out=by16, in_=by16, compare_op=ALU.is_ge, fill=0.0, base=0,
                                 pattern=[[-16, 8], [0, 16]], channel_multiplier=1))
            link(g.affine_select(out=by16, in_=by16, compare_op=ALU.is_ge, fill=0.0, base=15,
                                 pattern=[[16, 8], [0, 16]], channel_multiplier=-1))
            by_head = heads[:].rearrange("p (b c) -> p b c", c=DV)
            link(g.affine_select(out=by_head, in_=by_head, compare_op=ALU.is_ge, fill=0.0, base=0,
                                 pattern=[[-DV, H], [0, DV]], channel_multiplier=1))
            link(g.affine_select(out=by_head, in_=by_head, compare_op=ALU.is_ge, fill=0.0, base=DV - 1,
                                 pattern=[[DV, H], [0, DV]], channel_multiplier=-1))
            by32 = mask32[:].rearrange("p (b c) -> p b c", c=32)
            link(g.affine_select(out=by32, in_=by32, compare_op=ALU.is_ge, fill=0.0, base=-16,
                                 pattern=[[-32, 4], [0, 32]], channel_multiplier=1))
            link(g.affine_select(out=by32, in_=by32, compare_op=ALU.is_ge, fill=0.0, base=31,
                                 pattern=[[32, 4], [0, 32]], channel_multiplier=-1))
            link(g.affine_select(out=by32, in_=by32, compare_op=ALU.is_ge, fill=0.0, base=15,
                                 pattern=[[0, 4], [-1, 32]], channel_multiplier=0))
            g.iota(pidx[:], pattern=[[0, 1]], base=0, channel_multiplier=1).then_inc(consts_pool, 1)
            g.iota(iota8[:], pattern=[[1, E]], base=0, channel_multiplier=0,
                   allow_small_or_imprecise_dtypes=True).then_inc(consts_pool, 1)
            link(g.affine_select(out=id16[:], in_=id16[:], compare_op=ALU.not_equal, fill=1.0, base=0,
                                 pattern=[[-1, 16], [1, 16]], channel_multiplier=0))

            def solve(q):
                wait(pool, xi_st, 16 * q)
                apart(pool)
                link(g.tensor_copy(xs[:, 0], id16[:]))
                pool.wait_ge(ab_ld, 16 * q + 16)
                for j in range(15):
                    n = 15 - j
                    pr_ = prod[:, 0:n * (j + 1)].rearrange("p (i c) -> p i c", c=j + 1)
                    link(g.tensor_tensor(pr_, bc(ab[:, j + 1:, j], 2, j + 1), bc(xs[:, 0, j, 0:j + 1], 1, n), ALU.mult))
                    link(g.tensor_tensor(xs[:, 0, j + 1:, 0:j + 1], xs[:, 0, j + 1:, 0:j + 1], pr_, ALU.subtract))
                apart(pool)
                g.tensor_copy(xs[:, 1], xs[:, 0].rearrange("p r c -> p c r")).then_inc(solved, 1)

            def step(p, par, s1, main, outq):
                q, npar, o_ = p + 1, 1 - par, p - 1
                if outq:
                    pool.wait_ge(o_ready, p)
                    g.tensor_tensor(osq[:], o[:], o[:], ALU.mult).then_inc(osq_ready, 1)
                    pool.wait_ge(orms_ready, p)
                    link(g.tensor_tensor(on[:], o[:], orms[:], ALU.mult))
                    wait(pool, out_mm, 5 * (o_ - 1) + 2)
                    g.tensor_tensor(og[:], on[:], silu[:, npar], ALU.mult).then_inc(og_ready, 1)
                if s1:
                    pool.wait_ge(freed_dve, 4 * q + 2)
                    wait(pool, lvl_mm, 6 * p + 1)
                    g.tensor_tensor(m32[:], A[:, npar], bc(mask32[:], 1, U), ALU.mult).then_inc(m32_ready, 1)
                    solve(q)
                if outq:
                    pool.wait_ge(slot_ready, p)
                    if isinstance(p, int) and p == 1:
                        pool.wait_ge(zero_st, 16 * (ROWS // P // 8 + 1))
                    apart(pool)
                    for j in range(2):
                        for k in range(TOPK):
                            g.indirect_dma_start(
                                out=xs_d[:, :], out_offset=bass.IndirectOffsetOnAxis(ap=slot[:, npar, 2 * j + k:2 * j + k + 1], axis=0),
                                in_=x1[:, npar, j, :], in_offset=None).then_inc(scat[npar], 16)
                if s1:
                    pool.wait_ge(sg_ready, q + 1)
                    g.tensor_tensor(silu[:, npar], G[:], sg[:], ALU.mult).then_inc(gate_ready, 1)
                    pool.wait_ge(br_ready, q + 1)
                    wait(pool, r_ready, 2 * (q - 1))
                    for j in range(2):
                        last = g.tensor_tensor(Vp[:, npar, j, :].rearrange("p (h d) -> p h d", h=H),
                                               V[:, j, :].rearrange("p (h d) -> p h d", h=H),
                                               bc(br[:, H * j:H * j + H], 2, DV), ALU.mult)
                    last.then_inc(gate_ready, 1)

            phase_a(pool, step, link, POOL_LINKS)

            def gather(p, par):
                pool.wait_ge(gi_ready, p + 1)
                wait(pool, yo_ready, p - 1)
                apart(pool)
                for k in range(4):
                    g.indirect_dma_start(
                        out=gb[:, par, k, :], out_offset=None, in_=ys_d[:, :],
                        in_offset=bass.IndirectOffsetOnAxis(ap=gi[:, par, k:k + 1], axis=0)).then_inc(gb_ld[par], 16)

            pool.wait_ge(ye_st[0], 16 * B * E // 2)
            pool.wait_ge(ye_st[1], 16 * B * E // 2)
            gather(0, 0)
            gather(1, 1)
            with pool.Fori(1, NP // 2) as i:
                for par in range(2):
                    gather(2 * i + par, par)


ACT_LINKS = 8
DVE_LINKS = 44
POOL_LINKS = 64


def kernel(L0_attn_x, L0_attn_Wq, L0_attn_Wk, L0_attn_Wv, L0_attn_Wb, L0_attn_Wg, L0_attn_Wo, L0_attn_norm_w,
           L0_ffn_gate_w, L0_ffn_w1, L0_ffn_w2, L0_ffn_w3):
    import concourse.bacc as bacc
    from concourse.bass_utils import run_bass_kernel_spmd

    x = np.ascontiguousarray(L0_attn_x).reshape(B * S, D)
    arrays = {
        "x": x, "xT": np.ascontiguousarray(x.T),
        "Wq": np.ascontiguousarray(L0_attn_Wq), "Wk": np.ascontiguousarray(L0_attn_Wk),
        "Wvb": np.ascontiguousarray(np.concatenate([np.asarray(L0_attn_Wv), np.asarray(L0_attn_Wb)], axis=1)),
        "Wg": np.ascontiguousarray(L0_attn_Wg),
        "Wo": np.ascontiguousarray(L0_attn_Wo),
        "norm_w": np.ascontiguousarray(L0_attn_norm_w),
        "gateT": np.ascontiguousarray(np.asarray(L0_ffn_gate_w).T),
        "w1": np.ascontiguousarray(L0_ffn_w1), "w2": np.ascontiguousarray(L0_ffn_w2),
        "w3": np.ascontiguousarray(L0_ffn_w3),
    }
    nc = bacc.Bacc("TRN2", target_bir_lowering=False, num_devices=1)
    args = [nc.dram_tensor(n, a.shape, F32, kind="ExternalInput").ap() for n, a in arrays.items()]
    out = nc.dram_tensor("result", (B * S, D), F32, kind="ExternalOutput").ap()
    build(nc, *args, out)
    r = run_bass_kernel_spmd(nc, [arrays], core_ids=[0])
    return r.results[0]["result"].reshape(B, S, D)
```

```python
from contextlib import ExitStack

import numpy as np

import concourse.bass as bass
from concourse import mybir

F32 = mybir.dt.float32
F32R = mybir.dt.float32r
BF16 = mybir.dt.bfloat16
I32 = mybir.dt.int32
U32 = mybir.dt.uint32
ALU = mybir.AluOpType
ACT = mybir.ActivationFunctionType
AX = mybir.AxisListType

P = 128
B, S, D = 2, 2048, 128
H, DK, DV = 4, 128, 32
E, F, TOPK = 8, 448, 2
CAP = int(S * TOPK / E * 1.25)
FC, FW = 4, F // 4
NT = B * S // P
NP = NT // B
U = B * H
ROWS = B * E * CAP
SPARE = 4 * P
CT = CAP // P
HALF = CAP // 2
W = D + 1
RES = TOPK * S
NC = NT // 2
EPS = 1e-5
SCALE = DK ** -0.5
BLK = 16 * 32 + 16
VW = H * DV + H
ZEROS = 16 * (ROWS + B * RES) // P // 8
W_LOADS = 16 * (6 + H)
LOOP0, LOOP1 = 2, NP - 2


def wait(eng, sem, value):
    if isinstance(value, int) and value <= 0:
        return
    eng.wait_ge(sem, value)


def apart(eng):
    eng.nop(nofuse=True)


class Link:

    def __init__(self, eng, sem):
        self.eng, self.sem, self.n, self.off = eng, sem, 0, 0

    def __call__(self, ins):
        ins.then_inc(self.sem, 1)
        self.n += 1
        self.eng.wait_ge(self.sem, self.n + self.off)

    def enter(self, step, per_step):
        self.start, self.per, self.off = self.n, per_step, step * per_step

    def leave(self, steps):
        assert self.n - self.start == self.per, (self.n - self.start, self.per)
        self.n, self.off = self.start + self.per * steps, 0


def bc(ap, axis, n):
    shape = list(ap.shape)
    shape.insert(axis, n)
    return ap.unsqueeze(axis).to_broadcast(shape)


def build(nc, x, xT, Wq, Wk, Wvb, Wg, Wo, norm_w, gateT, w1, w2, w3, out):
    xs_d = nc.dram_tensor("slots_in", (ROWS + SPARE, W), F32, kind="Internal").ap()
    y_d = [nc.dram_tensor(f"results{b}", (RES + 2 * CAP, D), F32, kind="Internal").ap() for b in range(B)]
    x1_d = nc.dram_tensor("x1_store", (NT * P, D), F32, kind="Internal").ap()
    ad_d = nc.dram_tensor("a_diag", (U * 4, 2 * BLK), F32, kind="Internal").ap()
    xi_d = nc.dram_tensor("inv16", (2, U * P, 16), F32, kind="Internal").ap()

    def tile_of(rows, t):
        return rows.rearrange("(b t p) d -> p b t d", b=B, p=P)[:, :, bass.ds(t, 1), :].rearrange("p b o d -> p b (o d)")

    ctx = ExitStack()
    with ctx:
        def sb(name, shape, dt=F32):
            return ctx.enter_context(nc.sbuf_tensor(name, shape, dt))

        def sem(name):
            return ctx.enter_context(nc.semaphore(name))

        ps = ctx.enter_context(nc.psum_tensor("ps", [P, 8, 512], F32))

        ident = sb("ident", [P, P])
        strict = sb("strict", [P, P])
        upper = sb("upper", [P, P])
        tri = sb("tri", [P, P], BF16)
        ones = sb("ones", [P, P], BF16)
        iota8 = sb("iota8", [P, E])
        pidx = sb("pidx", [P, 1], I32)
        pbit = sb("pbit", [P, 1], I32)
        pcol = sb("pcol", [P, 1])
        low = sb("low", [P, 1])
        high = sb("high", [P, 1])
        spare = sb("spare", [P, 4])
        shift = sb("shift", [P, 4])
        id16 = sb("id16", [64, 16, 16])
        heads = sb("heads", [P, P])
        eps = sb("eps", [P, 1])
        one = sb("one", [P, 1])
        zeros = sb("zeros", [P, 8 * W])
        ids = sb("ids", [P, NP, B, TOPK])
        spare_y = sb("spare_y", [P, 2, CT])
        mask16 = sb("mask16", [P, P])
        mask32 = sb("mask32", [P, P])
        wq = sb("wq", [P, H * DK])
        wk = sb("wk", [P, H * DK])
        wvb = sb("wvb", [P, VW])
        wg = sb("wg", [P, H * DV])
        wo0 = sb("wo0", [P, D])
        wo = sb("wo", [P, D])
        nw = sb("nw", [P, 1])
        gt = sb("gt", [P, E])

        xTs = sb("xTs", [P, 2, 2 * P])
        xk = sb("xk", [P, 2, 2, D])
        KT = sb("KT", [P, 2, H, 2 * P])
        QT = sb("QT", [P, 2, H, 2 * P])
        K = sb("K", [P, 2, 2, H * DK])
        A = sb("A", [P, 2, U, P])
        PT = sb("PT", [P, 2, U, P])
        V = sb("V", [P, 2, H * DV])
        G = sb("G", [P, 2 * P])
        Vp = sb("Vp", [P, 2, U, DV])
        silu = sb("silu", [P, 2, 2 * P])
        c2 = sb("c2", [P, 2, U])
        ss = sb("ss", [P, U])
        ssp = sb("ssp", [P, U])
        rr = sb("rr", [P, U])
        lnk = sb("lnk", [P, U])
        rk = sb("rk", [P, U])
        br = sb("br", [P, U])
        eb = sb("eb", [P, 2, H])
        bden = sb("bden", [P, U])
        beta = sb("beta", [P, U])
        eg = sb("eg", [P, 2 * P])
        lsg = sb("lsg", [P, 2 * P])
        sg = sb("sg", [P, 2 * P])
        junk = sb("junk", [P, U, P])
        ab = sb("ab", [64, 16, 16])
        xs = sb("xs", [64, 2, 16, 16])
        prod = sb("prod", [64, 240])
        xi = sb("xi", [P, 2, U, 16])
        m32 = sb("m32", [P, U, P])
        x16d = sb("x16d", [P, U, P])
        z32 = sb("z32", [P, U, 16])
        x32T = sb("x32T", [P, U, 32])
        x32 = sb("x32", [P, U, 32])
        xh = sb("xh", [P, U, 32])
        z64 = sb("z64", [P, U, 32])
        x64 = sb("x64", [64, U, 64])
        z128 = sb("z128", [64, U, 64])
        TT = sb("TT", [P, U, P])
        St = sb("St", [P, U, DV])
        tmp = sb("tmp", [P, U, DV])
        R = sb("R", [P, U, DV])
        dl = sb("dl", [P, U, DV])
        o = sb("o", [P, 2 * P])
        osq = sb("osq", [P, 2 * P])
        oln = sb("oln", [P, 2 * P])
        orms = sb("orms", [P, 2 * P])
        on = sb("on", [P, 2 * P])
        og = sb("og", [P, 2 * P])
        r1 = sb("r1", [P, 2, D])
        bst = sb("bst", [P, 2, 6])
        mv = sb("mv", [P, 2, 2])
        ve = sb("ve", [P, 2])
        vl = sb("vl", [P, 2])
        rstd = sb("rstd", [P, 2])
        x1 = sb("x1", [P, 2, B, TOPK, W])
        x1T = sb("x1T", [P, 2 * P])
        lg = sb("lg", [P, 2, E])
        v8 = sb("v8", [P, 2, 8])
        i8 = sb("i8", [P, 2, 8], U32)
        nm = sb("nm", [P, 2])
        e8 = sb("e8", [P, 2, 8])
        es = sb("es", [P, 2])
        idxf = sb("idxf", [P, 2, TOPK])
        oh = sb("oh", [P, 2, TOPK, E])
        M = sb("M", [P, 2, E], BF16)
        cc = sb("cc", [P, 2, E])
        carry = sb("carry", [P, B, E])
        pr = sb("pr", [P, 2, TOPK, E])
        cnt = sb("cnt", [P, 4])
        valid = sb("valid", [P, 4])
        sl = sb("sl", [P, 4])
        sd = sb("sd", [P, 4])
        sv = sb("sv", [P, 4])
        slf = sb("slf", [P, 4])
        rs = sb("rs", [P, 2])
        wv = sb("wv", [P, 2, TOPK])
        slot = sb("slot", [P, 2, 4], U32)
        gates = sb("gates", [P, 4 * NP])

        w13 = sb("w13", [P, 2, 2, F])
        w13h = sb("w13h", [P, 2, 2, F], F32R)
        w13l = sb("w13l", [P, 2, 2, F], F32R)
        w2s = sb("w2s", [FW, 2, FC, D])
        xe = sb("xe", [P, 2, CT, W])
        xeTh = sb("xeTh", [P, 2, CAP], F32R)
        xeTl = sb("xeTl", [P, 2, CAP], F32R)
        hs = sb("hs", [FW, 2, HALF])
        hb = sb("hb", [FW, 2, FC, CAP])
        ye = sb("ye", [P, 2, CT, D])
        filled_s = sb("filled_s", [P, CT])
        row_m = sb("row_m", [P, CT])
        row_k = sb("row_k", [P, CT])
        row_f = sb("row_f", [P, CT])
        row = sb("row", [P, 2, CT], U32)
        yc = sb("yc", [P, 2, TOPK, 2, D])
        x1c = sb("x1c", [P, 2, 2, D])
        ya = sb("ya", [P, 2, D])
        yb = sb("yb", [P, 2, D])
        yo = sb("yo", [P, 2, 2, D])
        rstd_c = sb("rstd_c", [P, 2])
        minus_half = sb("minus_half", [P, 2])

        w_ld = sem("w_ld")
        zero_st = sem("zero_st")
        consts_pool = sem("consts_pool")
        consts_dve = sem("consts_dve")
        wo_ready = sem("wo_ready")
        xT_ld = [sem("xT_ld0"), sem("xT_ld1")]
        xk_ld = [sem("xk_ld0"), sem("xk_ld1")]
        filled = sem("filled")
        freed_act = sem("freed_act")
        freed_dve = sem("freed_dve")
        ssp_ready = sem("ssp_ready")
        rk_ready = sem("rk_ready")
        br_ready = sem("br_ready")
        sg_ready = sem("sg_ready")
        gate_ready = sem("gate_ready")
        a_st = sem("a_st")
        ab_ld = sem("ab_ld")
        m32_ready = sem("m32_ready")
        solved = sem("solved")
        xi_st = sem("xi_st")
        xi_ld = sem("xi_ld")
        prep = sem("prep")
        lvl_mm = sem("lvl_mm")
        lvl_dve = sem("lvl_dve")
        lvl_act = sem("lvl_act")
        xh_ready = sem("xh_ready")
        x64_diag = sem("x64_diag")
        chain_mm = sem("chain_mm")
        r_ready = sem("r_ready")
        s_ready = sem("s_ready")
        d_ready = sem("d_ready")
        o_ready = sem("o_ready")
        osq_ready = sem("osq_ready")
        orms_ready = sem("orms_ready")
        og_ready = sem("og_ready")
        out_mm = sem("out_mm")
        r1_ready = sem("r1_ready")
        ve_ready = sem("ve_ready")
        rstd_ready = sem("rstd_ready")
        x1_ready = sem("x1_ready")
        x1_st = [sem("x1_st0"), sem("x1_st1")]
        x1T_ready = sem("x1T_ready")
        nm_ready = sem("nm_ready")
        e8_ready = sem("e8_ready")
        M_ready = sem("M_ready")
        slot_ready = sem("slot_ready")
        scat = [sem("scat0"), sem("scat1")]
        link_dve = sem("link_dve")
        link_act = sem("link_act")
        link_pool = sem("link_pool")
        ew_ld = [sem("ew_ld0"), sem("ew_ld1")]
        w2_ld = [sem("w2_ld0"), sem("w2_ld1")]
        wh_ready = sem("wh_ready")
        wl_ready = sem("wl_ready")
        xl_ready = sem("xl_ready")
        xe_ld = [sem("xe_ld0"), sem("xe_ld1")]
        xeT_mm = sem("xeT_mm")
        xeT_ready = sem("xeT_ready")
        h_mm = sem("h_mm")
        hs_ready = sem("hs_ready")
        h_ready = sem("h_ready")
        y_mm = sem("y_mm")
        ye_ready = sem("ye_ready")
        row_ready = sem("row_ready")
        y_back = [sem("y_back0"), sem("y_back1")]
        yc_ld = [sem("yc_ld0"), sem("yc_ld1")]
        x1c_ld = [sem("x1c_ld0"), sem("x1c_ld1")]
        cve_ready = sem("cve_ready")
        crstd_ready = sem("crstd_ready")
        yo_ready = sem("yo_ready")
        out_st = [sem("out_st0"), sem("out_st1")]

        block = ctx.enter_context(nc.Block())

        def phase_a(eng, step, link=None, per_body=0):
            step(-1, 1, True, False, False)
            step(0, 0, True, True, False)
            step(1, 1, True, True, True)
            with eng.Fori(0, (LOOP1 - LOOP0) // 2) as i:
                if link:
                    link.enter(i, per_body)
                step(LOOP0 + 2 * i, 0, True, True, True)
                step(LOOP0 + 2 * i + 1, 1, True, True, True)
            if link:
                link.leave((LOOP1 - LOOP0) // 2)
            step(NP - 2, 0, True, True, True)
            step(NP - 1, 1, False, True, True)
            step(NP, 0, False, False, True)

        @block.sync
        def _(sp):
            for dst, src in ((wk, Wk), (wvb, Wvb), (wg, Wg), (wq, Wq), (wo0, Wo), (gt, gateT)):
                sp.dma_start(dst[:], src[:, :]).then_inc(w_ld, 16)
            for h in range(H):
                sp.dma_start(nw[h * DV:(h + 1) * DV, :], norm_w.rearrange("(d o) -> d o", o=1)).then_inc(w_ld, 16)

            def load_xT(r, par):
                wait(sp, filled, 12 * (r - 2) + 10)
                sp.dma_start(xTs[:, par, :].rearrange("d (b p) -> d b p", b=B),
                             xT.rearrange("d (b t p) -> d b t p", b=B, p=P)[:, :, bass.ds(r, 1), :]
                             .rearrange("d b o p -> d b (o p)")).then_inc(xT_ld[par], 16)

            blocks = ad_d.rearrange("b (k x) -> (b k) x", x=BLK)[:, 0:512].rearrange("b (r c) -> b r c", c=32)[:, :, 0:16]

            def step(p, par, s1, main, outq):
                q = p + 1
                if isinstance(p, int) and p == -1:
                    load_xT(0, 0)
                    sp.wait_ge(consts_pool, 1)
                    for k in range(ROWS // P // 8):
                        sp.dma_start(xs_d[k * 8 * P:(k + 1) * 8 * P, :].rearrange("(p r) d -> p (r d)", p=P),
                                     zeros[:]).then_inc(zero_st, 16)
                if not (isinstance(p, int) and p + 2 > NP - 1):
                    load_xT(p + 2, par)
                if isinstance(p, int) and p == 0:
                    for y in y_d:
                        for k in range(RES // P // 8):
                            sp.dma_start(y[k * 8 * P:(k + 1) * 8 * P, :].rearrange("(p r) d -> p (r d)", p=P),
                                         zeros[:, 0:8 * D]).then_inc(zero_st, 16)
                if main:
                    wait(sp, r1_ready, p - 1)
                    sp.dma_start(xk[:, par], tile_of(x, p)).then_inc(xk_ld[par], 16)
                if s1:
                    sp.wait_ge(freed_dve, 4 * q + 2)
                    apart(sp)
                    for k in range(4):
                        sp.dma_start(ad_d[k::4, 0:1024].rearrange("u (r c) -> r u c", c=32),
                                     A[32 * k:32 * k + 32, 1 - par, :, 32 * k:32 * k + 32]).then_inc(a_st, 16)
                    sp.wait_ge(a_st, 64 * q + 64)
                    wait(sp, solved, q)
                    sp.dma_start(ab[:], blocks).then_inc(ab_ld, 16)
                if outq:
                    wait(sp, x1_ready, p)
                    sp.dma_start(tile_of(x1_d, p - 1), x1[:, 1 - par, :, 0, 0:D]).then_inc(x1_st[1 - par], 16)
                if s1:
                    sp.wait_ge(solved, q + 1)
                    sp.dma_start(xi_d.rearrange("t (b r) c -> b t (r c)", r=16),
                                 xs[:].rearrange("p t r c -> p t (r c)")).then_inc(xi_st, 16)
                    sp.wait_ge(xi_st, 16 * q + 16)
                    wait(sp, lvl_dve, 4 * (q - 1) + 2)
                    sp.dma_start(xi[:], xi_d.rearrange("t (u r) c -> r t u c", r=P)).then_inc(xi_ld, 16)

            phase_a(sp, step)

            xs_n = xs_d[0:ROWS, :].rearrange("(n p i) d -> n p i d", p=P, i=CT)

            def load_weights(n, e, par):
                wait(sp, wl_ready, 2 * (n - 1))
                for k, w in enumerate((w1, w3)):
                    sp.dma_start(w13[:, par, k, :], w[bass.ds(e, 1)].rearrange("o p f -> p (o f)")).then_inc(ew_ld[par], 16)
                wait(sp, y_mm, n - 1)
                sp.dma_start(w2s[:, par], w2[bass.ds(e, 1)].rearrange("o (c p) d -> p (o c) d", p=FW)).then_inc(w2_ld[par], 16)

            def load_slots(n, par):
                wait(sp, xeT_mm, n - 1)
                wait(sp, row_ready, n - 1)
                sp.dma_start(xe[:, par], xs_n[bass.ds(n, 1)].rearrange("o p i d -> p (o i) d")).then_inc(xe_ld[par], 16)

            def load_unit(n, e, par):
                load_weights(n, e, par)
                load_slots(n, par)

            def load_c(b, i, par):
                c = b * (NC // B) + i
                wait(sp, cve_ready, c - 1)
                sp.dma_start(x1c[:, par], x1_d.rearrange("(t p) d -> p t d", p=P)
                             [:, bass.ds(2 * c, 2), :]).then_inc(x1c_ld[par], 16)
                for k in range(TOPK):
                    sp.dma_start(yc[:, par, k], y_d[b][k * S:(k + 1) * S, :].rearrange("(t p) d -> p t d", p=P)
                                 [:, bass.ds(2 * i, 2), :]).then_inc(yc_ld[par], 16)

            def store_c(c, par):
                sp.wait_ge(yo_ready, c + 1)
                sp.dma_start(out.rearrange("(t p) d -> p t d", p=P)[:, bass.ds(2 * c, 2), :],
                             yo[:, par]).then_inc(out_st[par], 16)

            load_weights(0, 0, 0)
            load_weights(1, 1, 1)
            sp.wait_ge(scat[0], 64 * (NP // 2))
            sp.wait_ge(scat[1], 64 * (NP // 2))
            sp.wait_ge(x1_st[0], 16 * (NP // 2))
            sp.wait_ge(x1_st[1], 16 * (NP // 2))
            load_slots(0, 0)
            load_slots(1, 1)
            with sp.Fori(0, E // 2 - 1) as i:
                for par in range(2):
                    load_unit(2 * i + par + 2, 2 * i + par + 2, par)
            load_unit(E, 0, 0)
            load_unit(E + 1, 1, 1)
            sp.wait_ge(y_back[0], 16 * CT * E // 2)
            sp.wait_ge(y_back[1], 16 * CT * E // 2)
            load_c(0, 0, 0)
            load_c(0, 1, 1)
            load_unit(E + 2, 2, 0)
            load_c(0, 2, 0)
            load_unit(E + 3, 3, 1)
            store_c(0, 0)
            with sp.Fori(1, E // 2 - 1) as i:
                for par in range(2):
                    load_c(0, 2 * i + par + 1, 1 - par)
                    load_unit(E + 2 * i + par + 2, 2 * i + par + 2, par)
                    store_c(2 * i + par - 1, 1 - par)
            load_c(0, E - 1, 1)
            store_c(E - 3, 1)
            store_c(E - 2, 0)
            sp.wait_ge(y_back[0], 16 * CT * E)
            sp.wait_ge(y_back[1], 16 * CT * E)
            load_c(1, 0, 0)
            load_c(1, 1, 1)
            store_c(E - 1, 1)
            with sp.Fori(0, E // 2 - 1) as i:
                for par in range(2):
                    load_c(1, 2 * i + par + 2, par)
                    store_c(E + 2 * i + par, par)
            for par in range(2):
                store_c(NC - 2 + par, par)
            for par in range(2):
                sp.wait_ge(out_st[par], 16 * NC // 2)

        @block.tensor
        def _(pe):
            mm = nc.tensor.matmul
            fill_bank = [g % 3 for g in range(12)]
            ZB, WB, CB, OB, MB = 3, 4, 5, 6, 7

            pe.wait_ge(w_ld, W_LOADS)
            pe.wait_ge(consts_pool, 5)

            def act_free(q, n):
                wait(pe, freed_act, 8 * q + n)

            def dve_free(q, n):
                wait(pe, freed_dve, 4 * q + n)

            def kt(q, par, g):
                if g == 0:
                    pe.wait_ge(xT_ld[par], 8 * q + 16 - 8 * par)
                    act_free(q - 1, 8)
                else:
                    dve_free(q - 1, 3)
                for k in range(2):
                    h = 2 * g + k
                    last = mm(ps[:, fill_bank[g], 256 * k:256 * k + 256], wk[:, DK * h:DK * h + DK], xTs[:, par, :],
                              start=True, stop=True)
                last.then_inc(filled, 1)

            def k_tok(q, par, j):
                if j == 0:
                    dve_free(q - 1, 4)
                else:
                    act_free(q, 1)
                mm(ps[:, fill_bank[2 + j], :], xTs[:, par, P * j:P * j + P], wk[:, :],
                   start=True, stop=True).then_inc(filled, 1)

            def vb(q, par):
                act_free(q, 2)
                for j in range(2):
                    last = mm(ps[:, fill_bank[4], VW * j:VW * j + VW], xTs[:, par, P * j:P * j + P], wvb[:],
                              start=True, stop=True)
                last.then_inc(filled, 1)

            def kk(q, par, j):
                act_free(q, 3 + j)
                for h in range(H):
                    kc = KT[:, par, h, P * j:P * j + P]
                    last = mm(ps[:, fill_bank[5 + j], P * h:P * h + P], kc, kc, start=True, stop=True)
                last.then_inc(filled, 1)

            def gate_t(q, par):
                act_free(q, 5)
                mm(ps[:, fill_bank[7], 0:2 * P], wg[:], xTs[:, par, :], start=True, stop=True).then_inc(filled, 1)

            def qt(q, par, g):
                dve_free(q, 1 + g)
                for k in range(2):
                    h = 2 * g + k
                    last = mm(ps[:, fill_bank[8 + g], 256 * k:256 * k + 256], wq[:, DK * h:DK * h + DK], xTs[:, par, :],
                              start=True, stop=True)
                last.then_inc(filled, 1)

            def kq(q, par, j):
                if j == 0:
                    act_free(q, 8)
                for h in range(H):
                    last = mm(ps[:, fill_bank[10 + j], P * h:P * h + P], KT[:, par, h, P * j:P * j + P],
                              QT[:, par, h, P * j:P * j + P], start=True, stop=True)
                last.then_inc(filled, 1)

            def z_32(p):
                pe.wait_ge(m32_ready, p + 1)
                pe.wait_ge(xi_ld, 16 * p + 16)
                wait(pe, lvl_act, 3 * p - 1)
                for u in range(U):
                    last = mm(ps[:, ZB, 16 * u:16 * u + 16], m32[:, u, :], xi[:, 1, u, :], start=True, stop=True)
                last.then_inc(lvl_mm, 1)

            def w_32(p):
                pe.wait_ge(prep, p + 1)
                pe.wait_ge(lvl_dve, 4 * p + 1)
                wait(pe, lvl_act, 3 * p)
                for u in range(U):
                    last = mm(ps[:, WB, 16 * u:16 * u + 16], x16d[:, u, :], z32[:, u, :], start=True, stop=True)
                last.then_inc(lvl_mm, 1)

            def z_64(p, par):
                pe.wait_ge(lvl_dve, 4 * p + 2)
                pe.wait_ge(xh_ready, p + 1)
                apart(pe)
                for u in range(U):
                    for m in range(2):
                        s = slice(64 * m, 64 * m + 64)
                        last = mm(ps[s, ZB, 32 * u:32 * u + 32], A[s, par, u, s], xh[s, u, :], start=True, stop=True)
                last.then_inc(lvl_mm, 1)

            def w_64(p):
                pe.wait_ge(lvl_dve, 4 * p + 3)
                apart(pe)
                for u in range(U):
                    for m in range(2):
                        s = slice(64 * m, 64 * m + 64)
                        last = mm(ps[64 * m:64 * m + 32, WB, 32 * u:32 * u + 32], x32[s, u, :], z64[s, u, :],
                                  start=True, stop=True)
                last.then_inc(lvl_mm, 1)

            def z_128(p, par):
                pe.wait_ge(lvl_dve, 4 * p + 4)
                pe.wait_ge(lvl_act, 3 * p + 1)
                apart(pe)
                for u in range(U):
                    last = mm(ps[0:64, ZB, 64 * u:64 * u + 64], A[64:128, par, u, 0:64], TT[64:128, u, 64:128],
                              start=True, stop=True)
                last.then_inc(lvl_mm, 1)

            def w_128(p):
                pe.wait_ge(lvl_act, 3 * p + 2)
                pe.wait_ge(x64_diag, p + 1)
                apart(pe)
                for u in range(U):
                    last = mm(ps[0:64, WB, 64 * u:64 * u + 64], x64[:, u, :], z128[:, u, :], start=True, stop=True)
                last.then_inc(lvl_mm, 1)

            def ks(p, par):
                if isinstance(p, int) and p == 0:
                    pe.wait_ge(consts_dve, 1)
                else:
                    pe.wait_ge(s_ready, p)
                for u in range(U):
                    j, h = u // H, u % H
                    last = mm(ps[:, CB, DV * u:DV * u + DV], KT[:, par, h, P * j:P * j + P], St[:, u, :],
                              start=True, stop=True)
                last.then_inc(chain_mm, 1)

            def qs(p, par):
                wait(pe, o_ready, p)
                for u in range(U):
                    j, h = u // H, u % H
                    mm(ps[DV * h:DV * h + DV, OB, P * j:P * j + P], St[:, u, :], QT[:, par, h, P * j:P * j + P],
                       start=(j == 0), stop=False, skip_group_check=True)

            def t_r(p):
                pe.wait_ge(r_ready, p + 1)
                pe.wait_ge(lvl_act, 3 * p + 3)
                for u in range(U):
                    last = mm(ps[:, CB, 256 + DV * u:256 + DV * u + DV], TT[:, u, :], R[:, u, :], start=True, stop=True)
                last.then_inc(chain_mm, 1)

            def k_d(p, par):
                pe.wait_ge(d_ready, p + 1)
                for u in range(U):
                    j, h = u // H, u % H
                    last = mm(ps[:, CB, DV * u:DV * u + DV], K[:, par, j, DK * h:DK * h + DK], dl[:, u, :],
                              start=True, stop=True)
                last.then_inc(chain_mm, 1)

            def p_d(p, par):
                pe.wait_ge(freed_dve, 4 * p + 4)
                for u in range(U):
                    j, h = u // H, u % H
                    last = mm(ps[DV * h:DV * h + DV, OB, P * j:P * j + P], dl[:, u, :], PT[:, par, u, :],
                              start=False, stop=True, skip_group_check=True)
                last.then_inc(chain_mm, 1)

            def o_sums(q):
                pe.wait_ge(osq_ready, q + 1)
                wait(pe, slot_ready, q)
                mm(ps[:, MB, 0:2 * P], heads[:], osq[:], start=True, stop=True).then_inc(out_mm, 1)

            def o_proj(q):
                pe.wait_ge(og_ready, q + 1)
                pe.wait_ge(wo_ready, 1)
                for j in range(2):
                    last = mm(ps[:, MB, P * j:P * j + P], og[:, P * j:P * j + P], wo[:], start=True, stop=True)
                last.then_inc(out_mm, 1)

            def x1_t(q, par):
                pe.wait_ge(x1_ready, q + 1)
                for j in range(2):
                    last = nc.tensor.transpose(ps[:, MB, P * j:P * j + P], x1[:, par, j, 0, 0:D], ident[:])
                last.then_inc(out_mm, 1)

            def logits(q):
                pe.wait_ge(x1T_ready, q + 1)
                for j in range(2):
                    last = mm(ps[:, MB, E * j:E * j + E], x1T[:, P * j:P * j + P], gt[:], start=True, stop=True)
                last.then_inc(out_mm, 1)

            def cum(q):
                pe.wait_ge(M_ready, q + 1)
                for j in range(B):
                    mm(ps[:, MB, E * j:E * j + E], tri[:], M[:, j, :], start=True, stop=True)
                for j in range(B):
                    last = mm(ps[:, MB, E * (B + j):E * (B + j) + E], ones[:], M[:, j, :], start=True, stop=True)
                last.then_inc(out_mm, 1)

            def step(p, par, s1, main, outq):
                q, npar, o_ = p + 1, 1 - par, p - 1
                if outq:
                    ks(o_, npar)
                    qs(o_, npar)
                if s1:
                    kt(q, npar, 0)
                    kt(q, npar, 1)
                if outq:
                    t_r(o_)
                if s1:
                    k_tok(q, npar, 0)
                if outq:
                    k_d(o_, npar)
                    p_d(o_, npar)
                if s1:
                    k_tok(q, npar, 1)
                    vb(q, npar)
                    kk(q, npar, 0)
                if main:
                    z_32(p)
                if s1:
                    kk(q, npar, 1)
                if outq:
                    o_sums(o_)
                if s1:
                    gate_t(q, npar)
                if main:
                    w_32(p)
                if s1:
                    qt(q, npar, 0)
                if main:
                    z_64(p, par)
                if outq:
                    o_proj(o_)
                if s1:
                    qt(q, npar, 1)
                if main:
                    w_64(p)
                if s1:
                    kq(q, npar, 0)
                if main:
                    z_128(p, par)
                if outq:
                    x1_t(o_, npar)
                    logits(o_)
                if s1:
                    kq(q, npar, 1)
                if main:
                    w_128(p)
                if outq:
                    cum(o_)

            phase_a(pe, step)

            def flip(n, par):
                pe.wait_ge(xe_ld[par], 8 * n + 16 - 8 * par)
                wait(pe, xl_ready, 2 * n)
                for i in range(CT):
                    last = nc.tensor.transpose(ps[:, i // 4, P * (i % 4):P * (i % 4) + P], xe[:, par, i, 0:D], ident[:])
                last.then_inc(xeT_mm, 1)

            def hidden(n, par):
                pe.wait_ge(wl_ready, 2 * n + 2)
                pe.wait_ge(xl_ready, 2 * n + 2)
                for c in range(FC):
                    for g in range(2):
                        s = 2 * c + g
                        wait(pe, h_ready, 8 * n + s - 1)
                        cols = slice(HALF * g, HALF * g + HALF)
                        for k in range(2):
                            for t, (wp, xp) in enumerate(((w13h, xeTh), (w13h, xeTl), (w13l, xeTh))):
                                last = mm(ps[0:FW, 2 + 2 * k + g, 0:HALF], wp[:, par, k, FW * c:FW * c + FW],
                                          xp[:, par, cols], start=(t == 0), stop=(t == 2))
                        last.then_inc(h_mm, 1)

            def down(n, par):
                pe.wait_ge(h_ready, 8 * n + 8)
                pe.wait_ge(w2_ld[par], 8 * n + 16 - 8 * par)
                wait(pe, ye_ready, n)
                for i in range(CT):
                    for c in range(FC):
                        last = mm(ps[:, 6 + i // 4, P * (i % 4):P * (i % 4) + P], hb[:, par, c, P * i:P * i + P],
                                  w2s[:, par, c, :], start=(c == 0), stop=(c == FC - 1))
                last.then_inc(y_mm, 1)

            pe.wait_ge(slot_ready, NP)
            def unit(n, par):
                hidden(n, par)
                flip(n + 1, 1 - par)
                down(n, par)

            flip(0, 0)
            for par in range(2):
                unit(par, par)
            with pe.Fori(1, B * E // 2 - 1) as i:
                for par in range(2):
                    unit(2 * i + par, par)
            hidden(B * E - 2, 0)
            flip(B * E - 1, 1)
            down(B * E - 2, 0)
            hidden(B * E - 1, 1)
            down(B * E - 1, 1)

        @block.scalar
        def _(act):
            link = Link(act, link_act)
            af = nc.scalar.activation
            nc.scalar.preload_act_table_set("natural_log_exp_and_others")
            fill_bank = [g % 3 for g in range(12)]
            ZB, WB, CB, OB, MB = 3, 4, 5, 6, 7

            def rsqrt(out_ap, ln_ap, in_ap):
                link(af(ln_ap, in_ap, ACT.Ln))
                return af(out_ap, ln_ap, ACT.Exp, scale=-0.5)

            def k_out(q, par, j):
                act.wait_ge(filled, 12 * q + 3 + j)
                if j == 0:
                    wait(act, chain_mm, 4 * (q - 2) + 3)
                    wait(act, br_ready, q)
                af(K[:, par, j, :], ps[:, fill_bank[2 + j], :], ACT.Copy)
                for h in range(H):
                    last = af(junk[:, H * j + h, :], ps[:, fill_bank[2 + j], DK * h:DK * h + DK], ACT.Square,
                              accum_out=ss[:, H * j + h:H * j + h + 1])
                last.then_inc(freed_act, 1)

            def vb_out(q):
                act.wait_ge(filled, 12 * q + 5)
                wait(act, gate_ready, 2 * q)
                both = ps[:, fill_bank[4], 0:2 * VW].rearrange("p (j c) -> p j c", j=2)
                af(eb[:], both[:, :, H * DV:], ACT.Exp, scale=-1.0)
                af(V[:], both[:, :, 0:H * DV], ACT.Copy).then_inc(freed_act, 1)

            def g_out(q):
                act.wait_ge(filled, 12 * q + 8)
                af(G[:], ps[:, fill_bank[7], 0:2 * P], ACT.Copy)
                ins = af(eg[:], ps[:, fill_bank[7], 0:2 * P], ACT.Exp, scale=-1.0)
                ins.then_inc(freed_act, 1)
                act.wait_ge(freed_act, 8 * q + 6)
                link(af(lsg[:], eg[:], ACT.Ln, bias=one[:]))
                af(sg[:], lsg[:], ACT.Exp, scale=-1.0).then_inc(sg_ready, 1)

            def q_out(q, par, g):
                act.wait_ge(filled, 12 * q + 9 + g)
                af(QT[:, par, 2 * g:2 * g + 2, :], ps[:, fill_bank[8 + g], :].rearrange("p (h t) -> p h t", h=2),
                   ACT.Copy, scale=SCALE).then_inc(freed_act, 1)

            def delta(p):
                act.wait_ge(chain_mm, 4 * p + 2)
                af(dl[:].rearrange("p u d -> p (u d)"), ps[:, CB, 256:512], ACT.Copy).then_inc(d_ready, 1)

            def o_out(p, par):
                act.wait_ge(chain_mm, 4 * p + 4)
                wait(act, og_ready, p)
                af(o[:], ps[:, OB, 0:2 * P], ACT.Copy).then_inc(o_ready, 1)

            def kt_out(q, par, g):
                act.wait_ge(filled, 12 * q + g + 1)
                if g == 0:
                    wait(act, chain_mm, 4 * (q - 2) + 1)
                af(KT[:, par, 2 * g:2 * g + 2, :], ps[:, fill_bank[g], :].rearrange("p (h t) -> p h t", h=2),
                   ACT.Copy).then_inc(freed_act, 1)

            def k_norm(q):
                act.wait_ge(ssp_ready, q + 1)
                rsqrt(rk[:], lnk[:], ssp[:]).then_inc(rk_ready, 1)

            def o_norm(p):
                act.wait_ge(out_mm, 5 * p + 1)
                link(af(oln[:], ps[:, MB, 0:2 * P], ACT.Ln, scale=1.0 / DV, bias=eps[:]))
                af(orms[:], oln[:], ACT.Exp, scale=-0.5).then_inc(orms_ready, 1)

            def t_diag(p):
                act.wait_ge(lvl_dve, 4 * p + 2)
                for m in range(2):
                    s = slice(64 * m + 32, 64 * m + 64)
                    last = af(xh[s], x32T[s], ACT.Copy)
                last.then_inc(xh_ready, 1)
                wait(act, chain_mm, 4 * (p - 1) + 2)
                for k in range(4):
                    s = slice(32 * k, 32 * k + 32)
                    last = af(TT[s, :, 32 * k:32 * k + 32], x32T[s, :, :], ACT.Copy)
                last.then_inc(lvl_act, 1)

            def x64_out(p):
                act.wait_ge(lvl_dve, 4 * p + 2)
                wait(act, lvl_mm, 6 * p)
                for k in range(2):
                    s = slice(32 * k, 32 * k + 32)
                    last = af(x64[s, :, 32 * k:32 * k + 32], x32[s, :, :], ACT.Copy)
                last.then_inc(x64_diag, 1)

            def z128_out(p):
                act.wait_ge(lvl_mm, 6 * p + 5)
                af(z128[:], ps[0:64, ZB, :].rearrange("p (u c) -> p u c", u=U), ACT.Copy).then_inc(lvl_act, 1)

            def t_out(p):
                act.wait_ge(lvl_mm, 6 * p + 6)
                af(TT[0:64, :, 64:128], ps[0:64, WB, :].rearrange("p (u c) -> p u c", u=U), ACT.Copy,
                   scale=-1.0).then_inc(lvl_act, 1)

            def x1_rstd(p):
                act.wait_ge(ve_ready, p + 1)
                rsqrt(rstd[:], vl[:], ve[:]).then_inc(rstd_ready, 1)

            def x1T_out(p):
                act.wait_ge(out_mm, 5 * p + 3)
                af(x1T[:], ps[:, MB, 0:256], ACT.Copy).then_inc(x1T_ready, 1)

            def softmax(p):
                act.wait_ge(nm_ready, p + 1)
                for j in range(2):
                    last = af(e8[:, j, :], v8[:, j, :], ACT.Exp, bias=nm[:, j:j + 1], accum_out=es[:, j:j + 1])
                last.then_inc(e8_ready, 1)

            def step(p, par, s1, main, outq):
                q, npar, o_ = p + 1, 1 - par, p - 1
                if s1:
                    kt_out(q, npar, 0)
                    kt_out(q, npar, 1)
                if outq:
                    delta(o_)
                if s1:
                    k_out(q, npar, 0)
                    k_out(q, npar, 1)
                    vb_out(q)
                if outq:
                    o_out(o_, npar)
                if s1:
                    k_norm(q)
                if outq:
                    o_norm(o_)
                if s1:
                    g_out(q)
                if main:
                    t_diag(p)
                    x64_out(p)
                if s1:
                    q_out(q, npar, 0)
                    q_out(q, npar, 1)
                if outq:
                    x1_rstd(o_)
                    x1T_out(o_)
                if main:
                    z128_out(p)
                    t_out(p)
                if outq:
                    softmax(o_)

            phase_a(act, step, link, ACT_LINKS)

            def turn(n, par):
                act.wait_ge(xeT_mm, n + 1)
                wait(act, h_mm, 8 * (n - 1))
                af(xeTh[:, par, 0:512], ps[:, 0, :], ACT.Copy).then_inc(xeT_ready, 1)
                af(xeTh[:, par, 512:CAP], ps[:, 1, 0:CAP - 512], ACT.Copy).then_inc(xeT_ready, 1)

            def gate(n, s):
                act.wait_ge(h_mm, 8 * n + s + 1)
                wait(act, h_ready, 8 * n + s - 1)
                af(hs[:, s % 2, :], ps[0:FW, 2 + s % 2, 0:HALF], ACT.Silu).then_inc(hs_ready, 1)

            def y_out(n, par):
                act.wait_ge(y_mm, n + 1)
                wait(act, y_back[par], CT * (8 * n - 8 * par))
                af(ye[:, par, 0:4, :], ps[:, 6, :].rearrange("p (i d) -> p i d", i=4), ACT.Copy)
                af(ye[:, par, 4, :], ps[:, 7, 0:P], ACT.Copy).then_inc(ye_ready, 1)

            def w_high(n, par, k):
                act.wait_ge(ew_ld[par], 2 * (8 * n + 16 - 8 * par))
                wait(act, h_mm, 8 * (n - 1))
                af(w13h[:, par, k, :], w13[:, par, k, :], ACT.Copy).then_inc(wh_ready, 1)

            def gates_of(n, par, ahead):
                for s in range(8):
                    gate(n, s)
                    if ahead and s in (2, 5):
                        w_high(n + 1, 1 - par, s // 3)

            w_high(0, 0, 0)
            w_high(0, 0, 1)
            turn(0, 0)
            for n in range(2):
                gates_of(n, n, True)
                turn(n + 1, 1 - n)
                y_out(n, n)
            with act.Fori(1, B * E // 2 - 1) as i:
                for par in range(2):
                    n = 2 * i + par
                    gates_of(n, par, True)
                    turn(n + 1, 1 - par)
                    y_out(n, par)
            gates_of(B * E - 2, 0, True)
            turn(B * E - 1, 1)
            y_out(B * E - 2, 0)
            gates_of(B * E - 1, 1, False)
            y_out(B * E - 1, 1)

        @block.vector
        def _(dve):
            link = Link(dve, link_dve)
            v = nc.vector
            fill_bank = [g % 3 for g in range(12)]
            ZB, WB, CB, OB, MB = 3, 4, 5, 6, 7

            for t in (TT, x64, xh, z64, St, carry):
                v.memset(t[:], 0.0)
            v.memset(eps[:], EPS)
            v.memset(one[:], 1.0)
            v.memset(minus_half[:], -0.5)
            dve.wait_ge(consts_pool, 6)
            link(v.tensor_scalar(pbit[:], pidx[:], 16, None, ALU.bitwise_and))
            link(v.tensor_copy(pcol[:], pbit[:]))
            link(v.tensor_scalar(high[:], pcol[:], 1.0 / 16, None, ALU.mult))
            link(v.tensor_scalar(low[:], high[:], -1.0, 1.0, ALU.mult, ALU.add))
            link(v.tensor_copy(pcol[:], pidx[:]))
            for k in range(4):
                link(v.tensor_scalar(spare[:, k:k + 1], pcol[:], float(ROWS + P * k), None, ALU.add))
                link(v.tensor_scalar(shift[:, k:k + 1], spare[:, k:k + 1], -1.0, float(k // TOPK * E * CAP - 1),
                                     ALU.mult, ALU.add))
            for k in range(2 * CT):
                v.tensor_scalar(spare_y[:, k // CT, k % CT:k % CT + 1], pcol[:], float(RES + P * k), None, ALU.add)
            v.tensor_copy(tri[:], upper[:])
            link(v.memset(ones[:], 1.0))
            v.tensor_copy(M[:, 0, :], tri[:, 0:E]).then_inc(consts_dve, 1)
            dve.wait_ge(w_ld, W_LOADS)
            v.tensor_scalar(wo[:], wo0[:], nw[:], None, ALU.mult).then_inc(wo_ready, 1)

            def spread(p):
                dve.wait_ge(xi_ld, 16 * p + 16)
                v.tensor_tensor(x16d[:].rearrange("p u (b c) -> p u b c", c=16), bc(xi[:, 0], 2, 8),
                                bc(mask16[:].rearrange("p (b c) -> p b c", c=16), 1, U), ALU.mult)
                v.tensor_scalar(x32T[:, :, 0:16], xi[:, 1], low[:], None, ALU.mult).then_inc(prep, 1)

            def factors(q, par):
                dve.wait_ge(freed_act, 8 * q + 4)
                v.tensor_scalar(ssp[:], ss[:], 1e-12, None, ALU.add).then_inc(ssp_ready, 1)
                dve.wait_ge(ssp_ready, q + 1)
                v.reciprocal(rr[:], ssp[:])
                dve.wait_ge(freed_act, 8 * q + 5)
                link(v.tensor_scalar(bden[:], eb[:].rearrange("p j h -> p (j h)"), 1.0, None, ALU.add))
                link(v.reciprocal(beta[:], bden[:]))
                v.tensor_tensor(c2[:, par, :], beta[:], rr[:], ALU.mult)
                dve.wait_ge(rk_ready, q + 1)
                v.tensor_tensor(br[:], beta[:], rk[:], ALU.mult).then_inc(br_ready, 1)
                dve.wait_ge(br_ready, q + 1)

            def z32_out(p):
                dve.wait_ge(lvl_mm, 6 * p + 1)
                v.tensor_copy(z32[:], ps[:, ZB, 0:128].rearrange("p (u c) -> p u c", u=U)).then_inc(lvl_dve, 1)

            def x32_out(p):
                dve.wait_ge(lvl_mm, 6 * p + 2)
                link(v.scalar_tensor_tensor(out=x32T[:, :, 16:32], in0=xi[:, 1], scalar=high[:],
                                            in1=ps[:, WB, 0:128].rearrange("p (u c) -> p u c", u=U),
                                            op0=ALU.mult, op1=ALU.subtract))
                v.transpose(x32[:].rearrange("p u c -> p (u c)"),
                            x32T[:].rearrange("p u c -> p (u c)")).then_inc(lvl_dve, 1)

            def z64_out(p):
                dve.wait_ge(lvl_mm, 6 * p + 3)
                for m in range(2):
                    s = slice(64 * m, 64 * m + 32)
                    last = v.tensor_copy(z64[s], ps[s, ZB, 0:256].rearrange("p (u c) -> p u c", u=U))
                last.then_inc(lvl_dve, 1)

            def t64_out(p):
                dve.wait_ge(lvl_mm, 6 * p + 4)
                dve.wait_ge(lvl_act, 3 * p + 1)
                for m in (1, 0):
                    s = slice(64 * m, 64 * m + 32)
                    last = v.tensor_scalar(TT[s, :, 64 * m + 32:64 * m + 64],
                                           ps[s, WB, 0:256].rearrange("p (u c) -> p u c", u=U), -1.0, None, ALU.mult)
                link(last)
                for u in range(U):
                    last = v.transpose(x64[32:64, u, 0:32], TT[0:32, u, 32:64])
                last.then_inc(lvl_dve, 1)

            def residual(p, par):
                dve.wait_ge(out_mm, 5 * p + 2)
                dve.wait_ge(xk_ld[par], 8 * p + 16 - 8 * par)
                v.tensor_tensor(r1[:], ps[:, MB, 0:256].rearrange("p (j d) -> p j d", j=2), xk[:, par],
                                ALU.add).then_inc(r1_ready, 1)
                dve.wait_ge(r1_ready, p + 1)
                moments(r1).then_inc(ve_ready, 1)

            def x1_out(p, par):
                dve.wait_ge(rstd_ready, p + 1)
                wait(dve, x1_st[par], 8 * p - 8 * par)
                wait(dve, scat[par], 4 * (8 * p - 8 * par))
                v.tensor_copy(x1[:, par, :, :, D], ids[:, bass.ds(p, 1)].rearrange("p o j k -> p (o j) k"))
                for j in range(2):
                    last = v.tensor_scalar(x1[:, par, j, :, 0:D], bc(r1[:, j, :], 1, TOPK), mv[:, j, 0:1],
                                           rstd[:, j:j + 1], ALU.subtract, ALU.mult)
                last.then_inc(x1_ready, 1)

            def step(p, par, s1, main, outq):
                q, npar, o_ = p + 1, 1 - par, p - 1
                if outq:
                    chain_r(o_, npar)
                    chain_s(o_)
                if s1:
                    factors(q, npar)
                if main:
                    spread(p)
                    z32_out(p)
                if s1:
                    lower(q, npar, 0)
                    lower(q, npar, 1)
                if main:
                    x32_out(p)
                    z64_out(p)
                if outq:
                    residual(o_, npar)
                if main:
                    t64_out(p)
                if s1:
                    masked_q(q, npar, 0)
                if outq:
                    x1_out(o_, npar)
                    route(o_)
                if s1:
                    masked_q(q, npar, 1)
                if outq:
                    place(o_, npar)

            def moments(src):
                for j in range(2):
                    last = v.bn_stats(bst[:, j, :], src[:, j, :])
                link(last)
                apart(dve)
                for j in range(2):
                    last = v.bn_aggr(mv[:, j, :], bst[:, j, :])
                link(last)
                return v.tensor_scalar(ve[:], mv[:, :, 1], EPS, None, ALU.add)

            def lower(q, par, j):
                dve.wait_ge(filled, 12 * q + 6 + j)
                if j == 0:
                    wait(dve, a_st, 64 * q)
                    wait(dve, m32_ready, q - 1)
                for h in range(H):
                    last = v.scalar_tensor_tensor(out=A[:, par, H * j + h, :], in0=ps[:, fill_bank[5 + j], P * h:P * h + P],
                                                  scalar=c2[:, par, H * j + h:H * j + h + 1], in1=strict[:],
                                                  op0=ALU.mult, op1=ALU.mult)
                last.then_inc(freed_dve, 1)

            def masked_q(q, par, j):
                dve.wait_ge(filled, 12 * q + 11 + j)
                if j == 0:
                    wait(dve, chain_mm, 4 * (q - 2) + 4)
                v.tensor_tensor(PT[:, par, H * j:H * j + H, :],
                                ps[:, fill_bank[10 + j], :].rearrange("p (h t) -> p h t", h=H),
                                bc(upper[:], 1, H), ALU.mult).then_inc(freed_dve, 1)

            def chain_r(p, par):
                dve.wait_ge(chain_mm, 4 * p + 1)
                link(v.tensor_tensor(tmp[:], ps[:, CB, 0:256].rearrange("p (u d) -> p u d", u=U),
                                     bc(c2[:, par, :], 2, DV), ALU.mult))
                dve.wait_ge(gate_ready, 2 * p + 2)
                v.tensor_tensor(R[:], Vp[:, par], tmp[:], ALU.subtract).then_inc(r_ready, 1)

            def chain_s(p):
                dve.wait_ge(chain_mm, 4 * p + 3)
                v.tensor_tensor(St[:], St[:], ps[:, CB, 0:256].rearrange("p (u d) -> p u d", u=U),
                                ALU.add).then_inc(s_ready, 1)

            def route(q):
                dve.wait_ge(out_mm, 5 * q + 4)
                link(v.tensor_copy(lg[:], ps[:, MB, 0:2 * E].rearrange("p (j e) -> p j e", j=2)))
                apart(dve)
                for j in range(2):
                    last = v.max(v8[:, j, :], lg[:, j, :])
                link(last)
                apart(dve)
                for j in range(2):
                    last = v.max_index(i8[:, j, :], v8[:, j, :], lg[:, j, :])
                v.tensor_scalar(nm[:], v8[:, :, 0], -1.0, None, ALU.mult).then_inc(nm_ready, 1)
                dve.wait_ge(nm_ready, q + 1)
                link(v.tensor_copy(idxf[:], i8[:, :, 0:TOPK]))
                link(v.tensor_tensor(oh[:].rearrange("p j k e -> p (j k) e"), bc(iota8[:], 1, 4),
                                     bc(idxf[:].rearrange("p j k -> p (j k)"), 2, E), ALU.is_equal))
                v.tensor_tensor(M[:], oh[:, :, 0, :], oh[:, :, 1, :], ALU.add).then_inc(M_ready, 1)

            def place(q, par):
                dve.wait_ge(out_mm, 5 * q + 5)
                link(v.tensor_tensor(cc[:], ps[:, MB, 0:B * E].rearrange("p (j e) -> p j e", j=B), carry[:], ALU.add))
                v.tensor_tensor(carry[:], ps[:, MB, B * E:2 * B * E].rearrange("p (j e) -> p j e", j=B), carry[:], ALU.add)
                for j in range(2):
                    last = v.tensor_tensor(pr[:, j], oh[:, j], bc(cc[:, j, :], 1, TOPK), ALU.mult)
                link(last)
                link(v.tensor_reduce(cnt[:], pr[:].rearrange("p j k e -> p (j k) e"), AX.X, ALU.add))
                v.tensor_scalar(valid[:], cnt[:], float(CAP), None, ALU.is_le)
                link(v.scalar_tensor_tensor(out=sl[:], in0=idxf[:].rearrange("p j k -> p (j k)"), scalar=float(CAP),
                                            in1=cnt[:], op0=ALU.mult, op1=ALU.add))
                link(v.tensor_tensor(sd[:], sl[:], shift[:], ALU.add))
                link(v.tensor_tensor(sv[:], sd[:], valid[:], ALU.mult))
                link(v.tensor_tensor(slf[:], sv[:], spare[:], ALU.add))
                wait(dve, scat[par], 4 * (8 * q - 8 * par))
                v.tensor_copy(slot[:, par, :], slf[:])
                dve.wait_ge(e8_ready, q + 1)
                link(v.reciprocal(rs[:], es[:]))
                link(v.tensor_tensor(wv[:], e8[:, :, 0:TOPK], bc(rs[:], 2, TOPK), ALU.mult))
                v.tensor_tensor(gates[:, bass.ds(4 * q, 4)], wv[:].rearrange("p j k -> p (j k)"), valid[:],
                                ALU.mult).then_inc(slot_ready, 1)

            phase_a(dve, step, link, DVE_LINKS)

            def gated(n, par, s):
                dve.wait_ge(hs_ready, 8 * n + s + 1)
                if s == 0:
                    wait(dve, y_mm, n - 1)
                c, g = s // 2, s % 2
                v.tensor_tensor(hb[:, par, c, HALF * g:HALF * g + HALF], ps[0:FW, 4 + g, 0:HALF], hs[:, g, :],
                                ALU.mult).then_inc(h_ready, 1)

            def rows(n, par):
                dve.wait_ge(xe_ld[par], 8 * n + 16 - 8 * par)
                v.tensor_scalar(filled_s[:], xe[:, par, :, D], 0.0, None, ALU.is_gt)
                link(v.scalar_tensor_tensor(out=row_m[:], in0=xe[:, par, :, D], scalar=-1.0, in1=spare_y[:, par],
                                            op0=ALU.add, op1=ALU.subtract))
                link(v.tensor_tensor(row_k[:], row_m[:], filled_s[:], ALU.mult))
                link(v.tensor_tensor(row_f[:], row_k[:], spare_y[:, par], ALU.add))
                wait(dve, y_back[par], CT * (8 * n - 8 * par))
                v.tensor_copy(row[:, par, :], row_f[:]).then_inc(row_ready, 1)

            def w_low(n, par, k):
                dve.wait_ge(wh_ready, 2 * n + k + 1)
                wait(dve, h_mm, 8 * (n - 1))
                v.tensor_tensor(w13l[:, par, k, :], w13[:, par, k, :], w13h[:, par, k, :].bitcast(F32),
                                ALU.subtract).then_inc(wl_ready, 1)

            def x_low(n, par):
                for k, cols in enumerate((slice(0, 512), slice(512, CAP))):
                    dve.wait_ge(xeT_ready, 2 * n + k + 1)
                    v.tensor_tensor(xeTl[:, par, cols], ps[:, k, 0:cols.stop - cols.start],
                                    xeTh[:, par, cols].bitcast(F32), ALU.subtract).then_inc(xl_ready, 1)

            def unit(n, par, ahead=True):
                rows(n, par)
                for s in range(8):
                    gated(n, par, s)
                    if ahead and s in (2, 5):
                        w_low(n + 1, 1 - par, s // 3)
                if ahead:
                    x_low(n + 1, 1 - par)

            def combine(b, i, par):
                c = b * (NC // B) + i
                dve.wait_ge(yc_ld[par], 2 * (8 * c + 16 - 8 * par))
                dve.wait_ge(x1c_ld[par], 8 * c + 16 - 8 * par)
                for j in range(2):
                    last = v.scalar_tensor_tensor(out=ya[:, j, :], in0=yc[:, par, 0, j, :],
                                                  scalar=gates[:, bass.ds(8 * i + 4 * j + 2 * b, 1)],
                                                  in1=x1c[:, par, j, :], op0=ALU.mult, op1=ALU.add)
                link(last)
                for j in range(2):
                    last = v.scalar_tensor_tensor(out=yb[:, j, :], in0=yc[:, par, 1, j, :],
                                                  scalar=gates[:, bass.ds(8 * i + 4 * j + 2 * b + 1, 1)],
                                                  in1=ya[:, j, :], op0=ALU.mult, op1=ALU.add)
                link(last)
                moments(yb).then_inc(cve_ready, 1)

            def normed(c, par):
                dve.wait_ge(crstd_ready, c + 1)
                wait(dve, out_st[par], 8 * c - 8 * par)
                for j in range(2):
                    last = v.tensor_scalar(yo[:, par, j, :], yb[:, j, :], mv[:, j, 0:1], rstd_c[:, j:j + 1],
                                           ALU.subtract, ALU.mult)
                last.then_inc(yo_ready, 1)

            w_low(0, 0, 0)
            w_low(0, 0, 1)
            x_low(0, 0)
            unit(0, 0)
            unit(1, 1)
            with dve.Fori(1, E // 2) as i:
                link.enter(i - 1, 6)
                for par in range(2):
                    unit(2 * i + par, par)
            link.leave(E // 2 - 1)
            unit(E, 0)
            combine(0, 0, 0)
            unit(E + 1, 1)
            normed(0, 0)
            combine(0, 1, 1)
            with dve.Fori(1, E // 2 - 1) as i:
                link.enter(i - 1, 14)
                for par in range(2):
                    unit(E + 2 * i + par, par)
                    normed(2 * i + par - 1, 1 - par)
                    combine(0, 2 * i + par, par)
            link.leave(E // 2 - 2)
            for par in range(2):
                unit(2 * E - 2 + par, par, ahead=(par == 0))
                normed(E - 3 + par, 1 - par)
                combine(0, E - 2 + par, par)
            normed(E - 1, 1)
            combine(1, 0, 0)
            normed(E, 0)
            combine(1, 1, 1)
            with dve.Fori(1, E // 2) as i:
                link.enter(i - 1, 8)
                for par in range(2):
                    normed(E + 2 * i + par - 1, 1 - par)
                    combine(1, 2 * i + par, par)
            link.leave(E // 2 - 1)
            normed(NC - 1, 1)

        @block.gpsimd
        def _(pool):
            link = Link(pool, link_pool)
            g = nc.gpsimd
            g.memset(zeros[:], 0.0).then_inc(consts_pool, 1)
            for t, fill in ((ident, 0.0), (strict, 1.0), (upper, 1.0), (id16, 0.0), (mask16, 1.0), (mask32, 1.0),
                            (heads, 1.0)):
                last = g.memset(t[:], fill)
            link(last)
            g.affine_select(out=ident[:], in_=ident[:], compare_op=ALU.not_equal, fill=1.0, base=0,
                            pattern=[[-1, P]], channel_multiplier=1).then_inc(consts_pool, 1)
            g.affine_select(out=strict[:], in_=strict[:], compare_op=ALU.is_ge, fill=0.0, base=-1,
                            pattern=[[-1, P]], channel_multiplier=1).then_inc(consts_pool, 1)
            g.affine_select(out=upper[:], in_=upper[:], compare_op=ALU.is_ge, fill=0.0, base=0,
                            pattern=[[1, P]], channel_multiplier=-1).then_inc(consts_pool, 1)
            by16 = mask16[:].rearrange("p (b c) -> p b c", c=16)
            link(g.affine_select(out=by16, in_=by16, compare_op=ALU.is_ge, fill=0.0, base=0,
                                 pattern=[[-16, 8], [0, 16]], channel_multiplier=1))
            link(g.affine_select(out=by16, in_=by16, compare_op=ALU.is_ge, fill=0.0, base=15,
                                 pattern=[[16, 8], [0, 16]], channel_multiplier=-1))
            by_head = heads[:].rearrange("p (b c) -> p b c", c=DV)
            link(g.affine_select(out=by_head, in_=by_head, compare_op=ALU.is_ge, fill=0.0, base=0,
                                 pattern=[[-DV, H], [0, DV]], channel_multiplier=1))
            link(g.affine_select(out=by_head, in_=by_head, compare_op=ALU.is_ge, fill=0.0, base=DV - 1,
                                 pattern=[[DV, H], [0, DV]], channel_multiplier=-1))
            by32 = mask32[:].rearrange("p (b c) -> p b c", c=32)
            link(g.affine_select(out=by32, in_=by32, compare_op=ALU.is_ge, fill=0.0, base=-16,
                                 pattern=[[-32, 4], [0, 32]], channel_multiplier=1))
            link(g.affine_select(out=by32, in_=by32, compare_op=ALU.is_ge, fill=0.0, base=31,
                                 pattern=[[32, 4], [0, 32]], channel_multiplier=-1))
            link(g.affine_select(out=by32, in_=by32, compare_op=ALU.is_ge, fill=0.0, base=15,
                                 pattern=[[0, 4], [-1, 32]], channel_multiplier=0))
            g.iota(pidx[:], pattern=[[0, 1]], base=0, channel_multiplier=1).then_inc(consts_pool, 1)
            g.iota(ids[:], pattern=[[P, NP], [0, B], [S, TOPK]], base=1, channel_multiplier=1,
                   allow_small_or_imprecise_dtypes=True)
            g.iota(iota8[:], pattern=[[1, E]], base=0, channel_multiplier=0,
                   allow_small_or_imprecise_dtypes=True).then_inc(consts_pool, 1)
            link(g.affine_select(out=id16[:], in_=id16[:], compare_op=ALU.not_equal, fill=1.0, base=0,
                                 pattern=[[-1, 16], [1, 16]], channel_multiplier=0))

            def solve(q):
                wait(pool, xi_st, 16 * q)
                apart(pool)
                link(g.tensor_copy(xs[:, 0], id16[:]))
                pool.wait_ge(ab_ld, 16 * q + 16)
                for j in range(15):
                    n = 15 - j
                    pr_ = prod[:, 0:n * (j + 1)].rearrange("p (i c) -> p i c", c=j + 1)
                    link(g.tensor_tensor(pr_, bc(ab[:, j + 1:, j], 2, j + 1), bc(xs[:, 0, j, 0:j + 1], 1, n), ALU.mult))
                    link(g.tensor_tensor(xs[:, 0, j + 1:, 0:j + 1], xs[:, 0, j + 1:, 0:j + 1], pr_, ALU.subtract))
                apart(pool)
                g.tensor_copy(xs[:, 1], xs[:, 0].rearrange("p r c -> p c r")).then_inc(solved, 1)

            def squares(p):
                pool.wait_ge(o_ready, p + 1)
                g.tensor_tensor(osq[:], o[:], o[:], ALU.mult).then_inc(osq_ready, 1)

            def gated_out(p, par):
                pool.wait_ge(orms_ready, p + 1)
                link(g.tensor_tensor(on[:], o[:], orms[:], ALU.mult))
                wait(pool, out_mm, 5 * (p - 1) + 2)
                g.tensor_tensor(og[:], on[:], silu[:, par], ALU.mult).then_inc(og_ready, 1)

            def joins(q, par):
                pool.wait_ge(freed_dve, 4 * q + 2)
                wait(pool, lvl_mm, 6 * (q - 1) + 1)
                g.tensor_tensor(m32[:], A[:, par], bc(mask32[:], 1, U), ALU.mult).then_inc(m32_ready, 1)

            def scatter(p, par):
                pool.wait_ge(slot_ready, p + 1)
                if isinstance(p, int) and p == 0:
                    pool.wait_ge(zero_st, ZEROS)
                apart(pool)
                for j in range(2):
                    for k in range(TOPK):
                        at = slot[:, par, 2 * j + k:2 * j + k + 1]
                        g.indirect_dma_start(out=xs_d[:, :], out_offset=bass.IndirectOffsetOnAxis(ap=at, axis=0),
                                             in_=x1[:, par, j, k, :], in_offset=None).then_inc(scat[par], 16)

            def silu_v(q, par):
                pool.wait_ge(sg_ready, q + 1)
                g.tensor_tensor(silu[:, par], G[:], sg[:], ALU.mult).then_inc(gate_ready, 1)
                pool.wait_ge(br_ready, q + 1)
                wait(pool, r_ready, q - 1)
                g.tensor_tensor(Vp[:, par], V[:].rearrange("p j (h d) -> p (j h) d", h=H), bc(br[:], 2, DV),
                                ALU.mult).then_inc(gate_ready, 1)

            def step(p, par, s1, main, outq):
                q, npar, o_ = p + 1, 1 - par, p - 1
                if outq:
                    squares(o_)
                    gated_out(o_, npar)
                if s1:
                    joins(q, npar)
                    solve(q)
                if outq:
                    scatter(o_, npar)
                if s1:
                    silu_v(q, npar)

            phase_a(pool, step, link, POOL_LINKS)

            def send_back(b, n, par):
                pool.wait_ge(row_ready, n + 1)
                pool.wait_ge(ye_ready, n + 1)
                wait(pool, y_back[par], CT * (8 * n - 8 * par))
                apart(pool)
                for i in range(CT):
                    g.indirect_dma_start(out=y_d[b][:, :], in_=ye[:, par, i, :], in_offset=None,
                                         out_offset=bass.IndirectOffsetOnAxis(ap=row[:, par, i:i + 1], axis=0)
                                         ).then_inc(y_back[par], 16)

            def c_rstd(c):
                pool.wait_ge(cve_ready, c + 1)
                g.tensor_tensor(rstd_c[:], ve[:], minus_half[:], ALU.pow).then_inc(crstd_ready, 1)

            send_back(0, 0, 0)
            send_back(0, 1, 1)
            with pool.Fori(1, E // 2) as i:
                for par in range(2):
                    send_back(0, 2 * i + par, par)
            with pool.Fori(0, E // 2) as i:
                for par in range(2):
                    send_back(1, E + 2 * i + par, par)
                    c_rstd(2 * i + par)
            with pool.Fori(0, E // 2) as i:
                for par in range(2):
                    c_rstd(E + 2 * i + par)


ACT_LINKS = 8
DVE_LINKS = 40
POOL_LINKS = 64


def kernel(L0_attn_x, L0_attn_Wq, L0_attn_Wk, L0_attn_Wv, L0_attn_Wb, L0_attn_Wg, L0_attn_Wo, L0_attn_norm_w,
           L0_ffn_gate_w, L0_ffn_w1, L0_ffn_w2, L0_ffn_w3):
    import concourse.bacc as bacc
    from concourse.bass_utils import run_bass_kernel_spmd

    x = np.ascontiguousarray(L0_attn_x).reshape(B * S, D)
    arrays = {
        "x": x, "xT": np.ascontiguousarray(x.T),
        "Wq": np.ascontiguousarray(L0_attn_Wq), "Wk": np.ascontiguousarray(L0_attn_Wk),
        "Wvb": np.ascontiguousarray(np.concatenate([np.asarray(L0_attn_Wv), np.asarray(L0_attn_Wb)], axis=1)),
        "Wg": np.ascontiguousarray(L0_attn_Wg),
        "Wo": np.ascontiguousarray(L0_attn_Wo),
        "norm_w": np.ascontiguousarray(L0_attn_norm_w),
        "gateT": np.ascontiguousarray(np.asarray(L0_ffn_gate_w).T),
        "w1": np.ascontiguousarray(L0_ffn_w1), "w2": np.ascontiguousarray(L0_ffn_w2),
        "w3": np.ascontiguousarray(L0_ffn_w3),
    }
    nc = bacc.Bacc("TRN2", target_bir_lowering=False, num_devices=1)
    args = [nc.dram_tensor(n, a.shape, F32, kind="ExternalInput").ap() for n, a in arrays.items()]
    out = nc.dram_tensor("result", (B * S, D), F32, kind="ExternalOutput").ap()
    build(nc, *args, out)
    r = run_bass_kernel_spmd(nc, [arrays], core_ids=[0])
    return r.results[0]["result"].reshape(B, S, D)
```
